# Optimizing a Trainium2 kernel written in Bass

```python
import numpy as np
import jax
import jax.numpy as jnp

def _softmax(x, axis=-1):
    return jax.nn.softmax(x, axis=axis)

def _gelu(x):
    return jax.nn.gelu(x, approximate=True)

def _silu(x):
    return jax.nn.silu(x)

def _sigmoid(x):
    return jax.nn.sigmoid(x)

def _layernorm(x, axis=-1, eps=1e-05):
    m = jnp.mean(x, axis=axis, keepdims=True)
    v = jnp.var(x, axis=axis, keepdims=True)
    return (x - m) / jnp.sqrt(v + eps)

def _scatter_add(tgt, idx, src, axis=0):
    return tgt.at[idx].add(src)

def _segment_sum(src, seg, n):
    return jax.ops.segment_sum(src, seg, n)
kernel_name = 'mk_hybrid_d2_jaxref_r8_9a69d3'

def setup_inputs(seed: int=0):
    np.random.seed(seed)
    _w = jnp.asarray

    def _L0_attn_a_setup():
        import jax, jax.numpy as jnp
        import numpy as np
        D_MODEL = 256
        N_HEADS = 16
        N_KV = 4
        HEAD_DIM = D_MODEL // N_HEADS
        N_GROUPS = N_HEADS // N_KV
        BLOCK_SIZE = 128
        THETA = 10000.0

        def _rope_tables(T):
            freqs = 1.0 / THETA ** (jnp.arange(0, HEAD_DIM, 2, dtype=jnp.float32) / HEAD_DIM)
            t = jnp.arange(T, dtype=jnp.float32)
            emb = jnp.outer(t, freqs)
            cos = jnp.cos(emb)
            sin = jnp.sin(emb)
            return (jnp.concatenate([cos, cos], -1), jnp.concatenate([sin, sin], -1))

        def _apply_rope(x, cos, sin):
            half = HEAD_DIM // 2
            x1, x2 = (x[..., :half], x[..., half:])
            rot = jnp.concatenate([-x2, x1], -1)
            return x * cos + rot * sin
        key = jax.random.key(seed)
        ks = jax.random.split(key, 5)
        B, T = (2, 256)
        x = jax.random.normal(ks[0], (B, T, D_MODEL), dtype=jnp.float32)
        s = 0.02
        Wq = jax.random.normal(ks[1], (D_MODEL, N_HEADS * HEAD_DIM), dtype=jnp.float32) * s
        Wk = jax.random.normal(ks[2], (D_MODEL, N_KV * HEAD_DIM), dtype=jnp.float32) * s
        Wv = jax.random.normal(ks[3], (D_MODEL, N_KV * HEAD_DIM), dtype=jnp.float32) * s
        Wo = jax.random.normal(ks[4], (N_HEADS * HEAD_DIM, D_MODEL), dtype=jnp.float32) * s
        return {'x': x, 'Wq': Wq, 'Wk': Wk, 'Wv': Wv, 'Wo': Wo}
    _L0_attn_a_in = _L0_attn_a_setup()

    def _L0_attn_b_setup():
        import jax, jax.numpy as jnp
        import numpy as np
        import math
        B, T, C = (2, 256, 256)
        N_HEAD = 16
        N_KV = 4
        GROUP = N_HEAD // N_KV
        HS = C // N_HEAD
        WINDOW = 128
        SINK = 4

        def _sliding_window_sink_mask(t):
            i = jnp.arange(t)[:, None]
            j = jnp.arange(t)[None, :]
            causal = j <= i
            band = j >= i - (WINDOW - 1)
            mask = causal & band
            mask = mask | (j < SINK)
            mask = mask & ((i >= SINK) | causal)
            return mask
        key = jax.random.key(seed)
        ks = jax.random.split(key, 5)
        s = 1.0 / math.sqrt(C)
        return {'x': jax.random.normal(ks[0], (B, T, C), dtype=jnp.float32), 'Wq': jax.random.normal(ks[1], (C, C), dtype=jnp.float32) * s, 'Wk': jax.random.normal(ks[2], (N_KV * HS, C), dtype=jnp.float32) * s, 'Wv': jax.random.normal(ks[3], (N_KV * HS, C), dtype=jnp.float32) * s, 'Wo': jax.random.normal(ks[4], (C, C), dtype=jnp.float32) * s}
    _L0_attn_b_in = _L0_attn_b_setup()

    def _L0_ffn_setup():
        import jax, jax.numpy as jnp
        import numpy as np
        NUM_EXPERTS = 64
        TOP_K = 8
        HIDDEN = 256
        INTER = 96
        key = jax.random.key(seed)
        k1, k2, k3, k4, k5 = jax.random.split(key, 5)
        hidden_states = jax.random.normal(k1, (4, 32, HIDDEN), dtype=jnp.float32)
        gate_w = jax.random.normal(k2, (HIDDEN, NUM_EXPERTS), dtype=jnp.float32) * 0.02
        w_gate = jax.random.normal(k3, (NUM_EXPERTS, HIDDEN, INTER), dtype=jnp.float32) * 0.02
        w_up = jax.random.normal(k4, (NUM_EXPERTS, HIDDEN, INTER), dtype=jnp.float32) * 0.02
        w_down = jax.random.normal(k5, (NUM_EXPERTS, INTER, HIDDEN), dtype=jnp.float32) * 0.02
        return {'hidden_states': hidden_states, 'gate_w': gate_w, 'w_gate': w_gate, 'w_up': w_up, 'w_down': w_down}
    _L0_ffn_in = _L0_ffn_setup()

    def _L1_attn_a_setup():
        import jax, jax.numpy as jnp
        import numpy as np
        NUM_HEADS = 16
        LN_EPS = 1e-05

        def _rope(x):
            S, D = (x.shape[-2], x.shape[-1])
            rot = D // 2
            inv_freq = 1.0 / 10000.0 ** (jnp.arange(0, rot, 2, dtype=jnp.float32) / rot)
            ang = jnp.arange(S, dtype=jnp.float32)[:, None] * inv_freq[None, :]
            ang = jnp.repeat(ang, 2, axis=-1)
            cos, sin = (jnp.cos(ang), jnp.sin(ang))
            xr, xp = (x[..., :rot], x[..., rot:])
            x1, x2 = (xr[..., 0::2], xr[..., 1::2])
            rot_half = jnp.stack((-x2, x1), axis=-1).reshape(xr.shape)
            xr = xr * cos + rot_half * sin
            return jnp.concatenate([xr, xp], axis=-1)
        key = jax.random.key(seed)
        k1, k2, k3 = jax.random.split(key, 3)
        B, S, D = (4, 256, 256)
        X = jax.random.normal(k1, (B, S, D), dtype=jnp.float32)
        ln_w = jnp.ones((D,), dtype=jnp.float32)
        ln_b = jnp.zeros((D,), dtype=jnp.float32)
        W_in = jax.random.normal(k2, (D, 3 * D), dtype=jnp.float32) * 0.02
        W_out = jax.random.normal(k3, (D, D), dtype=jnp.float32) * 0.02
        return {'X': X, 'ln_w': ln_w, 'ln_b': ln_b, 'W_in': W_in, 'W_out': W_out}
    _L1_attn_a_in = _L1_attn_a_setup()

    def _L1_attn_b_setup():
        import jax, jax.numpy as jnp
        import numpy as np
        B, S, D, H = (2, 256, 256, 16)
        QR, KVR = (96, 64)
        DN, DR, DV = (128, 64, 128)
        EPS = 1e-06
        WSCALE = 0.02

        def rms_norm(x, w, eps=EPS):
            return x * jax.lax.rsqrt(jnp.mean(x * x, axis=-1, keepdims=True) + eps) * w

        def rope_cos_sin(seq_len, d):
            inv = 1.0 / 10000.0 ** (jnp.arange(0, d, 2, dtype=jnp.float32) / d)
            t = jnp.arange(seq_len, dtype=jnp.float32)
            f = jnp.outer(t, inv)
            return (jnp.cos(f)[:, None, :], jnp.sin(f)[:, None, :])

        def apply_rope(x, cos, sin):
            x1, x2 = (x[..., 0::2], x[..., 1::2])
            o1 = x1 * cos - x2 * sin
            o2 = x1 * sin + x2 * cos
            return jnp.stack([o1, o2], axis=-1).reshape(x.shape)
        key = jax.random.key(seed)
        ks = jax.random.split(key, 10)
        return {'x': jax.random.normal(ks[0], (B, S, D), jnp.float32), 'wq_down': jax.random.normal(ks[1], (D, QR), jnp.float32) * WSCALE, 'q_norm_w': jnp.ones((QR,), jnp.float32), 'wq_up': jax.random.normal(ks[2], (QR, H * DN), jnp.float32) * WSCALE, 'wq_rope': jax.random.normal(ks[3], (QR, H * DR), jnp.float32) * WSCALE, 'wkv_down': jax.random.normal(ks[4], (D, KVR), jnp.float32) * WSCALE, 'kv_norm_w': jnp.ones((KVR,), jnp.float32), 'wkv_up': jax.random.normal(ks[5], (KVR, H * (DN + DV)), jnp.float32) * WSCALE, 'wk_rope': jax.random.normal(ks[6], (D, DR), jnp.float32) * WSCALE, 'wo': jax.random.normal(ks[7], (H * DV, D), jnp.float32) * WSCALE}
    _L1_attn_b_in = _L1_attn_b_setup()

    def _L1_ffn_setup():
        import jax, jax.numpy as jnp
        import numpy as np
        DIM = 256
        N_EXPERTS = 8
        TOP_K = 2
        key = jax.random.key(seed)
        ks = jax.random.split(key, 5)
        x = jax.random.normal(ks[0], (4, 512, DIM), dtype=jnp.float32)
        W_up = jax.random.normal(ks[1], (DIM, DIM), dtype=jnp.float32) * (1.0 / np.sqrt(DIM))
        W_down = jax.random.normal(ks[2], (DIM, DIM), dtype=jnp.float32) * (1.0 / np.sqrt(DIM))
        W_gate = jax.random.normal(ks[3], (N_EXPERTS, DIM), dtype=jnp.float32) * (1.0 / np.sqrt(DIM))
        W_expert = jax.random.normal(ks[4], (DIM, DIM), dtype=jnp.float32) * (1.0 / np.sqrt(DIM))
        return {'x': x, 'W_up': W_up, 'W_down': W_down, 'W_gate': W_gate, 'W_expert': W_expert}
    _L1_ffn_in = _L1_ffn_setup()
    _d = {'L0_attn_a_x': _L0_attn_a_in['x'], 'L0_attn_a_Wq': _L0_attn_a_in['Wq'], 'L0_attn_a_Wk': _L0_attn_a_in['Wk'], 'L0_attn_a_Wv': _L0_attn_a_in['Wv'], 'L0_attn_a_Wo': _L0_attn_a_in['Wo'], 'L0_attn_b_Wq': _L0_attn_b_in['Wq'], 'L0_attn_b_Wk': _L0_attn_b_in['Wk'], 'L0_attn_b_Wv': _L0_attn_b_in['Wv'], 'L0_attn_b_Wo': _L0_attn_b_in['Wo'], 'L0_ffn_gate_w': _L0_ffn_in['gate_w'], 'L0_ffn_w_gate': _L0_ffn_in['w_gate'], 'L0_ffn_w_up': _L0_ffn_in['w_up'], 'L0_ffn_w_down': _L0_ffn_in['w_down'], 'L1_attn_a_ln_w': _L1_attn_a_in['ln_w'], 'L1_attn_a_ln_b': _L1_attn_a_in['ln_b'], 'L1_attn_a_W_in': _L1_attn_a_in['W_in'], 'L1_attn_a_W_out': _L1_attn_a_in['W_out'], 'L1_attn_b_wq_down': _L1_attn_b_in['wq_down'], 'L1_attn_b_q_norm_w': _L1_attn_b_in['q_norm_w'], 'L1_attn_b_wq_up': _L1_attn_b_in['wq_up'], 'L1_attn_b_wq_rope': _L1_attn_b_in['wq_rope'], 'L1_attn_b_wkv_down': _L1_attn_b_in['wkv_down'], 'L1_attn_b_kv_norm_w': _L1_attn_b_in['kv_norm_w'], 'L1_attn_b_wkv_up': _L1_attn_b_in['wkv_up'], 'L1_attn_b_wk_rope': _L1_attn_b_in['wk_rope'], 'L1_attn_b_wo': _L1_attn_b_in['wo'], 'L1_ffn_W_up': _L1_ffn_in['W_up'], 'L1_ffn_W_down': _L1_ffn_in['W_down'], 'L1_ffn_W_gate': _L1_ffn_in['W_gate'], 'L1_ffn_W_expert': _L1_ffn_in['W_expert']}
    _x0 = _d['L0_attn_a_x']
    _d['L0_attn_a_x'] = jax.random.normal(jax.random.fold_in(jax.random.key(seed), 1), (1, 1024, 256), dtype=_x0.dtype)
    del _x0
    return _d

def reference(L0_attn_a_x, L0_attn_a_Wq, L0_attn_a_Wk, L0_attn_a_Wv, L0_attn_a_Wo, L0_attn_b_Wq, L0_attn_b_Wk, L0_attn_b_Wv, L0_attn_b_Wo, L0_ffn_gate_w, L0_ffn_w_gate, L0_ffn_w_up, L0_ffn_w_down, L1_attn_a_ln_w, L1_attn_a_ln_b, L1_attn_a_W_in, L1_attn_a_W_out, L1_attn_b_wq_down, L1_attn_b_q_norm_w, L1_attn_b_wq_up, L1_attn_b_wq_rope, L1_attn_b_wkv_down, L1_attn_b_kv_norm_w, L1_attn_b_wkv_up, L1_attn_b_wk_rope, L1_attn_b_wo, L1_ffn_W_up, L1_ffn_W_down, L1_ffn_W_gate, L1_ffn_W_expert):

    def _L0_attn_a_ref(x, Wq, Wk, Wv, Wo):
        import jax, jax.numpy as jnp
        import numpy as np
        D_MODEL = 256
        N_HEADS = 16
        N_KV = 4
        HEAD_DIM = D_MODEL // N_HEADS
        N_GROUPS = N_HEADS // N_KV
        BLOCK_SIZE = 128
        THETA = 10000.0

        def _rope_tables(T):
            freqs = 1.0 / THETA ** (jnp.arange(0, HEAD_DIM, 2, dtype=jnp.float32) / HEAD_DIM)
            t = jnp.arange(T, dtype=jnp.float32)
            emb = jnp.outer(t, freqs)
            cos = jnp.cos(emb)
            sin = jnp.sin(emb)
            return (jnp.concatenate([cos, cos], -1), jnp.concatenate([sin, sin], -1))

        def _apply_rope(x, cos, sin):
            half = HEAD_DIM // 2
            x1, x2 = (x[..., :half], x[..., half:])
            rot = jnp.concatenate([-x2, x1], -1)
            return x * cos + rot * sin
        B, T, C = x.shape
        q = (x @ Wq).reshape(B, T, N_HEADS, HEAD_DIM).transpose(0, 2, 1, 3)
        k = (x @ Wk).reshape(B, T, N_KV, HEAD_DIM).transpose(0, 2, 1, 3)
        v = (x @ Wv).reshape(B, T, N_KV, HEAD_DIM).transpose(0, 2, 1, 3)
        cos, sin = _rope_tables(T)
        q = _apply_rope(q, cos, sin)
        k = _apply_rope(k, cos, sin)
        qg = q.reshape(B, N_KV, N_GROUPS, T, HEAD_DIM)
        scale = 1.0 / jnp.sqrt(jnp.float32(HEAD_DIM))
        scores = jnp.einsum('bngtd,bnsd->bngts', qg, k) * scale
        blk = jnp.arange(T) // BLOCK_SIZE
        masked = blk[None, :] > blk[:, None]
        scores = jnp.where(masked, -jnp.inf, scores)
        attn = jax.nn.softmax(scores, axis=-1)
        y = jnp.einsum('bngts,bnsd->bngtd', attn, v)
        y = y.reshape(B, N_HEADS, T, HEAD_DIM).transpose(0, 2, 1, 3).reshape(B, T, C)
        return y @ Wo

    def _L0_attn_b_ref(x, Wq, Wk, Wv, Wo):
        import jax, jax.numpy as jnp
        import numpy as np
        import math
        B, T, C = (2, 256, 256)
        N_HEAD = 16
        N_KV = 4
        GROUP = N_HEAD // N_KV
        HS = C // N_HEAD
        WINDOW = 128
        SINK = 4

        def _sliding_window_sink_mask(t):
            i = jnp.arange(t)[:, None]
            j = jnp.arange(t)[None, :]
            causal = j <= i
            band = j >= i - (WINDOW - 1)
            mask = causal & band
            mask = mask | (j < SINK)
            mask = mask & ((i >= SINK) | causal)
            return mask
        b, t, c = x.shape
        q = (x @ Wq.T).reshape(b, t, N_HEAD, HS).transpose(0, 2, 1, 3)
        q = q.reshape(b, N_KV, GROUP, t, HS)
        k = (x @ Wk.T).reshape(b, t, N_KV, HS).transpose(0, 2, 1, 3)
        v = (x @ Wv.T).reshape(b, t, N_KV, HS).transpose(0, 2, 1, 3)
        scale = 1.0 / math.sqrt(HS)
        att = jnp.einsum('bkgqd,bkjd->bkgqj', q, k) * scale
        mask = _sliding_window_sink_mask(t)
        att = jnp.where(mask[None, None, None, :, :], att, -jnp.inf)
        att = jax.nn.softmax(att, axis=-1)
        y = jnp.einsum('bkgqj,bkjd->bkgqd', att, v)
        y = y.reshape(b, N_HEAD, t, HS).transpose(0, 2, 1, 3).reshape(b, t, c)
        return y @ Wo.T

    def _L0_ffn_ref(hidden_states, gate_w, w_gate, w_up, w_down):
        import jax, jax.numpy as jnp
        import numpy as np
        NUM_EXPERTS = 64
        TOP_K = 8
        HIDDEN = 256
        INTER = 96
        orig_shape = hidden_states.shape
        x = hidden_states.reshape(-1, orig_shape[-1])
        T = x.shape[0]
        router_logits = x @ gate_w
        probs = jax.nn.softmax(router_logits.astype(jnp.float32), axis=-1)
        top_vals, top_idx = jax.lax.top_k(probs, TOP_K)
        top_vals = top_vals / jnp.sum(top_vals, axis=-1, keepdims=True)
        rw = jnp.zeros((T, NUM_EXPERTS), dtype=x.dtype)
        rw = rw.at[jnp.arange(T)[:, None], top_idx].set(top_vals)
        g = jnp.einsum('th,ehi->tei', x, w_gate)
        u = jnp.einsum('th,ehi->tei', x, w_up)
        h = jax.nn.silu(g) * u
        h = h * rw[:, :, None]
        out = jnp.einsum('tei,eih->th', h, w_down)
        return out.reshape(orig_shape)

    def _L1_attn_a_ref(X, ln_w, ln_b, W_in, W_out):
        import jax, jax.numpy as jnp
        import numpy as np
        NUM_HEADS = 16
        LN_EPS = 1e-05

        def _rope(x):
            S, D = (x.shape[-2], x.shape[-1])
            rot = D // 2
            inv_freq = 1.0 / 10000.0 ** (jnp.arange(0, rot, 2, dtype=jnp.float32) / rot)
            ang = jnp.arange(S, dtype=jnp.float32)[:, None] * inv_freq[None, :]
            ang = jnp.repeat(ang, 2, axis=-1)
            cos, sin = (jnp.cos(ang), jnp.sin(ang))
            xr, xp = (x[..., :rot], x[..., rot:])
            x1, x2 = (xr[..., 0::2], xr[..., 1::2])
            rot_half = jnp.stack((-x2, x1), axis=-1).reshape(xr.shape)
            xr = xr * cos + rot_half * sin
            return jnp.concatenate([xr, xp], axis=-1)
        B, S, D = X.shape
        H = NUM_HEADS
        Dh = D // H
        mu = jnp.mean(X, axis=-1, keepdims=True)
        var = jnp.mean(jnp.square(X - mu), axis=-1, keepdims=True)
        Xn = (X - mu) * jax.lax.rsqrt(var + LN_EPS) * ln_w + ln_b
        qkv = jnp.einsum('bsd,df->bsf', Xn, W_in)
        Q, K, V = jnp.split(qkv, 3, axis=-1)
        Q = Q.reshape(B, S, H, Dh).transpose(0, 2, 1, 3)
        K = K.reshape(B, S, H, Dh).transpose(0, 2, 1, 3)
        V = V.reshape(B, S, H, Dh).transpose(0, 2, 1, 3)
        Q, K = (_rope(Q), _rope(K))
        scores = jnp.einsum('bhqd,bhkd->bhqk', Q, K) / jnp.sqrt(jnp.float32(Dh))
        probs = jax.nn.softmax(scores, axis=-1)
        ctx = jnp.einsum('bhqk,bhkd->bhqd', probs, V)
        ctx = ctx.transpose(0, 2, 1, 3).reshape(B, S, D)
        out = jnp.einsum('bsd,df->bsf', ctx, W_out)
        return out + X

    def _L1_attn_b_ref(x, wq_down, q_norm_w, wq_up, wq_rope, wkv_down, kv_norm_w, wkv_up, wk_rope, wo):
        import jax, jax.numpy as jnp
        import numpy as np
        B, S, D, H = (2, 256, 256, 16)
        QR, KVR = (96, 64)
        DN, DR, DV = (128, 64, 128)
        EPS = 1e-06
        WSCALE = 0.02

        def rms_norm(x, w, eps=EPS):
            return x * jax.lax.rsqrt(jnp.mean(x * x, axis=-1, keepdims=True) + eps) * w

        def rope_cos_sin(seq_len, d):
            inv = 1.0 / 10000.0 ** (jnp.arange(0, d, 2, dtype=jnp.float32) / d)
            t = jnp.arange(seq_len, dtype=jnp.float32)
            f = jnp.outer(t, inv)
            return (jnp.cos(f)[:, None, :], jnp.sin(f)[:, None, :])

        def apply_rope(x, cos, sin):
            x1, x2 = (x[..., 0::2], x[..., 1::2])
            o1 = x1 * cos - x2 * sin
            o2 = x1 * sin + x2 * cos
            return jnp.stack([o1, o2], axis=-1).reshape(x.shape)
        bs, seq_len, _ = x.shape
        qc = rms_norm(x @ wq_down, q_norm_w)
        q_nope = (qc @ wq_up).reshape(bs, seq_len, H, DN)
        q_pe = (qc @ wq_rope).reshape(bs, seq_len, H, DR)
        kvc = rms_norm(x @ wkv_down, kv_norm_w)
        kv = (kvc @ wkv_up).reshape(bs, seq_len, H, DN + DV)
        k_nope, v = (kv[..., :DN], kv[..., DN:])
        k_rope = (x @ wk_rope).reshape(bs, seq_len, 1, DR)
        cos, sin = rope_cos_sin(seq_len, DR)
        q_pe = apply_rope(q_pe, cos, sin)
        k_rope = apply_rope(k_rope, cos, sin)
        k_rope = jnp.broadcast_to(k_rope, (bs, seq_len, H, DR))
        q = jnp.concatenate([q_nope, q_pe], axis=-1)
        k = jnp.concatenate([k_nope, k_rope], axis=-1)
        scale = 1.0 / np.sqrt(DN + DR).astype(np.float32)
        scores = jnp.einsum('bqhd,bkhd->bhqk', q, k) * scale
        mask = jnp.triu(jnp.full((seq_len, seq_len), -jnp.inf, jnp.float32), k=1)
        probs = jax.nn.softmax(scores.astype(jnp.float32) + mask, axis=-1).astype(q.dtype)
        out = jnp.einsum('bhqk,bkhd->bqhd', probs, v).reshape(bs, seq_len, H * DV)
        return out @ wo

    def _L1_ffn_ref(x, W_up, W_down, W_gate, W_expert):
        import jax, jax.numpy as jnp
        import numpy as np
        DIM = 256
        N_EXPERTS = 8
        TOP_K = 2
        logits = jnp.einsum('bsd,ed->bse', x, W_gate)
        routing_weights, selected_experts = jax.lax.top_k(logits, TOP_K)
        shared_out = jnp.einsum('bsd,od->bso', jax.nn.relu(jnp.einsum('bsd,od->bso', x, W_up)), W_down)
        rw = jax.nn.softmax(routing_weights, axis=-1)
        expert_out = jnp.einsum('bsd,do->bso', x, W_expert)
        moe_out = jnp.sum(rw, axis=-1, keepdims=True) * expert_out
        return shared_out + moe_out
    x = L0_attn_a_x
    x = x + _L0_attn_a_ref(_layernorm(x, axis=-1), L0_attn_a_Wq, L0_attn_a_Wk, L0_attn_a_Wv, L0_attn_a_Wo)
    x = x + _L0_ffn_ref(_layernorm(x, axis=-1), L0_ffn_gate_w, L0_ffn_w_gate, L0_ffn_w_up, L0_ffn_w_down)
    x = x + _L0_attn_b_ref(_layernorm(x, axis=-1), L0_attn_b_Wq, L0_attn_b_Wk, L0_attn_b_Wv, L0_attn_b_Wo)
    x = x + _L0_ffn_ref(_layernorm(x, axis=-1), L0_ffn_gate_w, L0_ffn_w_gate, L0_ffn_w_up, L0_ffn_w_down)
    x = x + _L1_attn_a_ref(_layernorm(x, axis=-1), L1_attn_a_ln_w, L1_attn_a_ln_b, L1_attn_a_W_in, L1_attn_a_W_out)
    x = x + _L1_ffn_ref(_layernorm(x, axis=-1), L1_ffn_W_up, L1_ffn_W_down, L1_ffn_W_gate, L1_ffn_W_expert)
    x = x + _L1_attn_b_ref(_layernorm(x, axis=-1), L1_attn_b_wq_down, L1_attn_b_q_norm_w, L1_attn_b_wq_up, L1_attn_b_wq_rope, L1_attn_b_wkv_down, L1_attn_b_kv_norm_w, L1_attn_b_wkv_up, L1_attn_b_wk_rope, L1_attn_b_wo)
    x = x + _L1_ffn_ref(_layernorm(x, axis=-1), L1_ffn_W_up, L1_ffn_W_down, L1_ffn_W_gate, L1_ffn_W_expert)
    return x

_drawn_inputs = setup_inputs


def setup_inputs(seed=0):
    import zlib

    import numpy as np

    out = dict(_drawn_inputs(seed))
    spreads = {'L1_attn_a_ln_w': (1.0, 0.6),
     'L1_attn_a_ln_b': (0.0, 0.8),
     'L1_attn_b_q_norm_w': (1.0, 0.6),
     'L1_attn_b_kv_norm_w': (1.0, 0.6)}
    factors = {'L0_attn_a_Wq': 8.0,
     'L0_attn_a_Wk': 8.0,
     'L0_attn_a_Wv': 6.672,
     'L0_attn_a_Wo': 7.948,
     'L0_ffn_gate_w': 8.0,
     'L0_ffn_w_gate': 8.0,
     'L0_ffn_w_up': 8.0,
     'L0_ffn_w_down': 8.0,
     'L1_attn_a_W_in': 8.0,
     'L1_attn_a_W_out': 8.0,
     'L1_attn_b_wq_down': 8.0,
     'L1_attn_b_wq_up': 8.0,
     'L1_attn_b_wq_rope': 8.0,
     'L1_attn_b_wkv_down': 5.849,
     'L1_attn_b_wkv_up': 5.593,
     'L1_attn_b_wk_rope': 8.0,
     'L1_attn_b_wo': 5.667,
     'L1_ffn_W_gate': 8.0}
    for name, (base, spread) in spreads.items():
        noise = np.random.default_rng([zlib.crc32(name.encode()), seed]).standard_normal(out[name].shape)
        drawn = base * np.exp(spread * noise) if base else spread * noise
        out[name] = jnp.asarray(drawn.astype(out[name].dtype))
    for name, factor in factors.items():
        out[name] = (out[name] * factor).astype(out[name].dtype)
    return out
```

```python
from contextlib import ExitStack

import numpy as np

import concourse.bass as bass
from concourse import mybir

ALU = mybir.AluOpType
ACT = mybir.ActivationFunctionType
AX_X = mybir.AxisListType.X
F32 = mybir.dt.float32
BF16 = mybir.dt.bfloat16

P = 128
T = 1024
TT = T // P
D = 256
KC = D // P
HALF = 512
NEG = -1.0e30

HEADS = 16
HD = 16
PAIRS = [(0, 0), (0, 1), (1, 0), (0, 2), (1, 1), (2, 0)]
PARTS = 3
ROWS = HD * len(PAIRS)
KROWS = ROWS + PARTS

EXPERTS = 64
INTER = 96
TOP = 8
GE = 4
GC = GE * INTER // P
GROUPS = EXPERTS // GE

ROUTES = 8

QR, KVR, DN, DR, DV = 96, 64, 128, 64, 128


class Core:

    def __init__(self, nc, ctx, dram):
        self.nc, self.ctx, self.dram = nc, ctx, dram
        self.sems = []
        self.x = self.sb("x", [P, TT, D], F32)
        self.xn = self.sb("xn", [P, TT, D], F32)
        self.xi = self.sb("xi", [P, TT, D], F32)
        self.xT = self.sb("xT", [P, KC, T], F32)
        self.ident = self.sb("ident", [P, P], F32)
        self.ident_h = self.sb("ident_h", [P, P], BF16)
        self.zero_h = self.sb("zero_h", [P, HALF], BF16)
        self.psum = ctx.enter_context(nc.psum_tensor("psum", [P, 8, HALF], F32))
        self.bank = [self.psum[:, i, :] for i in range(8)]

    def sb(self, name, shape, dt):
        return self.ctx.enter_context(self.nc.sbuf_tensor(name, shape, dt))

    def sem(self, name):
        self.sems.append(self.nc.alloc_semaphore(name))
        return self.sems[-1]

    def clear_semaphores(self):
        self.nc.clear_and_free_semaphores(self.sems)
        self.sems = []
        self.nc.all_engine_barrier()


def start(core):
    nc, dram = core.nc, core.dram
    loaded, const_made, turned, stored = (core.sem(f"start_{n}") for n in ("loaded", "const", "turned", "stored"))
    core.mask = {n: core.sb(f"m_{n}", [P, P], F32) for n in ("causal", "causalT", "prev", "prevT", "prev1", "prev1T", "sinkT")}
    core.mask_h = {n: core.sb(f"mh_{n}", [P, P], BF16) for n in core.mask}
    core.wup = core.sb("wup", [P, KC, D], F32)
    core.wdn = core.sb("wdn", [P, KC, D], F32)
    core.wex = core.sb("wex", [P, KC, D], F32)
    core.wrt = core.sb("wrt", [P, KC, ROUTES], F32)
    core.bqkv = core.sb("bqkv", [P, KC, 384], F32)
    core.bwo = core.sb("bwo", [P, KC, D], F32)
    core.row = {n: core.sb(f"row_{n}", [P, w], F32) for n, w in
            (("L1_attn_a_ln_w", D), ("L1_attn_a_ln_b", D), ("L1_attn_b_q_norm_w", QR), ("L1_attn_b_kv_norm_w", KVR))}
    with ExitStack() as ctx:
        raw = []
        plan = [("L1_ffn_W_up", core.wup, 0, D), ("L1_ffn_W_down", core.wdn, 0, D),
                ("L0_attn_b_Wq", core.bqkv, 0, D), ("L0_attn_b_Wk", core.bqkv, 256, 64),
                ("L0_attn_b_Wv", core.bqkv, 320, 64), ("L0_attn_b_Wo", core.bwo, 0, D),
                ("L1_ffn_W_gate", core.wrt, 0, ROUTES)]
        for name, dst, col, rows in plan:
            for r in range(0, rows, P):
                n = min(P, rows - r)
                t = ctx.enter_context(nc.sbuf_tensor(f"raw_{name}_{r}", [P, D], F32))
                raw.append((name, t, dst, col + r, r, n))
        block = ctx.enter_context(nc.Block())
        loads = len(raw) + 3 + len(core.mask) + len(core.row)

        @block.sync
        def _(sp):
            sp.dma_start(core.ident[:], dram["c_ident"]).then_inc(loaded, 16)
            for name, t, _, _, r, n in raw:
                sp.dma_start(t[0:n, :], dram[name][r:r + n, :]).then_inc(loaded, 16)
            for name in core.mask:
                sp.dma_start(core.mask[name][:], dram[f"c_{name}"]).then_inc(loaded, 16)
            for name, row in core.row.items():
                sp.dma_start(row[:], dram[name].unsqueeze(0).broadcast_to(list(row.shape))).then_inc(loaded, 16)
            sp.dma_start(core.wex[:], dram["L1_ffn_W_expert"].rearrange("(k p) n -> p k n", p=P)).then_inc(loaded, 16)
            sp.dma_start(core.x[:], dram["L0_attn_a_x"].rearrange("b (t p) d -> p (b t) d", p=P)).then_inc(loaded, 16)

        @block.gpsimd
        def _(pool):
            pool.memset(core.zero_h[:], 0.0)
            pool.wait_ge(loaded, 16 * loads)
            pool.tensor_copy(core.ident_h[:], core.ident[:])
            for name in core.mask:
                pool.tensor_copy(core.mask_h[name][:], core.mask[name][:])

        @block.tensor
        def _(pe):
            pe.wait_ge(loaded, 16 * loads)
            for i, (_, t, _, _, _, n) in enumerate(raw):
                if i >= 8:
                    pe.wait_ge(stored, i - 7)
                for k in range(KC):
                    last = nc.tensor.transpose(core.bank[i % 8][:, k * P:k * P + n],
                                               t[0:n, k * P:(k + 1) * P], core.ident[0:n, 0:n])
                last.then_inc(turned, 1)

        @block.vector
        def _(dve):
            for i, (_, _, dst, col, _, n) in enumerate(raw):
                dve.wait_ge(turned, i + 1)
                src = core.bank[i % 8][:, 0:KC * P].rearrange("p (k n) -> p k n", k=KC)
                nc.vector.tensor_copy(dst[:, :, col:col + n], src[:, :, 0:n]).then_inc(stored, 1)


def normalize(core, tag, src, dst, eps=1e-5, turn=True, affine=None):
    nc = core.nc
    stats_done, mv_done, var_ready, std_ready, rstd_done, scaled, normed, turned = (
        core.sem(f"{tag}_{n}") for n in ("stats", "mv", "var", "std", "rstd", "scaled", "normed", "turned"))
    with ExitStack() as ctx:
        stats = ctx.enter_context(nc.sbuf_tensor(f"{tag}_stats_b", [P, TT, 6], F32))
        mv = ctx.enter_context(nc.sbuf_tensor(f"{tag}_mv_b", [P, TT, 2], F32))
        var, std, rstd = (ctx.enter_context(nc.sbuf_tensor(f"{tag}_{n}_b", [P, TT], F32)) for n in ("var", "std", "rstd"))
        block = ctx.enter_context(nc.Block())

        @block.vector
        def _(dve):
            for t in range(TT):
                nc.vector.bn_stats(stats[:, t, :], src[:, t, :]).then_inc(stats_done, 1)
            for t in range(TT):
                dve.wait_ge(stats_done, t + 1)
                nc.vector.bn_aggr(mv[:, t, :], stats[:, t, :]).then_inc(mv_done, 1)
            dve.wait_ge(mv_done, TT)
            nc.vector.tensor_scalar(var[:], mv[:, :, 1], eps, None, ALU.add).then_inc(var_ready, 1)
            dve.wait_ge(std_ready, 1)
            nc.vector.reciprocal(rstd[:], std[:]).then_inc(rstd_done, 1)
            dve.wait_ge(rstd_done, 1)
            n_scaled = 0
            for t in range(TT):
                last = nc.vector.tensor_scalar(dst[:, t, :], src[:, t, :], mv[:, t, 0:1], rstd[:, t:t + 1],
                                               ALU.subtract, ALU.mult)
                if affine is not None:
                    for row, op in zip(affine, (ALU.mult, ALU.add)):
                        last.then_inc(scaled, 1)
                        n_scaled += 1
                        dve.wait_ge(scaled, n_scaled)
                        last = nc.vector.tensor_tensor(dst[:, t, :], dst[:, t, :], row[:], op)
                last.then_inc(normed, 1)
            if turn:
                for h in range(2):
                    dve.wait_ge(turned, 4 * h + 4)
                    nc.vector.tensor_copy(core.xT[:, 1, h * HALF:(h + 1) * HALF], core.bank[2 * h + 1][:])

        @block.scalar
        def _(act):
            act.wait_ge(var_ready, 1)
            nc.scalar.activation(std[:], var[:], ACT.Sqrt).then_inc(std_ready, 1)
            if turn:
                for h in range(2):
                    act.wait_ge(turned, 4 * h + 4)
                    nc.scalar.copy(core.xT[:, 0, h * HALF:(h + 1) * HALF], core.bank[2 * h][:])

        if turn:
            @block.tensor
            def _(pe):
                for t in range(TT):
                    pe.wait_ge(normed, t + 1)
                    for k in range(KC):
                        last = nc.tensor.transpose(core.bank[2 * (t // 4) + k][:, (t % 4) * P:(t % 4 + 1) * P],
                                                   dst[:, t, k * P:(k + 1) * P], core.ident[:])
                    last.then_inc(turned, 1)


def ffn(core, tag):
    nc = core.nc
    up_ready, up_stored, out_ready, logits_ready, sorted_, diff, exped, step, added = (
        core.sem(f"{tag}_{n}") for n in ("up", "ups", "out", "lg", "sort", "diff", "exp", "step", "added"))
    with ExitStack() as ctx:
        hT = ctx.enter_context(nc.sbuf_tensor(f"{tag}_hT", [P, KC, T], F32))
        top = ctx.enter_context(nc.sbuf_tensor(f"{tag}_top", [P, TT, ROUTES], F32))
        d21 = ctx.enter_context(nc.sbuf_tensor(f"{tag}_d21", [P, TT], F32))
        e21 = ctx.enter_context(nc.sbuf_tensor(f"{tag}_e21", [P, TT], F32))
        den = ctx.enter_context(nc.sbuf_tensor(f"{tag}_den", [P, TT], F32))
        w1 = ctx.enter_context(nc.sbuf_tensor(f"{tag}_w1", [P, TT], F32))
        w2 = ctx.enter_context(nc.sbuf_tensor(f"{tag}_w2", [P, TT], F32))
        wsum = ctx.enter_context(nc.sbuf_tensor(f"{tag}_wsum", [P, TT], F32))
        block = ctx.enter_context(nc.Block())
        lg = core.bank[7]

        @block.tensor
        def _(pe):
            for t in range(TT):
                for k in range(KC):
                    last = nc.tensor.matmul(lg[:, t * ROUTES:(t + 1) * ROUTES], core.xT[:, k, t * P:(t + 1) * P],
                                            core.wrt[:, k, :], start=(k == 0), stop=(k == KC - 1))
            last.then_inc(logits_ready, 1)
            for u in range(4):
                m, h = u % 2, u // 2
                for k in range(KC):
                    last = nc.tensor.matmul(core.bank[u][:], core.wup[:, k, m * P:(m + 1) * P],
                                            core.xT[:, k, h * HALF:(h + 1) * HALF], start=(k == 0), stop=(k == KC - 1))
                last.then_inc(up_ready, 1)
            for t in range(TT):
                pe.wait_ge(up_stored, 2 * (t // 4) + 2)
                b = 4 + t % 3
                if t >= 3:
                    pe.wait_ge(added, t - 2)
                for k in range(KC):
                    nc.tensor.matmul(core.bank[b][:, 0:D], hT[:, k, t * P:(t + 1) * P], core.wdn[:, k, :],
                                     start=(k == 0), stop=(k == KC - 1))
                for k in range(KC):
                    last = nc.tensor.matmul(core.bank[b][:, D:2 * D], core.xT[:, k, t * P:(t + 1) * P],
                                            core.wex[:, k, :], start=(k == 0), stop=(k == KC - 1))
                last.then_inc(out_ready, 1)

        @block.scalar
        def _(act):
            act.wait_ge(diff, 1)
            nc.scalar.activation(e21[:], d21[:], ACT.Exp).then_inc(exped, 1)
            for u in range(4):
                m, h = u % 2, u // 2
                act.wait_ge(up_ready, u + 1)
                nc.scalar.activation(hT[:, m, h * HALF:(h + 1) * HALF], core.bank[u][:], ACT.Relu).then_inc(up_stored, 1)

        @block.vector
        def _(dve):
            dve.wait_ge(logits_ready, 1)
            for t in range(TT):
                nc.vector.max(top[:, t, :], lg[:, t * ROUTES:(t + 1) * ROUTES]).then_inc(sorted_, 1)
            dve.wait_ge(sorted_, TT)
            nc.vector.tensor_tensor(d21[:], top[:, :, 1], top[:, :, 0], ALU.subtract).then_inc(diff, 1)
            dve.wait_ge(exped, 1)
            nc.vector.tensor_scalar(den[:], e21[:], 1.0, None, ALU.add).then_inc(step, 1)
            dve.wait_ge(step, 1)
            nc.vector.reciprocal(w1[:], den[:]).then_inc(step, 1)
            dve.wait_ge(step, 2)
            nc.vector.tensor_tensor(w2[:], e21[:], w1[:], ALU.mult).then_inc(step, 1)
            dve.wait_ge(step, 3)
            nc.vector.tensor_tensor(wsum[:], w1[:], w2[:], ALU.add).then_inc(step, 1)
            dve.wait_ge(step, 4)
            for t in range(TT):
                b = 4 + t % 3
                dve.wait_ge(out_ready, t + 1)
                nc.vector.tensor_tensor(core.x[:, t, :], core.x[:, t, :], core.bank[b][:, 0:D], ALU.add).then_inc(step, 1)
                dve.wait_ge(step, 5 + t)
                nc.vector.scalar_tensor_tensor(out=core.x[:, t, :], in0=core.bank[b][:, D:2 * D],
                                               scalar=wsum[:, t:t + 1], in1=core.x[:, t, :],
                                               op0=ALU.mult, op1=ALU.add).then_inc(added, 1)


def finish(core):
    nc = core.nc
    out_stored = core.sem("out_stored")
    with nc.Block() as block:
        @block.sync
        def _(sp):
            sp.dma_start(core.dram["out"].rearrange("b (t p) d -> p (b t) d", p=P), core.x[:]).then_inc(out_stored, 16)
            sp.wait_ge(out_stored, 16)


def moe(core, tag):
    routing_weights(core, tag)
    experts(core, tag)


def routing_weights(core, tag):
    nc = core.nc
    logits_ready, copied, max_ready, exped, recip_ready, probs_ready, top_ready, replaced = (
        core.sem(f"{tag}_{n}") for n in ("lg", "lgc", "max", "exp", "rec", "prob", "top", "repl"))
    sum_ready, scale_ready, kept, weighted, gate_loaded, turned, rows_copied, rows_stored = (
        core.sem(f"{tag}_{n}") for n in ("sum", "scale", "kept", "wtd", "gate", "turned", "rows", "rst"))
    core.rw_dram = nc.dram_tensor(f"{tag}_rw_dram", (EXPERTS, T), F32, kind="Internal").ap()
    with ExitStack() as ctx:
        def sb(name, shape):
            return ctx.enter_context(nc.sbuf_tensor(f"{tag}_{name}", shape, F32))

        wr = sb("wr", [P, KC, EXPERTS])
        lg = sb("lg_b", [P, TT, EXPERTS])
        probs = sb("probs", [P, TT, EXPERTS])
        repl = sb("repl_b", [P, TT, EXPERTS])
        top = sb("top_b", [P, TT, TOP])
        big, total, rtotal, tsum, rtsum = (sb(n, [P, TT]) for n in ("big", "total", "rtotal", "tsum", "rtsum"))
        rwT = sb("rwT", [EXPERTS, T])
        block = ctx.enter_context(nc.Block())

        @block.sync
        def _(sp):
            sp.dma_start(wr[:], core.dram["L0_ffn_gate_w"].rearrange("(k p) e -> p k e", p=P)).then_inc(gate_loaded, 16)
            sp.wait_ge(rows_copied, 2)
            sp.dma_start(core.rw_dram, rwT[:]).then_inc(rows_stored, 16)
            sp.wait_ge(rows_stored, 16)

        @block.tensor
        def _(pe):
            pe.wait_ge(gate_loaded, 16)
            for t in range(TT):
                for k in range(KC):
                    last = nc.tensor.matmul(core.bank[0][:, t * EXPERTS:(t + 1) * EXPERTS],
                                            core.xT[:, k, t * P:(t + 1) * P], wr[:, k, :],
                                            start=(k == 0), stop=(k == KC - 1))
            last.then_inc(logits_ready, 1)
            pe.wait_ge(weighted, 1)
            for t in range(TT):
                last = nc.tensor.transpose(core.bank[1 + t // 4][0:EXPERTS, (t % 4) * P:(t % 4 + 1) * P],
                                           probs[:, t, :], core.ident[:])
            last.then_inc(turned, 1)

        @block.scalar
        def _(act):
            act.wait_ge(max_ready, 1)
            nc.scalar.activation(lg[:], lg[:], ACT.Exp).then_inc(exped, 1)
            act.wait_ge(turned, 1)
            nc.scalar.copy(rwT[:, 0:HALF], core.bank[1][0:EXPERTS, :]).then_inc(rows_copied, 1)

        @block.vector
        def _(dve):
            def rows(v):
                return v[:].unsqueeze(2).broadcast_to([P, TT, EXPERTS])

            dve.wait_ge(logits_ready, 1)
            raw = core.bank[0][:].rearrange("p (t e) -> p t e", e=EXPERTS)
            nc.vector.tensor_reduce(big[:], raw, AX_X, ALU.max).then_inc(copied, 1)
            dve.wait_ge(copied, 1)
            nc.vector.tensor_tensor(lg[:], raw, rows(big), ALU.subtract).then_inc(max_ready, 1)
            dve.wait_ge(exped, 1)
            nc.vector.tensor_reduce(total[:], lg[:], AX_X, ALU.add).then_inc(recip_ready, 1)
            dve.wait_ge(recip_ready, 1)
            nc.vector.reciprocal(rtotal[:], total[:]).then_inc(recip_ready, 1)
            dve.wait_ge(recip_ready, 2)
            nc.vector.tensor_tensor(probs[:], lg[:], rows(rtotal), ALU.mult).then_inc(probs_ready, 1)
            dve.wait_ge(probs_ready, 1)
            for t in range(TT):
                nc.vector.max(top[:, t, :], probs[:, t, :]).then_inc(top_ready, 1)
            for t in range(TT):
                dve.wait_ge(top_ready, t + 1)
                nc.vector.match_replace(repl[:, t, :], top[:, t, :], probs[:, t, :], -1.0).then_inc(replaced, 1)
            nc.vector.tensor_reduce(tsum[:], top[:], AX_X, ALU.add).then_inc(sum_ready, 1)
            dve.wait_ge(sum_ready, 1)
            nc.vector.reciprocal(rtsum[:], tsum[:]).then_inc(scale_ready, 1)
            dve.wait_ge(replaced, TT)
            nc.vector.tensor_scalar(repl[:], repl[:], 0.0, None, ALU.max).then_inc(kept, 1)
            dve.wait_ge(kept, 1)
            nc.vector.tensor_tensor(probs[:], probs[:], repl[:], ALU.subtract).then_inc(kept, 1)
            dve.wait_ge(kept, 2)
            dve.wait_ge(scale_ready, 1)
            nc.vector.tensor_tensor(probs[:], probs[:], rows(rtsum), ALU.mult).then_inc(weighted, 1)
            dve.wait_ge(turned, 1)
            nc.vector.tensor_copy(rwT[:, HALF:T], core.bank[2][0:EXPERTS, :]).then_inc(rows_copied, 1)


def experts(core, tag):
    nc, dram = core.nc, core.dram
    UNITS = 2 * GC
    BODY = 2 * UNITS
    TURNS = GROUPS // 2
    N_UNITS = GROUPS * UNITS
    w_loaded = [core.sem(f"{tag}_wld{s}") for s in range(2)]
    r_loaded = [core.sem(f"{tag}_rld{s}") for s in range(2)]
    gu_ready, silu_done, weighted, inner_ready, down_done, summed, sum_copied, turned, added = (
        core.sem(f"{tag}_{n}") for n in ("gu", "silu", "w2", "inner", "down", "summed", "scp", "st", "sadd"))
    spans = []
    for j in range(GC):
        for e in range(GE):
            a, b = max(j * P, e * INTER), min((j + 1) * P, (e + 1) * INTER)
            if a < b:
                spans.append((j, e, a - j * P, b - j * P))
    W_DMAS, R_DMAS = 2 * KC + 1, len(spans)
    with ExitStack() as ctx:
        def sb(name, shape):
            return ctx.enter_context(nc.sbuf_tensor(f"{tag}_{name}", shape, F32))

        wg, wu = sb("wg", [P, 2, KC, GE * INTER]), sb("wu", [P, 2, KC, GE * INTER])
        wd = sb("wd", [P, 2, GC, D])
        rw = sb("rw", [P, 2, GC, T])
        silu, wsilu, inner = (sb(n, [P, 2, HALF]) for n in ("silu_b", "wsilu", "inner_b"))
        oT = sb("oT", [P, KC, T])
        block = ctx.enter_context(nc.Block())
        gbank, ubank, obank = core.bank[0:2], core.bank[2:4], core.bank[4:8]
        gate_dram = dram["L0_ffn_w_gate"].rearrange("e (k p) i -> k p e i", p=P)
        up_dram = dram["L0_ffn_w_up"].rearrange("e (k p) i -> k p e i", p=P)
        down_dram = dram["L0_ffn_w_down"].rearrange("e i n -> (e i) n").rearrange("(j p) n -> p j n", p=P)

        @block.sync
        def _(sp):
            def load_group(g, s):
                for k in range(KC):
                    for w, src in ((wg, gate_dram), (wu, up_dram)):
                        sp.dma_start(w[:, s, k, :].rearrange("p (e i) -> p e i", e=GE),
                                     src[k][:, bass.ds(g * GE, GE), :]).then_inc(w_loaded[s], 16)
                sp.dma_start(wd[:, s, :, :], down_dram[:, bass.ds(g * GC, GC), :]).then_inc(w_loaded[s], 16)
                for j, e, a, b in spans:
                    sp.dma_start(rw[a:b, s, j, :],
                                 core.rw_dram[bass.ds(g * GE + e, 1), :].broadcast_to([b - a, T])).then_inc(r_loaded[s], 16)

            for s in range(2):
                load_group(s, s)
            with sp.Fori(1, TURNS) as i:
                for s in range(2):
                    sp.wait_ge(down_done, BODY * i + UNITS * (s - 1))
                    load_group(2 * i + s, s)

        @block.tensor
        def _(pe):
            def gate_up(i, u):
                s, j, h = u // UNITS, u % UNITS // 2, u % 2
                if h == 0 and j == 0:
                    pe.wait_ge(w_loaded[s], 16 * W_DMAS * (i + 1))
                if not (isinstance(i, int) and i == 0 and u < 2):
                    pe.wait_ge(inner_ready, BODY * i + u - 1)
                for w, bank in ((wg, gbank), (wu, ubank)):
                    for k in range(KC):
                        last = nc.tensor.matmul(bank[u % 2][:], w[:, s, k, j * P:(j + 1) * P],
                                                core.xT[:, k, h * HALF:(h + 1) * HALF], start=(k == 0), stop=(k == KC - 1))
                last.then_inc(gu_ready, 1)

            def down(i, u):
                s, j, h = u // UNITS, u % UNITS // 2, u % 2
                pe.wait_ge(inner_ready, BODY * i + u + 1)
                for m in range(KC):
                    last = nc.tensor.matmul(obank[2 * h + m][:], wd[:, s, j, m * P:(m + 1) * P], inner[:, u % 2, :],
                                            start=False, stop=False, skip_group_check=True)
                last.then_inc(down_done, 1)

            def turn(i, final=False):
                for u in range(BODY):
                    if u < BODY - 1:
                        gate_up(i, u + 1)
                    elif not final:
                        gate_up(i + 1, 0)
                    down(i, u)

            for b in range(4):
                nc.tensor.matmul(obank[b][:], core.zero_h[:, 0:P], core.zero_h[:], start=True, stop=False,
                                 skip_group_check=True)
            gate_up(0, 0)
            turn(0)
            with pe.Fori(1, TURNS - 1) as i:
                turn(i)
            turn(TURNS - 1, final=True)
            for b in range(4):
                last = nc.tensor.matmul(obank[b][:], core.zero_h[:, 0:P], core.zero_h[:], start=False, stop=True,
                                        skip_group_check=True)
            last.then_inc(summed, 1)
            for t in range(TT):
                pe.wait_ge(sum_copied, 2 * (t // 4) + 2)
                if t >= 4:
                    pe.wait_ge(added, t - 3)
                for m in range(KC):
                    last = nc.tensor.transpose(core.bank[t % 4][:, m * P:(m + 1) * P], oT[:, m, t * P:(t + 1) * P],
                                               core.ident[:])
                last.then_inc(turned, 1)

        @block.scalar
        def _(act):
            def turn(i):
                for u in range(BODY):
                    act.wait_ge(gu_ready, BODY * i + u + 1)
                    if not (isinstance(i, int) and i == 0 and u < 2):
                        act.wait_ge(weighted, BODY * i + u - 1)
                    nc.scalar.activation(silu[:, u % 2, :], gbank[u % 2][:], ACT.Silu).then_inc(silu_done, 1)

            turn(0)
            with act.Fori(1, TURNS) as i:
                turn(i)
            act.wait_ge(summed, 1)
            for b in range(4):
                h, m = b // 2, b % 2
                nc.scalar.copy(oT[:, m, h * HALF:(h + 1) * HALF], obank[b][:]).then_inc(sum_copied, 1)

        @block.gpsimd
        def _(pool):
            def turn(i):
                for u in range(BODY):
                    s, j, h = u // UNITS, u % UNITS // 2, u % 2
                    if h == 0 and j == 0:
                        pool.wait_ge(r_loaded[s], 16 * R_DMAS * (i + 1))
                    pool.wait_ge(silu_done, BODY * i + u + 1)
                    if not (isinstance(i, int) and i == 0 and u < 2):
                        pool.wait_ge(inner_ready, BODY * i + u - 1)
                    nc.gpsimd.tensor_tensor(wsilu[:, u % 2, :], silu[:, u % 2, :],
                                            rw[:, s, j, h * HALF:(h + 1) * HALF], ALU.mult).then_inc(weighted, 1)

            turn(0)
            with pool.Fori(1, TURNS) as i:
                turn(i)

        @block.vector
        def _(dve):
            def turn(i):
                for u in range(BODY):
                    dve.wait_ge(weighted, BODY * i + u + 1)
                    if not (isinstance(i, int) and i == 0 and u < 2):
                        dve.wait_ge(down_done, BODY * i + u - 1)
                    nc.vector.tensor_tensor(inner[:, u % 2, :], ubank[u % 2][:], wsilu[:, u % 2, :],
                                            ALU.mult).then_inc(inner_ready, 1)

            turn(0)
            with dve.Fori(1, TURNS) as i:
                turn(i)
            for t in range(TT):
                dve.wait_ge(turned, t + 1)
                nc.vector.tensor_tensor(core.x[:, t, :], core.x[:, t, :], core.bank[t % 4][:, 0:D], ALU.add).then_inc(added, 1)


class Attention:

    def __init__(self, kv_heads, rotation, maxima, units):
        self.kv_heads, self.rotation, self.maxima, self.units = kv_heads, rotation, maxima, units
        self.qk_heads = HEADS + kv_heads
        self.width = (HEADS + 2 * kv_heads) * HD
        self.k_chunks = -(-kv_heads * HD // P)
        self.chunks = HEADS * HD // P + self.k_chunks


def _blocks_seen():
    maxima = [[(k, min(HALF, (t + 1) * P - k), None) for k in range(0, (t + 1) * P, HALF)] for t in range(TT)]
    units = []
    for s in range(TT):
        for q in range(s * P // HALF * HALF, T, HALF):
            q0 = max(q, s * P)
            units.append((s * P, P, q0, q + HALF - q0, []))
    return maxima, units


def _window_seen(sink=4):
    maxima = [[(0, P, "causal")], [(0, P, "prev1"), (P, P, "causal")]]
    maxima += [[(0, sink, None), ((t - 1) * P, P, "prev"), (t * P, P, "causal")] for t in range(2, TT)]
    units = []
    for s in range(TT):
        masks = [(0, "causalT")] + ([(P, "prev1T" if s == 0 else "prevT")] if s < TT - 1 else [])
        units.append((s * P, P, s * P, P * len(masks), masks))
    units += [(0, P, q, 3 * P, [(c, "sinkT") for c in range(0, 3 * P, P)]) for q in (2 * P, 5 * P)]
    return maxima, units


def _all_seen():
    maxima = [[(0, HALF, None), (HALF, HALF, None)] for _ in range(TT)]
    units = [(s * P, P, q, HALF, []) for s in range(TT) for q in (0, HALF)]
    return maxima, units


ATT_A = Attention(4, "halves", *_blocks_seen())
ATT_B = Attention(4, None, *_window_seen())
ATT_C = Attention(16, "pairs", *_all_seen())


def attention(core, tag, cfg):
    with ExitStack() as ctx:
        def sb(name, shape, dt):
            return ctx.enter_context(core.nc.sbuf_tensor(f"{tag}_{name}", shape, dt))

        v = sb("v", [P, TT, cfg.kv_heads, HD + 1], F32)
        qs = sb("qs", [KROWS, HEADS, T], BF16)
        ks = sb("ks", [KROWS, cfg.kv_heads, T], BF16)
        project_and_stack(core, tag, cfg, v, qs, ks)
        ctxs = sb("ctxs", [P, TT, HEADS * HD], F32)
        attend(core, tag, cfg, v, qs, ks, ctxs)
        project_out(core, tag, ctxs, extra=core.xn if tag == "c" else None)


def project_and_stack(core, tag, cfg, v, qs, ks):
    nc, dram = core.nc, core.dram
    NQK = cfg.qk_heads * HD
    w_loaded, projected, copied, v_copied, rot, roped, turned = (
        core.sem(f"{tag}_{n}") for n in ("wl", "proj", "cp", "vcp", "rot", "roped", "tqk"))
    ones_made, part1, rest1, part2, part3, parts_stored, stacked = (
        core.sem(f"{tag}_{n}") for n in ("ones", "p1", "r1", "p2", "p3", "pst", "stk"))
    C = cfg.chunks
    parts_dram = nc.dram_tensor(f"{tag}_parts_dram", (PARTS, C, P, T), BF16, kind="Internal").ap()
    rows_of = [P if (j + 1) * P <= NQK else NQK - j * P for j in range(C)]
    rope = cfg.rotation is not None
    if not rope:
        roped = copied
    with ExitStack() as ctx:
        def sb(name, shape, dt=F32):
            return ctx.enter_context(nc.sbuf_tensor(f"{tag}_{name}", shape, dt))

        qk = sb("qk", [P, TT, cfg.qk_heads, HD])
        part = sb("part", [P, PARTS, C, T], BF16)
        rest = sb("rest", [P, 2, HALF])
        if tag == "b":
            w, loads = core.bqkv, []
        else:
            w = sb("wqkv", [P, KC, cfg.width])
            if tag == "a":
                loads = [(w[:, :, 0:256], "L0_attn_a_Wq"), (w[:, :, 256:320], "L0_attn_a_Wk"), (w[:, :, 320:384], "L0_attn_a_Wv")]
            else:
                loads = [(w[:], "L1_attn_a_W_in")]
        if rope:
            cos, sin = sb("cos", [P, TT, HD]), sb("sin", [P, TT, HD])
            turned_qk = sb("turned_qk", [P, 2, cfg.qk_heads, HD])
        n_loads = len(loads) + 2 * rope
        block = ctx.enter_context(nc.Block())

        @block.sync
        def _(sp):
            for dst, name in loads:
                sp.dma_start(dst, dram[name].rearrange("(k p) n -> p k n", p=P)).then_inc(w_loaded, 16)
            if rope:
                for dst, name in ((cos, f"c_cos_{tag}"), (sin, f"c_sin_{tag}")):
                    sp.dma_start(dst[:], dram[name].rearrange("(t p) d -> p t d", p=P)).then_inc(w_loaded, 16)
            for n in range(2 * C):
                h, j = n // C, n % C
                sp.wait_ge(part3, n + 1)
                sp.wait_ge(part2, n + 1)
                sp.wait_ge(part1, n + 1)
                sp.dma_start(parts_dram[:, j, 0:rows_of[j], h * HALF:(h + 1) * HALF].rearrange("a p t -> p a t"),
                             part[0:rows_of[j], :, j, h * HALF:(h + 1) * HALF]).then_inc(parts_stored, 16)
            sp.wait_ge(parts_stored, 16 * 2 * C)
            n_stacks = 0
            for c in range(HEADS * HD // P):
                for g, (pq, pk) in enumerate(PAIRS):
                    todo = [(qs, pq, c)]
                    if c < cfg.k_chunks:
                        todo.append((ks, pk, HEADS * HD // P + c))
                    for dst, which, j in todo:
                        heads = rows_of[j] // HD
                        h0 = 8 * c
                        sp.dma_start(dst[g * HD:(g + 1) * HD, h0:h0 + heads, :],
                                     parts_dram[which, j, 0:rows_of[j], :].rearrange("(h d) t -> d h t", d=HD)
                                     ).then_inc(stacked, 16)
                        n_stacks += 1
            sp.wait_ge(stacked, 16 * n_stacks)

        @block.tensor
        def _(pe):
            if n_loads:
                pe.wait_ge(w_loaded, 16 * n_loads)
            for t in range(TT):
                if t >= 2:
                    pe.wait_ge(copied, t - 1)
                    pe.wait_ge(v_copied, t - 1)
                for n0, b in ([(0, 0)] if cfg.width <= HALF else [(0, 0), (HALF, 1)]):
                    n = min(HALF, cfg.width - n0)
                    for k in range(KC):
                        last = nc.tensor.matmul(core.bank[2 * (t % 2) + b][:, 0:n], core.xT[:, k, t * P:(t + 1) * P],
                                                w[:, k, n0:n0 + n], start=(k == 0), stop=(k == KC - 1))
                last.then_inc(projected, 1)
            for n in range(2 * C):
                h, j = n // C, n % C
                pe.wait_ge(roped, 4 * h + 4)
                if n >= 4:
                    pe.wait_ge(rest1, n - 3)
                for t in range(4 * h, 4 * h + 4):
                    flat = qk[:, t, :, :].rearrange("p h d -> p (h d)")
                    last = nc.tensor.transpose(core.bank[4 + n % 4][0:rows_of[j], (t % 4) * P:(t % 4 + 1) * P],
                                               flat[:, j * P:j * P + rows_of[j]], core.ident[:])
                last.then_inc(turned, 1)

        @block.scalar
        def _(act):
            for t in range(TT):
                act.wait_ge(projected, t + 1)
                nc.scalar.copy(qk[:, t, :, :].rearrange("p h d -> p (h d)"),
                               core.bank[2 * (t % 2)][:, 0:NQK]).then_inc(copied, 1)
            for n in range(2 * C):
                h, j = n // C, n % C
                act.wait_ge(turned, n + 1)
                nc.scalar.copy(part[0:rows_of[j], 0, j, h * HALF:(h + 1) * HALF],
                               core.bank[4 + n % 4][0:rows_of[j], :]).then_inc(part1, 1)

        @block.vector
        def _(dve):
            for t in range(TT):
                dve.wait_ge(projected, t + 1)
                dve.wait_ge(copied, t + 1)
                b, c0 = (2 * (t % 2), NQK) if cfg.width <= HALF else (2 * (t % 2) + 1, 0)
                nc.vector.tensor_copy(v[:, t, :, 0:HD],
                                      core.bank[b][:, c0:c0 + cfg.kv_heads * HD].rearrange("p (h d) -> p h d", d=HD)
                                      ).then_inc(v_copied, 1)
                if not rope:
                    continue
                tq = turned_qk[:, t % 2, :, :]

                def over_heads(table, a, step, n):
                    return table[:, t, a:a + step * (n - 1) + 1:step].unsqueeze(1).broadcast_to([P, cfg.qk_heads, n])

                if cfg.rotation == "halves":
                    moves, step, n_rot = [(0, HD // 2), (HD // 2, 0)], 1, HD // 2
                else:
                    moves, step, n_rot = [(0, 1), (1, 0)], 2, HD // 4
                for to, frm in moves:
                    e = step * (n_rot - 1) + 1
                    nc.vector.tensor_tensor(tq[:, :, to:to + e:step], qk[:, t, :, frm:frm + e:step],
                                            over_heads(sin, to, step, n_rot), ALU.mult).then_inc(rot, 1)
                dve.wait_ge(rot, 3 * t + 2)
                nc.vector.tensor_tensor(qk[:, t, :, :], qk[:, t, :, :], over_heads(cos, 0, 1, HD), ALU.mult).then_inc(rot, 1)
                dve.wait_ge(rot, 3 * t + 3)
                rotated = HD if cfg.rotation == "halves" else HD // 2
                nc.vector.tensor_tensor(qk[:, t, :, 0:rotated], qk[:, t, :, 0:rotated], tq[:, :, 0:rotated],
                                        ALU.add).then_inc(roped, 1)
            for n in range(2 * C):
                h, j = n // C, n % C
                dve.wait_ge(part1, n + 1)
                if n >= 2:
                    dve.wait_ge(part3, n - 1)
                nc.vector.tensor_tensor(rest[0:rows_of[j], n % 2, :], core.bank[4 + n % 4][0:rows_of[j], :],
                                        part[0:rows_of[j], 0, j, h * HALF:(h + 1) * HALF], ALU.subtract).then_inc(rest1, 1)

        @block.gpsimd
        def _(pool):
            pool.memset(v[:, :, :, HD:HD + 1], 1.0).then_inc(ones_made, 1)
            pool.wait_ge(ones_made, 1)
            pool.memset(ks[ROWS:KROWS, :, :], 1.0).then_inc(ones_made, 1)
            pool.wait_ge(ones_made, 2)
            for n in range(2 * C):
                h, j = n // C, n % C
                span = slice(h * HALF, (h + 1) * HALF)
                pool.wait_ge(rest1, n + 1)
                nc.gpsimd.tensor_copy(part[0:rows_of[j], 1, j, span], rest[0:rows_of[j], n % 2, :]).then_inc(part2, 1)
                pool.wait_ge(part2, n + 1)
                nc.gpsimd.tensor_tensor(part[0:rows_of[j], 2, j, span], rest[0:rows_of[j], n % 2, :],
                                        part[0:rows_of[j], 1, j, span], ALU.subtract).then_inc(part3, 1)


def attend(core, tag, cfg, v, qs, ks, ctxs):
    nc = core.nc
    U = len(cfg.units)
    scores_ready, max_done, maxed, shift_step, shift_ready, shift_rows, rows_stored = (
        core.sem(f"{tag}_{n}") for n in ("sc", "mxd", "maxed", "shs", "shr", "shrow", "rst"))
    tsc_ready, probs_ready, probs_used, norm_step, ctx_stored = (
        core.sem(f"{tag}_{n}") for n in ("tsc", "pr", "pu", "nst", "cst"))
    NB = next(n for n in (4, 5, 3, 2) if U % n == 0)
    group = HEADS // cfg.kv_heads
    tiles_at = [[] for _ in range(U)]
    for t in range(TT):
        tiles_at[t * (3 * U // 4) // TT].append(t)
    with ExitStack() as ctx:
        def sb(name, shape, dt=F32):
            return ctx.enter_context(nc.sbuf_tensor(f"{tag}_{name}", shape, dt))

        mx, rest, rden = sb("mx", [P, TT]), sb("mrest", [P, TT]), sb("rden", [P, TT])
        shift = sb("shift", [P, TT, PARTS], BF16)
        probs = sb("probs", [P, NB, HALF])
        block = ctx.enter_context(nc.Block())
        pv = core.bank[6][:, 0:TT * (HD + 1)].rearrange("p (t c) -> p t c", c=HD + 1)

        def kv(h):
            return h // group

        @block.tensor
        def _(pe):
            def maxima(h, t, kvh):
                n = TT * h + t
                if not (isinstance(h, int) and n < 2):
                    pe.wait_ge(max_done, n - 1)
                col = 0
                for k0, nk, mask in cfg.maxima[t]:
                    out = core.psum[:, 2 * (t % 2):2 * (t % 2) + 2, :].rearrange("p b n -> p (b n)")[:, col:col + nk]
                    last = nc.tensor.matmul(out, qs[0:ROWS, h, t * P:(t + 1) * P], ks[0:ROWS, kvh, k0:k0 + nk],
                                            start=True, stop=mask is None, skip_group_check=True)
                    if mask is not None:
                        last = nc.tensor.matmul(out, core.ident_h[:], core.mask_h[mask][:, 0:nk],
                                                start=False, stop=True, skip_group_check=True)
                    col += nk
                last.then_inc(scores_ready, 1)

            def shift_to_rows(h):
                pe.wait_ge(shift_ready, h + 1)
                for half in range(2):
                    n = 2 * h + half
                    if not (isinstance(h, int) and n == 0):
                        pe.wait_ge(rows_stored, n)
                    for t in range(4):
                        last = nc.tensor.matmul(core.bank[7][ROWS:KROWS, t * P:(t + 1) * P], shift[:, 4 * half + t, :],
                                                core.ident_h[:], start=True, stop=True)
                    last.then_inc(shift_rows, 1)

            def scores(h, u, kvh):
                k0, nk, q0, nq, masks = cfg.units[u]
                n = U * h + u
                if u == 0:
                    pe.wait_ge(rows_stored, 2 * h + 2)
                if not (isinstance(h, int) and n < 2):
                    pe.wait_ge(probs_ready, n - 1)
                bank = core.bank[4 + u % 2]
                last = nc.tensor.matmul(bank[0:nk, 0:nq], ks[:, kvh, k0:k0 + nk], qs[:, h, q0:q0 + nq],
                                        start=True, stop=not masks, skip_group_check=True)
                for m, (c0, mask) in enumerate(masks):
                    last = nc.tensor.matmul(bank[:, c0:c0 + P], core.ident_h[:], core.mask_h[mask][:],
                                            start=False, stop=m == len(masks) - 1, skip_group_check=True)
                last.then_inc(tsc_ready, 1)

            def values(h, u, kvh):
                k0, nk, q0, nq, _ = cfg.units[u]
                n = U * h + u
                pe.wait_ge(probs_ready, n + 1)
                if u == 0 and not (isinstance(h, int) and h == 0):
                    pe.wait_ge(ctx_stored, h)
                for q in range(q0, q0 + nq, P):
                    last = nc.tensor.matmul(pv[:, q // P, :], probs[0:nk, u % NB, q - q0:q - q0 + P],
                                            v[0:nk, k0 // P, kvh, :], start=(u == 0 and q == q0),
                                            stop=(u == U - 1 and q == q0 + nq - P), skip_group_check=True)
                last.then_inc(probs_used, 1)

            def head(h, kvh, nxt, kv_nxt):
                for u in range(U):
                    scores(h, u, kvh)
                    if nxt is not None:
                        for t in tiles_at[u]:
                            maxima(nxt, t, kv_nxt)
                    if u >= 1:
                        values(h, u - 1, kvh)
                values(h, U - 1, kvh)
                if nxt is not None:
                    shift_to_rows(nxt)

            for t in range(TT):
                maxima(0, t, 0)
            shift_to_rows(0)
            def turn(g):
                for i in range(UNROLL):
                    h = UNROLL * g + i
                    kv_i = h if group == 1 else g
                    if i < UNROLL - 1:
                        head(h, kv_i, h + 1, h + 1 if group == 1 else g)
                    else:
                        head(h, kv_i, h + 1, h + 1 if group == 1 else g + 1)

            UNROLL = 4
            GS = HEADS // UNROLL
            turn(0)
            with pe.Fori(1, GS - 1) as g:
                turn(g)
            for i in range(UNROLL):
                h = HEADS - UNROLL + i
                nxt = h + 1 if i < UNROLL - 1 else None
                head(h, kv(h), nxt, None if nxt is None else kv(nxt))

        @block.scalar
        def _(act):
            def store_rows(h):
                for half in range(2):
                    act.wait_ge(shift_rows, 2 * h + half + 1)
                    nc.scalar.copy(qs[ROWS:KROWS, h, half * HALF:(half + 1) * HALF],
                                   core.bank[7][ROWS:KROWS, :]).then_inc(rows_stored, 1)

            def head(h, first=False):
                for u in range(U):
                    k0, nk, q0, nq, _ = cfg.units[u]
                    n = U * h + u
                    act.wait_ge(tsc_ready, n + 1)
                    if not (first and u < NB):
                        act.wait_ge(probs_used, n - NB + 1)
                    nc.scalar.activation(probs[0:nk, u % NB, 0:nq], core.bank[4 + u % 2][0:nk, 0:nq], ACT.Exp,
                                         scale=HD ** -0.5).then_inc(probs_ready, 1)

            store_rows(0)
            head(0, first=True)
            with act.Fori(1, HEADS) as h:
                store_rows(h)
                head(h)

        @block.vector
        def _(dve):
            def maxima(h, first=False):
                for t in range(TT):
                    n = TT * h + t
                    dve.wait_ge(scores_ready, n + 1)
                    width = sum(nk for _, nk, _ in cfg.maxima[t])
                    buf = core.psum[:, 2 * (t % 2):2 * (t % 2) + 2, :].rearrange("p b n -> p (b n)")
                    nc.vector.tensor_reduce(mx[:, t:t + 1], buf[:, 0:width], AX_X, ALU.max).then_inc(max_done, 1)
                dve.wait_ge(max_done, TT * h + TT)
                if not first:
                    dve.wait_ge(shift_rows, 2 * h)
                nc.vector.tensor_scalar(shift[:, :, 0], mx[:], -1.0, None, ALU.mult).then_inc(shift_step, 1)
                dve.wait_ge(shift_step, 3 * h + 1)
                nc.vector.scalar_tensor_tensor(out=rest[:], in0=mx[:], scalar=-1.0, in1=shift[:, :, 0],
                                               op0=ALU.mult, op1=ALU.subtract).then_inc(shift_step, 1)
                dve.wait_ge(shift_step, 3 * h + 2)
                nc.vector.tensor_copy(shift[:, :, 1], rest[:]).then_inc(shift_step, 1)
                dve.wait_ge(shift_step, 3 * h + 3)
                nc.vector.tensor_tensor(shift[:, :, 2], rest[:], shift[:, :, 1], ALU.subtract).then_inc(shift_ready, 1)

            def store(h):
                dve.wait_ge(probs_used, U * (h + 1))
                nc.vector.reciprocal(rden[:], pv[:, :, HD]).then_inc(norm_step, 1)
                dve.wait_ge(norm_step, h + 1)
                nc.vector.tensor_tensor(ctxs[:, :, bass.ds(h * HD, HD)], pv[:, :, 0:HD],
                                        rden[:].unsqueeze(2).broadcast_to([P, TT, HD]), ALU.mult).then_inc(ctx_stored, 1)

            maxima(0, first=True)
            with dve.Fori(1, HEADS) as h:
                maxima(h)
                store(h - 1)
            store(HEADS - 1)


def project_out(core, tag, ctxs, extra=None):
    nc, dram = core.nc, core.dram
    wo_loaded, turned, turn_copied, projected, step, added = (
        core.sem(f"{tag}_{n}") for n in ("wol", "tc", "tcc", "po", "poa", "pod"))
    with ExitStack() as ctx:
        ctxT = ctx.enter_context(nc.sbuf_tensor(f"{tag}_ctxT", [P, KC, T], F32))
        wo = core.bwo if tag == "b" else ctx.enter_context(nc.sbuf_tensor(f"{tag}_wo", [P, KC, D], F32))
        block = ctx.enter_context(nc.Block())

        if tag != "b":
            @block.sync
            def _(sp):
                name = {"a": "L0_attn_a_Wo", "c": "L1_attn_a_W_out"}[tag]
                sp.dma_start(wo[:], dram[name].rearrange("(k p) n -> p k n", p=P)).then_inc(wo_loaded, 16)

        @block.tensor
        def _(pe):
            for u in range(4):
                h, k = u // 2, u % 2
                for t in range(4 * h, 4 * h + 4):
                    last = nc.tensor.transpose(core.bank[u][:, (t % 4) * P:(t % 4 + 1) * P],
                                               ctxs[:, t, k * P:(k + 1) * P], core.ident[:])
                last.then_inc(turned, 1)
            if tag != "b":
                pe.wait_ge(wo_loaded, 16)
            for t in range(TT):
                pe.wait_ge(turn_copied, 2 * (t // 4) + 2)
                if t >= 4:
                    pe.wait_ge(added, t - 3)
                for k in range(KC):
                    last = nc.tensor.matmul(core.bank[4 + t % 4][:, 0:D], ctxT[:, k, t * P:(t + 1) * P], wo[:, k, :],
                                            start=(k == 0), stop=(k == KC - 1))
                last.then_inc(projected, 1)

        @block.scalar
        def _(act):
            for u in range(4):
                h, k = u // 2, u % 2
                act.wait_ge(turned, u + 1)
                nc.scalar.copy(ctxT[:, k, h * HALF:(h + 1) * HALF], core.bank[u][:]).then_inc(turn_copied, 1)

        @block.vector
        def _(dve):
            if extra is not None:
                nc.vector.tensor_tensor(core.x[:], core.x[:], extra[:], ALU.add).then_inc(step, 1)
                dve.wait_ge(step, 1)
            for t in range(TT):
                dve.wait_ge(projected, t + 1)
                nc.vector.tensor_tensor(core.x[:, t, :], core.x[:, t, :], core.bank[4 + t % 4][:, 0:D], ALU.add).then_inc(added, 1)


LSCALE = float(np.float32(1.0) / np.sqrt(np.float32(DN + DR)))
LPAIRS = HEADS // 2
UP = DN + DV


def latent(core, tag):
    with ExitStack() as ctx:
        def sb(name, shape, dt=F32):
            return ctx.enter_context(core.nc.sbuf_tensor(f"{tag}_{name}", shape, dt))

        wvo = sb("wvo", [P, LPAIRS, D])
        ctxs = sb("ctxs", [P, TT, HEADS * KVR])
        with ExitStack() as inner:
            def sbi(name, shape, dt=F32):
                return inner.enter_context(core.nc.sbuf_tensor(f"{tag}_{name}", shape, dt))

            wq = sbi("wq", [QR, HEADS, KVR + 2 * DR])
            qcT = sbi("qcT", [QR, T])
            kT = sbi("kT", [P, T])
            v = sbi("v", [P, TT, KVR + 1])
            latent_down(core, tag, qcT, kT, v)
            latent_weights(core, tag, wq, wvo)
            latent_attend(core, tag, wq, qcT, kT, v, ctxs)
        latent_out(core, tag, wvo, ctxs)


def latent_down(core, tag, qcT, kT, v):
    nc, dram = core.nc, core.dram
    W = QR + KVR + DR
    loaded, projected, copied, squared, meaned, rooted, inverted, normed, roped, valued, turned, qk_copied = (
        core.sem(f"{tag}d_{n}") for n in ("ld", "pr", "cp", "sq", "mean", "root", "inv", "norm", "rope", "val", "turn", "qkc"))
    with ExitStack() as ctx:
        def sb(name, shape, dt=F32):
            return ctx.enter_context(nc.sbuf_tensor(f"{tag}d_{name}", shape, dt))

        w = sb("w", [P, KC, W])
        lat = sb("lat", [P, TT, W])
        junk = sb("junk", [P, 2, QR])
        ssq, root, inv = (sb(n, [P, 2, TT]) for n in ("ssq", "rt", "iv"))
        cos, sin = sb("cos", [P, TT, DR]), sb("sin", [P, TT, DR])
        swapped = sb("swapped", [P, TT, DR])
        block = ctx.enter_context(nc.Block())
        spans = ((0, QR, "L1_attn_b_q_norm_w"), (QR, KVR, "L1_attn_b_kv_norm_w"))

        @block.sync
        def _(sp):
            for name, c0, n in (("wq_down", 0, QR), ("wkv_down", QR, KVR), ("wk_rope", QR + KVR, DR)):
                sp.dma_start(w[:, :, c0:c0 + n], dram[f"L1_attn_b_{name}"].rearrange("(k p) n -> p k n", p=P)).then_inc(loaded, 16)
            sp.dma_start(cos[:], dram["c_cos_k"].rearrange("(t p) d -> p t d", p=P)).then_inc(loaded, 16)
            sp.dma_start(sin[:], dram["c_sin_k"].rearrange("(t p) d -> p t d", p=P)).then_inc(loaded, 16)

        @block.tensor
        def _(pe):
            pe.wait_ge(loaded, 80)
            for t in range(TT):
                if t >= 4:
                    pe.wait_ge(copied, t - 3)
                for k in range(KC):
                    last = nc.tensor.matmul(core.bank[t % 4][:, 0:W], core.xT[:, k, t * P:(t + 1) * P], w[:, k, :],
                                            start=(k == 0), stop=(k == KC - 1))
                last.then_inc(projected, 1)
            pe.wait_ge(normed, 4)
            pe.wait_ge(roped, 4)
            for h in range(2):
                for t in range(4 * h, 4 * h + 4):
                    nc.tensor.transpose(core.bank[4 + h][0:QR, (t % 4) * P:(t % 4 + 1) * P], lat[:, t, 0:QR], core.ident[:])
                    last = nc.tensor.transpose(core.bank[6 + h][:, (t % 4) * P:(t % 4 + 1) * P], lat[:, t, QR:W], core.ident[:])
                last.then_inc(turned, 1)

        @block.scalar
        def _(act):
            for t in range(TT):
                act.wait_ge(projected, t + 1)
                nc.scalar.copy(lat[:, t, :], core.bank[t % 4][:, 0:W]).then_inc(copied, 1)
            act.wait_ge(meaned, 2)
            nc.scalar.activation(root[:], ssq[:], ACT.Sqrt).then_inc(rooted, 1)
            for h in range(2):
                act.wait_ge(turned, h + 1)
                nc.scalar.copy(kT[:, h * HALF:(h + 1) * HALF], core.bank[6 + h][:]).then_inc(qk_copied, 1)

        @block.vector
        def _(dve):
            for t in range(TT):
                dve.wait_ge(copied, t + 1)
                for i, (c0, n, _) in enumerate(spans):
                    if t >= 1:
                        dve.wait_ge(squared, 2 * t - 1 + i)
                    nc.vector.tensor_tensor_reduce(junk[:, i, 0:n], lat[:, t, c0:c0 + n], lat[:, t, c0:c0 + n], 1.0, 0.0,
                                                   ALU.mult, ALU.add, ssq[:, i, t:t + 1]).then_inc(squared, 1)
            dve.wait_ge(squared, 2 * TT)
            for i, (c0, n, _) in enumerate(spans):
                nc.vector.tensor_scalar(ssq[:, i, :], ssq[:, i, :], 1.0 / n, 1e-6, ALU.mult, ALU.add).then_inc(meaned, 1)
            dve.wait_ge(rooted, 1)
            nc.vector.reciprocal(inv[:], root[:]).then_inc(inverted, 1)
            dve.wait_ge(inverted, 1)
            for i, (c0, n, _) in enumerate(spans):
                nc.vector.tensor_tensor(lat[:, :, c0:c0 + n], lat[:, :, c0:c0 + n],
                                        inv[:, i, :].unsqueeze(2).broadcast_to([P, TT, n]), ALU.mult).then_inc(normed, 1)
            for i, (c0, n, name) in enumerate(spans):
                dve.wait_ge(normed, i + 1)
                nc.vector.tensor_tensor(lat[:, :, c0:c0 + n], lat[:, :, c0:c0 + n],
                                        core.row[name][:].unsqueeze(1).broadcast_to([P, TT, n]), ALU.mult).then_inc(normed, 1)
            k0 = QR + KVR
            for to, frm in ((0, 1), (1, 0)):
                nc.vector.tensor_tensor(swapped[:, :, to:to + DR - 1:2], lat[:, :, k0 + frm:k0 + frm + DR - 1:2],
                                        sin[:, :, to:to + DR - 1:2], ALU.mult).then_inc(roped, 1)
            dve.wait_ge(roped, 2)
            nc.vector.tensor_tensor(lat[:, :, k0:W], lat[:, :, k0:W], cos[:], ALU.mult).then_inc(roped, 1)
            dve.wait_ge(roped, 3)
            nc.vector.tensor_tensor(lat[:, :, k0:W], lat[:, :, k0:W], swapped[:], ALU.add).then_inc(roped, 1)
            dve.wait_ge(normed, 4)
            nc.vector.tensor_copy(v[:, :, 0:KVR], lat[:, :, QR:QR + KVR]).then_inc(valued, 1)
            nc.vector.memset(v[:, :, KVR:KVR + 1], 1.0).then_inc(valued, 1)
            for h in range(2):
                dve.wait_ge(turned, h + 1)
                nc.vector.tensor_copy(qcT[:, h * HALF:(h + 1) * HALF], core.bank[4 + h][0:QR, :]).then_inc(qk_copied, 1)


def latent_weights(core, tag, wq, wvo):
    nc, dram = core.nc, core.dram
    up_loaded, rope_copied, turned, turn_copied, folded, fold_copied = (
        core.sem(f"{tag}w_{n}") for n in ("ld", "rc", "turn", "tc", "fold", "fc"))
    NT = QR + 2 * KVR
    with ExitStack() as ctx:
        def sb(name, shape, dt=F32):
            return ctx.enter_context(nc.sbuf_tensor(f"{tag}w_{name}", shape, dt))

        wqu = sb("wqu", [QR, HEADS * DN])
        wkv = sb("wkv", [KVR, HEADS * UP])
        wo = sb("wo", [P, HEADS, D])
        wr = sb("wr", [QR, HEADS, DR])
        wt = sb("wt", [P, 2, NT])
        block = ctx.enter_context(nc.Block())

        @block.sync
        def _(sp):
            sp.dma_start(wqu[:], dram["L1_attn_b_wq_up"]).then_inc(up_loaded, 16)
            sp.dma_start(wkv[:], dram["L1_attn_b_wkv_up"]).then_inc(up_loaded, 16)
            sp.dma_start(wr[:], dram["L1_attn_b_wq_rope"].rearrange("r (h d) -> r h d", d=DR)).then_inc(up_loaded, 16)
            sp.dma_start(wo[:], dram["L1_attn_b_wo"].rearrange("(h p) n -> p h n", p=P)).then_inc(up_loaded, 16)

        @block.gpsimd
        def _(pool):
            pool.wait_ge(up_loaded, 64)
            nc.gpsimd.tensor_copy(wq[:, :, KVR:KVR + DR], wr[:]).then_inc(rope_copied, 1)
            for n, (to, frm) in enumerate(((0, 1), (1, 0))):
                pool.wait_ge(rope_copied, n + 1)
                nc.gpsimd.tensor_copy(wq[:, :, KVR + DR + to:KVR + 2 * DR:2], wr[:, :, frm:DR:2]).then_inc(rope_copied, 1)

        @block.tensor
        def _(pe):
            pe.wait_ge(up_loaded, 64)

            def turn(h):
                if h >= 2:
                    pe.wait_ge(turn_copied, h - 1)
                b = core.bank[h % 2]
                nc.tensor.transpose(b[:, 0:QR], wqu[:, h * DN:(h + 1) * DN], core.ident[0:QR, 0:QR])
                nc.tensor.transpose(b[:, QR:QR + KVR], wkv[:, h * UP:h * UP + DN], core.ident[0:KVR, 0:KVR])
                nc.tensor.transpose(b[:, QR + KVR:NT], wkv[:, h * UP + DN:(h + 1) * UP],
                                    core.ident[0:KVR, 0:KVR]).then_inc(turned, 1)

            def fold(h):
                pe.wait_ge(turn_copied, h + 1)
                if h >= 2:
                    pe.wait_ge(fold_copied, 2 * (h - 1))
                t = wt[:, h % 2, :]
                p0 = KVR * (h % 2)
                nc.tensor.matmul(core.bank[2 + h % 2][0:QR, 0:KVR], t[:, 0:QR], t[:, QR:QR + KVR], start=True, stop=True)
                nc.tensor.matmul(core.bank[4 + h % 2][p0:p0 + KVR, 0:D], t[:, QR + KVR:NT], wo[:, h, :],
                                 start=True, stop=True).then_inc(folded, 1)

            turn(0)
            for h in range(HEADS):
                if h + 1 < HEADS:
                    turn(h + 1)
                fold(h)

        @block.vector
        def _(dve):
            def turned_out(h):
                dve.wait_ge(turned, h + 1)
                if h >= 2:
                    dve.wait_ge(folded, h - 1)
                nc.vector.tensor_copy(wt[:, h % 2, :], core.bank[h % 2][:, 0:NT]).then_inc(turn_copied, 1)

            turned_out(0)
            for h in range(HEADS):
                if h + 1 < HEADS:
                    turned_out(h + 1)
                dve.wait_ge(folded, h + 1)
                nc.vector.tensor_copy(wq[:, h, 0:KVR], core.bank[2 + h % 2][0:QR, 0:KVR]).then_inc(fold_copied, 1)
                p0 = KVR * (h % 2)
                nc.vector.tensor_copy(wvo[p0:p0 + KVR, h // 2, :], core.bank[4 + h % 2][p0:p0 + KVR, 0:D]).then_inc(fold_copied, 1)


def latent_attend(core, tag, wq, qcT, kT, v, ctxs):
    nc, dram = core.nc, core.dram
    tab_loaded, w_placed, proj_ready, lat_copied, proj_used, q_ready = (
        core.sem(f"{tag}a_{n}") for n in ("tab", "wpl", "pj", "lc", "pjd", "qr"))
    score_ready, negmax_ready, exp_done, turned, turn_copied, pv_done, norm_step, ctx_stored = (
        core.sem(f"{tag}a_{n}") for n in ("sc", "nm", "ex", "tu", "tcp", "pv", "ns", "cs"))
    NP_, NT_ = 4, 4
    STEPS = 2 * TT
    TURNS = HEADS // 2
    batches = [[list(range(b, min(b + 4, t + 1))) for b in range(0, t + 1, 4)] for t in range(TT)]
    before = [sum(len(b) for b in batches[:t]) for t in range(TT + 1)]
    NBAT = before[TT]
    assert NBAT % NT_ == 0 and STEPS % NP_ == 0
    PROJ_AT = {0: 0, 2: 1, 4: 2, 6: 3}
    with ExitStack() as ctx:
        def sb(name, shape, dt=F32):
            return ctx.enter_context(nc.sbuf_tensor(f"{tag}a_{name}", shape, dt))

        cos, sin = sb("cos", [P, T]), sb("sin", [P, T])
        wh = sb("wh", [QR, 2, KVR + 2 * DR])
        q = sb("q", [P, 2, T])
        swapped = sb("swapped", [P, T])
        negmax = sb("negmax", [P, 2])
        rden = sb("rden", [P, 2])
        probs = sb("probs", [P, NP_, T])
        probsT = sb("probsT", [P, NT_, HALF])
        block = ctx.enter_context(nc.Block())
        pv = core.bank[6][:, 0:KVR + 1]

        def known(i, s):
            return isinstance(i, int)

        def head_of(i, s):
            return 2 * i + s // TT

        def through(i, s, back):
            s2 = s - back
            return NBAT * 2 * i + NBAT * (s2 // TT) + before[s2 % TT + 1]

        def scores_of(n2):
            return core.psum[:, 2 * n2:2 * n2 + 2, :].rearrange("p b n -> p (b n)")

        @block.sync
        def _(sp):
            sp.dma_start(cos[KVR:P, :], dram["c_cos_q"]).then_inc(tab_loaded, 16)
            sp.dma_start(sin[KVR:P, :], dram["c_sin_q"]).then_inc(tab_loaded, 16)

        @block.tensor
        def _(pe):
            def project(h, slot, c):
                half = c % 2
                if c == 0:
                    pe.wait_ge(w_placed, h + 1)
                if not (isinstance(h, int) and h == 0 and c == 0):
                    pe.wait_ge(proj_used, 4 * h + c)
                if c in (1, 2):
                    pe.wait_ge(lat_copied, 2 * h + c)
                rhs = qcT[:, half * HALF:(half + 1) * HALF]
                if c < 2:
                    last = nc.tensor.matmul(core.bank[7][:], wh[:, slot, 0:KVR + DR], rhs, start=True, stop=True)
                else:
                    last = nc.tensor.matmul(core.bank[7][KVR:P, :], wh[:, slot, KVR + DR:KVR + 2 * DR], rhs, start=True, stop=True)
                last.then_inc(proj_ready, 1)

            def score(i, s):
                h, t = head_of(i, s), s % TT
                if t == 0:
                    pe.wait_ge(q_ready, 2 * h + 2)
                    pe.wait_ge(lat_copied, 2 * h + 2)
                if not (known(i, s) and STEPS * i + s < 2):
                    pe.wait_ge(exp_done, STEPS * i + s - 1)
                out = scores_of(s % 2)
                for k0 in range(0, (t + 1) * P, HALF):
                    nk = min(HALF, (t + 1) * P - k0)
                    nc.tensor.matmul(out[:, k0:k0 + nk], q[:, s // TT % 2, t * P:(t + 1) * P], kT[:, k0:k0 + nk],
                                     start=True, stop=False, skip_group_check=True)
                nc.tensor.matmul(out[:, t * P:(t + 1) * P], core.ident_h[:], core.mask_h["causal"][:],
                                 start=False, stop=True, skip_group_check=True).then_inc(score_ready, 1)

            def back(i, s):
                s2 = s - 2
                t = s2 % TT
                first = through(i, s, 2) - len(batches[t])
                for b, blocks in enumerate(batches[t]):
                    if b == 0:
                        pe.wait_ge(exp_done, STEPS * i + s2 + 1)
                    if not (known(i, s) and first + b < 2):
                        pe.wait_ge(turn_copied, first + b - 1)
                    for x, k in enumerate(blocks):
                        last = nc.tensor.transpose(core.bank[4 + (before[t] + b) % 2][:, x * P:(x + 1) * P],
                                                   probs[:, s2 % NP_, k * P:(k + 1) * P], core.ident[:])
                    last.then_inc(turned, 1)
                for b, blocks in enumerate(batches[t]):
                    pe.wait_ge(turn_copied, first + b + 1)
                    if b == 0 and not (known(i, s) and STEPS * i + s2 == 0):
                        pe.wait_ge(ctx_stored, STEPS * i + s2)
                    for x, k in enumerate(blocks):
                        last = nc.tensor.matmul(pv, probsT[:, (before[t] + b) % NT_, x * P:(x + 1) * P], v[:, k, :],
                                                start=(k == 0), stop=(k == t))
                    last.then_inc(pv_done, 1)

            def turn(i, final=False):
                for s in range(STEPS):
                    score(i, s)
                    if s % TT in PROJ_AT and not (final and s >= TT):
                        project(head_of(i, s) + 1, (s // TT + 1) % 2, PROJ_AT[s % TT])
                    if not (known(i, s) and STEPS * i + s < 2):
                        back(i, s)

            for c in range(4):
                project(0, 0, c)
            turn(0)
            with pe.Fori(1, TURNS - 1) as i:
                turn(i)
            turn(TURNS - 1, final=True)
            back(TURNS - 1, STEPS)
            back(TURNS - 1, STEPS + 1)

        @block.scalar
        def _(act):
            def copy_latent(h, slot, c):
                act.wait_ge(proj_ready, 4 * h + c + 1)
                nc.scalar.activation(q[0:KVR, slot, c * HALF:(c + 1) * HALF], core.bank[7][0:KVR, :], ACT.Copy,
                                     scale=LSCALE).then_inc(lat_copied, 1)

            def copy_turned(i, s):
                s2 = s - 2
                t = s2 % TT
                first = through(i, s, 2) - len(batches[t])
                for b, blocks in enumerate(batches[t]):
                    act.wait_ge(turned, first + b + 1)
                    if not (known(i, s) and first + b < NT_):
                        act.wait_ge(pv_done, first + b - NT_ + 1)
                    n = len(blocks) * P
                    nc.scalar.copy(probsT[:, (before[t] + b) % NT_, 0:n],
                                   core.bank[4 + (before[t] + b) % 2][:, 0:n]).then_inc(turn_copied, 1)

            def turn(i, final=False):
                for s in range(STEPS):
                    t = s % TT
                    if PROJ_AT.get(t, 4) < 2 and not (final and s >= TT):
                        copy_latent(head_of(i, s) + 1, (s // TT + 1) % 2, PROJ_AT[t])
                    if not (known(i, s) and STEPS * i + s < 2):
                        copy_turned(i, s)
                    act.wait_ge(negmax_ready, STEPS * i + s + 1)
                    if not (known(i, s) and STEPS * i + s < NP_):
                        act.wait_ge(turned, through(i, s, NP_))
                    w = (t + 1) * P
                    nc.scalar.activation(probs[:, s % NP_, 0:w], scores_of(s % 2)[:, 0:w], ACT.Exp,
                                         bias=negmax[:, s % 2:s % 2 + 1]).then_inc(exp_done, 1)

            for c in range(2):
                copy_latent(0, 0, c)
            turn(0)
            with act.Fori(1, TURNS - 1) as i:
                turn(i)
            turn(TURNS - 1, final=True)
            copy_turned(TURNS - 1, STEPS)
            copy_turned(TURNS - 1, STEPS + 1)

        @block.gpsimd
        def _(pool):
            def place(h, slot, first=False):
                if not first:
                    pool.wait_ge(proj_ready, 4 * (h - 1))
                    pool.wait_ge(q_ready, 2 * h - 2)
                elif h == 1:
                    pool.wait_ge(w_placed, 1)
                nc.gpsimd.tensor_copy(wh[:, slot, :], wq[:, bass.ds(h, 1), :].rearrange("r a c -> r (a c)")).then_inc(w_placed, 1)

            def add(h, slot, last=False):
                if last:
                    pool.wait_ge(q_ready, 2 * h)
                else:
                    pool.wait_ge(w_placed, h + 2)
                for half in range(2):
                    if half == 1:
                        pool.wait_ge(q_ready, 2 * h + 1)
                    pool.wait_ge(proj_used, 4 * h + 3 + half)
                    span = slice(half * HALF, (half + 1) * HALF)
                    nc.gpsimd.tensor_tensor(q[KVR:P, slot, span], q[KVR:P, slot, span], swapped[KVR:P, span],
                                            ALU.add).then_inc(q_ready, 1)

            place(0, 0, first=True)
            place(1, 1, first=True)
            add(0, 0)
            with pool.Fori(1, TURNS) as i:
                place(2 * i, 0)
                add(2 * i - 1, 1)
                place(2 * i + 1, 1)
                add(2 * i, 0)
            add(HEADS - 1, 1, last=True)

        @block.vector
        def _(dve):
            def rotate(h, slot, c):
                half = c % 2
                span = slice(half * HALF, (half + 1) * HALF)
                dve.wait_ge(proj_ready, 4 * h + c + 1)
                if c >= 2 and not (isinstance(h, int) and h == 0):
                    dve.wait_ge(q_ready, 2 * h + half - 1)
                out, table = (q[KVR:P, slot, span], cos) if c < 2 else (swapped[KVR:P, span], sin)
                nc.vector.scalar_tensor_tensor(out=out, in0=core.bank[7][KVR:P, :], scalar=LSCALE,
                                               in1=table[KVR:P, span], op0=ALU.mult, op1=ALU.mult).then_inc(proj_used, 1)

            def store(i, s):
                s2 = s - 2
                h, t = 2 * i + s2 // TT, s2 % TT
                n = STEPS * i + s2
                dve.wait_ge(pv_done, through(i, s, 2))
                nc.vector.reciprocal(rden[:, s2 % 2:s2 % 2 + 1], pv[:, KVR:KVR + 1]).then_inc(norm_step, 1)
                dve.wait_ge(norm_step, n + 1)
                nc.vector.tensor_scalar(ctxs[:, t, bass.ds(h * KVR, KVR)], pv[:, 0:KVR], rden[:, s2 % 2:s2 % 2 + 1],
                                        None, ALU.mult).then_inc(ctx_stored, 1)

            def turn(i, final=False):
                for s in range(STEPS):
                    t = s % TT
                    dve.wait_ge(score_ready, STEPS * i + s + 1)
                    if not (known(i, s) and STEPS * i + s < 2):
                        dve.wait_ge(exp_done, STEPS * i + s - 1)
                    nc.vector.tensor_reduce(negmax[:, s % 2:s % 2 + 1], scores_of(s % 2)[:, 0:(t + 1) * P], AX_X, ALU.max,
                                            negate=True).then_inc(negmax_ready, 1)
                    if t in PROJ_AT and not (final and s >= TT):
                        rotate(head_of(i, s) + 1, (s // TT + 1) % 2, PROJ_AT[t])
                    if not (known(i, s) and STEPS * i + s < 2):
                        store(i, s)

            dve.wait_ge(tab_loaded, 32)
            for c in range(4):
                rotate(0, 0, c)
            turn(0)
            with dve.Fori(1, TURNS - 1) as i:
                turn(i)
            turn(TURNS - 1, final=True)
            store(TURNS - 1, STEPS)
            store(TURNS - 1, STEPS + 1)


def latent_out(core, tag, wvo, ctxs):
    nc = core.nc
    turned, copied_act, copied_dve, projected, added = (core.sem(f"{tag}o_{n}") for n in ("tu", "ca", "cd", "pr", "ad"))
    with ExitStack() as ctx:
        ctxT = ctx.enter_context(nc.sbuf_tensor(f"{tag}o_ctxT", [P, LPAIRS, T], F32))
        block = ctx.enter_context(nc.Block())

        @block.tensor
        def _(pe):
            for h in range(2):
                for c in range(LPAIRS):
                    u = LPAIRS * h + c
                    if u >= 4:
                        pe.wait_ge(copied_act if u % 2 == 0 else copied_dve, (u - 4) // 2 + 1)
                    for t in range(4 * h, 4 * h + 4):
                        last = nc.tensor.transpose(core.bank[u % 4][:, (t % 4) * P:(t % 4 + 1) * P],
                                                   ctxs[:, t, c * P:(c + 1) * P], core.ident[:])
                    last.then_inc(turned, 1)
                for t in range(4 * h, 4 * h + 4):
                    pe.wait_ge(copied_act, 4 * h + 4)
                    pe.wait_ge(copied_dve, 4 * h + 4)
                    if t >= 4:
                        pe.wait_ge(added, t - 3)
                    for c in range(LPAIRS):
                        last = nc.tensor.matmul(core.bank[4 + t % 4][:, 0:D], ctxT[:, c, t * P:(t + 1) * P], wvo[:, c, :],
                                                start=(c == 0), stop=(c == LPAIRS - 1))
                    last.then_inc(projected, 1)

        @block.scalar
        def _(act):
            for u in range(0, 2 * LPAIRS, 2):
                act.wait_ge(turned, u + 1)
                h, c = u // LPAIRS, u % LPAIRS
                nc.scalar.copy(ctxT[:, c, h * HALF:(h + 1) * HALF], core.bank[u % 4][:]).then_inc(copied_act, 1)

        @block.vector
        def _(dve):
            for h in range(2):
                for u in range(h * LPAIRS + 1, (h + 1) * LPAIRS, 2):
                    dve.wait_ge(turned, u + 1)
                    nc.vector.tensor_copy(ctxT[:, u % LPAIRS, h * HALF:(h + 1) * HALF], core.bank[u % 4][:]).then_inc(copied_dve, 1)
                for t in range(4 * h, 4 * h + 4):
                    dve.wait_ge(projected, t + 1)
                    nc.vector.tensor_tensor(core.x[:, t, :], core.x[:, t, :], core.bank[4 + t % 4][:, 0:D], ALU.add).then_inc(added, 1)


def program(nc, dram):
    with ExitStack() as ctx:
        core = Core(nc, ctx, dram)
        start(core)
        normalize(core, "n1", core.x, core.xn)
        attention(core, "a", ATT_A)
        normalize(core, "n2", core.x, core.xn)
        moe(core, "e1")
        core.clear_semaphores()
        normalize(core, "n3", core.x, core.xn)
        attention(core, "b", ATT_B)
        normalize(core, "n4", core.x, core.xn)
        moe(core, "e2")
        core.clear_semaphores()
        normalize(core, "n5", core.x, core.xn, turn=False)
        normalize(core, "n5i", core.xn, core.xi, affine=(core.row["L1_attn_a_ln_w"], core.row["L1_attn_a_ln_b"]))
        attention(core, "c", ATT_C)
        normalize(core, "n6", core.x, core.xn)
        ffn(core, "f1")
        core.clear_semaphores()
        normalize(core, "n7", core.x, core.xn)
        latent(core, "l")
        normalize(core, "n8", core.x, core.xn)
        ffn(core, "f2")
        finish(core)


def _constants():
    c = {}
    c["c_ident"] = np.eye(P, dtype=np.float32)
    i, j = np.arange(P)[:, None], np.arange(P)[None, :]
    neg = np.float32(NEG)
    causal = np.where(j <= i, np.float32(0), neg)
    prev = np.where(j > i, np.float32(0), neg)
    prev1 = np.where((j > i) | (j < 4), np.float32(0), neg)
    for n, m in (("causal", causal), ("prev", prev), ("prev1", prev1)):
        c[f"c_{n}"] = np.ascontiguousarray(m.astype(np.float32))
        c[f"c_{n}T"] = np.ascontiguousarray(m.T.astype(np.float32))
    c["c_sinkT"] = np.where(np.broadcast_to(i, (P, P)) < 4, np.float32(0), neg).astype(np.float32)
    t = np.arange(T, dtype=np.float32)

    def angles(n):
        inv = np.float32(1) / np.float32(10000) ** (np.arange(0, n, 2, dtype=np.float32) / np.float32(n))
        a = t[:, None] * inv[None, :].astype(np.float32)
        return np.cos(a).astype(np.float32), np.sin(a).astype(np.float32)

    cos, sin = angles(HD)
    c["c_cos_a"] = np.concatenate([cos, cos], 1)
    c["c_sin_a"] = np.concatenate([-sin, sin], 1)
    cos, sin = angles(HD // 2)
    c["c_cos_c"] = np.concatenate([np.repeat(cos, 2, 1), np.ones((T, HD // 2), np.float32)], 1)
    s = np.repeat(sin, 2, 1)
    s[:, 0::2] *= -1
    c["c_sin_c"] = np.concatenate([s, np.zeros((T, HD // 2), np.float32)], 1)
    cos, sin = angles(DR)
    s = np.repeat(sin, 2, 1)
    s[:, 0::2] *= -1
    c["c_cos_k"] = np.repeat(cos, 2, 1)
    c["c_sin_k"] = s
    c["c_cos_q"] = np.repeat(cos, 2, 1).T
    c["c_sin_q"] = s.T
    return {k: np.ascontiguousarray(v, dtype=np.float32) for k, v in c.items()}


def kernel(**inputs):
    import concourse.bacc as _bacc
    from concourse.bass_utils import run_bass_kernel_spmd as _run

    nc = _bacc.Bacc("TRN2", target_bir_lowering=False, num_devices=1)
    arrays, dram = {}, {}
    for name, a in {**inputs, **_constants()}.items():
        a = np.ascontiguousarray(a)
        arrays[f"in_{name}"] = a
        dram[name] = nc.dram_tensor(f"in_{name}", a.shape, mybir.dt.from_np(a.dtype), kind="ExternalInput").ap()
    dram["out"] = nc.dram_tensor("out_0", (1, T, D), F32, kind="ExternalOutput").ap()
    program(nc, dram)
    r = _run(nc, [arrays], core_ids=[0])
    return r.results[0]["out_0"]
```

```python
from contextlib import ExitStack

import numpy as np

import concourse.bass as bass
from concourse import mybir

ALU = mybir.AluOpType
ACT = mybir.ActivationFunctionType
AX_X = mybir.AxisListType.X
F32 = mybir.dt.float32
BF16 = mybir.dt.bfloat16
F32R = mybir.dt.float32r

P = 128
T = 1024
TT = T // P
D = 256
KC = D // P
HALF = 512
NEG = -1.0e30

HEADS = 16
HD = 16
PAIRS = [(0, 0), (0, 1), (1, 0), (0, 2), (1, 1), (2, 0)]
PARTS = 3
ROWS = HD * len(PAIRS)
KROWS = ROWS + PARTS

EXPERTS = 64
INTER = 96
TOP = 8
GE = 4
GC = GE * INTER // P
GROUPS = EXPERTS // GE

ROUTES = 8

QR, KVR, DN, DR, DV = 96, 64, 128, 64, 128


class Core:

    def __init__(self, nc, ctx, dram):
        self.nc, self.ctx, self.dram = nc, ctx, dram
        self.sems = []
        self.x = self.sb("x", [P, TT, D], F32)
        self.xn = self.sb("xn", [P, TT, D], F32)
        self.xi = self.sb("xi", [P, TT, D], F32)
        self.xT = self.sb("xT", [P, KC, T], F32)
        self.ident = self.sb("ident", [P, P], F32)
        self.ident_h = self.sb("ident_h", [P, P], BF16)
        self.zero_h = self.sb("zero_h", [P, HALF], BF16)
        self.psum = ctx.enter_context(nc.psum_tensor("psum", [P, 8, HALF], F32))
        self.bank = [self.psum[:, i, :] for i in range(8)]

    def sb(self, name, shape, dt):
        return self.ctx.enter_context(self.nc.sbuf_tensor(name, shape, dt))

    def sem(self, name):
        self.sems.append(self.nc.alloc_semaphore(name))
        return self.sems[-1]

    def clear_semaphores(self):
        self.nc.clear_and_free_semaphores(self.sems)
        self.sems = []
        self.nc.all_engine_barrier()


def start(core):
    nc, dram = core.nc, core.dram
    loaded, const_made, turned, stored = (core.sem(f"start_{n}") for n in ("loaded", "const", "turned", "stored"))
    core.mask = {n: core.sb(f"m_{n}", [P, P], F32) for n in ("causal", "causalT", "prev", "prevT", "prev1", "prev1T", "sinkT")}
    core.mask_h = {n: core.sb(f"mh_{n}", [P, P], BF16) for n in core.mask}
    core.wup = core.sb("wup", [P, KC, D], F32)
    core.wdn = core.sb("wdn", [P, KC, D], F32)
    core.wex = core.sb("wex", [P, KC, D], F32)
    core.wrt = core.sb("wrt", [P, KC, ROUTES], F32)
    core.bqkv = core.sb("bqkv", [P, KC, 384], F32)
    core.bwo = core.sb("bwo", [P, KC, D], F32)
    core.row = {n: core.sb(f"row_{n}", [P, w], F32) for n, w in
            (("L1_attn_a_ln_w", D), ("L1_attn_a_ln_b", D), ("L1_attn_b_q_norm_w", QR), ("L1_attn_b_kv_norm_w", KVR))}
    with ExitStack() as ctx:
        raw = []
        plan = [("L1_ffn_W_up", core.wup, 0, D), ("L1_ffn_W_down", core.wdn, 0, D),
                ("L0_attn_b_Wq", core.bqkv, 0, D), ("L0_attn_b_Wk", core.bqkv, 256, 64),
                ("L0_attn_b_Wv", core.bqkv, 320, 64), ("L0_attn_b_Wo", core.bwo, 0, D),
                ("L1_ffn_W_gate", core.wrt, 0, ROUTES)]
        for name, dst, col, rows in plan:
            for r in range(0, rows, P):
                n = min(P, rows - r)
                t = ctx.enter_context(nc.sbuf_tensor(f"raw_{name}_{r}", [P, D], F32))
                raw.append((name, t, dst, col + r, r, n))
        block = ctx.enter_context(nc.Block())
        loads = len(raw) + 3 + len(core.mask) + len(core.row)

        @block.sync
        def _(sp):
            sp.dma_start(core.ident[:], dram["c_ident"]).then_inc(loaded, 16)
            for name, t, _, _, r, n in raw:
                sp.dma_start(t[0:n, :], dram[name][r:r + n, :]).then_inc(loaded, 16)
            for name in core.mask:
                sp.dma_start(core.mask[name][:], dram[f"c_{name}"]).then_inc(loaded, 16)
            for name, row in core.row.items():
                sp.dma_start(row[:], dram[name].unsqueeze(0).broadcast_to(list(row.shape))).then_inc(loaded, 16)
            sp.dma_start(core.wex[:], dram["L1_ffn_W_expert"].rearrange("(k p) n -> p k n", p=P)).then_inc(loaded, 16)
            sp.dma_start(core.x[:], dram["L0_attn_a_x"].rearrange("b (t p) d -> p (b t) d", p=P)).then_inc(loaded, 16)

        @block.gpsimd
        def _(pool):
            pool.memset(core.zero_h[:], 0.0)
            pool.wait_ge(loaded, 16 * loads)
            pool.tensor_copy(core.ident_h[:], core.ident[:])
            for name in core.mask:
                pool.tensor_copy(core.mask_h[name][:], core.mask[name][:])

        @block.tensor
        def _(pe):
            pe.wait_ge(loaded, 16 * loads)
            for i, (_, t, _, _, _, n) in enumerate(raw):
                if i >= 8:
                    pe.wait_ge(stored, i - 7)
                for k in range(KC):
                    last = nc.tensor.transpose(core.bank[i % 8][:, k * P:k * P + n],
                                               t[0:n, k * P:(k + 1) * P], core.ident[0:n, 0:n])
                last.then_inc(turned, 1)

        @block.vector
        def _(dve):
            for i, (_, _, dst, col, _, n) in enumerate(raw):
                dve.wait_ge(turned, i + 1)
                src = core.bank[i % 8][:, 0:KC * P].rearrange("p (k n) -> p k n", k=KC)
                nc.vector.tensor_copy(dst[:, :, col:col + n], src[:, :, 0:n]).then_inc(stored, 1)


def normalize(core, tag, src, dst, eps=1e-5, turn=True, affine=None):
    nc = core.nc
    stats_done, mv_done, var_ready, std_ready, rstd_done, scaled, normed, turned = (
        core.sem(f"{tag}_{n}") for n in ("stats", "mv", "var", "std", "rstd", "scaled", "normed", "turned"))
    with ExitStack() as ctx:
        stats = ctx.enter_context(nc.sbuf_tensor(f"{tag}_stats_b", [P, TT, 6], F32))
        mv = ctx.enter_context(nc.sbuf_tensor(f"{tag}_mv_b", [P, TT, 2], F32))
        var, std, rstd = (ctx.enter_context(nc.sbuf_tensor(f"{tag}_{n}_b", [P, TT], F32)) for n in ("var", "std", "rstd"))
        block = ctx.enter_context(nc.Block())

        @block.vector
        def _(dve):
            for t in range(TT):
                nc.vector.bn_stats(stats[:, t, :], src[:, t, :]).then_inc(stats_done, 1)
            for t in range(TT):
                dve.wait_ge(stats_done, t + 1)
                nc.vector.bn_aggr(mv[:, t, :], stats[:, t, :]).then_inc(mv_done, 1)
            dve.wait_ge(mv_done, TT)
            nc.vector.tensor_scalar(var[:], mv[:, :, 1], eps, None, ALU.add).then_inc(var_ready, 1)
            dve.wait_ge(std_ready, 1)
            nc.vector.reciprocal(rstd[:], std[:]).then_inc(rstd_done, 1)
            dve.wait_ge(rstd_done, 1)
            n_scaled = 0
            for t in range(TT):
                last = nc.vector.tensor_scalar(dst[:, t, :], src[:, t, :], mv[:, t, 0:1], rstd[:, t:t + 1],
                                               ALU.subtract, ALU.mult)
                if affine is not None:
                    for row, op in zip(affine, (ALU.mult, ALU.add)):
                        last.then_inc(scaled, 1)
                        n_scaled += 1
                        dve.wait_ge(scaled, n_scaled)
                        last = nc.vector.tensor_tensor(dst[:, t, :], dst[:, t, :], row[:], op)
                last.then_inc(normed, 1)
            if turn:
                for h in range(2):
                    dve.wait_ge(turned, 4 * h + 4)
                    nc.vector.tensor_copy(core.xT[:, 1, h * HALF:(h + 1) * HALF], core.bank[2 * h + 1][:])

        @block.scalar
        def _(act):
            act.wait_ge(var_ready, 1)
            nc.scalar.activation(std[:], var[:], ACT.Sqrt).then_inc(std_ready, 1)
            if turn:
                for h in range(2):
                    act.wait_ge(turned, 4 * h + 4)
                    nc.scalar.copy(core.xT[:, 0, h * HALF:(h + 1) * HALF], core.bank[2 * h][:])

        if turn:
            @block.tensor
            def _(pe):
                for t in range(TT):
                    pe.wait_ge(normed, t + 1)
                    for k in range(KC):
                        last = nc.tensor.transpose(core.bank[2 * (t // 4) + k][:, (t % 4) * P:(t % 4 + 1) * P],
                                                   dst[:, t, k * P:(k + 1) * P], core.ident[:])
                    last.then_inc(turned, 1)


def ffn(core, tag):
    nc = core.nc
    up_ready, up_stored, out_ready, logits_ready, sorted_, diff, exped, step, added = (
        core.sem(f"{tag}_{n}") for n in ("up", "ups", "out", "lg", "sort", "diff", "exp", "step", "added"))
    with ExitStack() as ctx:
        hT = ctx.enter_context(nc.sbuf_tensor(f"{tag}_hT", [P, KC, T], F32))
        top = ctx.enter_context(nc.sbuf_tensor(f"{tag}_top", [P, TT, ROUTES], F32))
        d21 = ctx.enter_context(nc.sbuf_tensor(f"{tag}_d21", [P, TT], F32))
        e21 = ctx.enter_context(nc.sbuf_tensor(f"{tag}_e21", [P, TT], F32))
        den = ctx.enter_context(nc.sbuf_tensor(f"{tag}_den", [P, TT], F32))
        w1 = ctx.enter_context(nc.sbuf_tensor(f"{tag}_w1", [P, TT], F32))
        w2 = ctx.enter_context(nc.sbuf_tensor(f"{tag}_w2", [P, TT], F32))
        wsum = ctx.enter_context(nc.sbuf_tensor(f"{tag}_wsum", [P, TT], F32))
        block = ctx.enter_context(nc.Block())
        lg = core.bank[7]

        @block.tensor
        def _(pe):
            for t in range(TT):
                for k in range(KC):
                    last = nc.tensor.matmul(lg[:, t * ROUTES:(t + 1) * ROUTES], core.xT[:, k, t * P:(t + 1) * P],
                                            core.wrt[:, k, :], start=(k == 0), stop=(k == KC - 1))
            last.then_inc(logits_ready, 1)
            for u in range(4):
                m, h = u % 2, u // 2
                for k in range(KC):
                    last = nc.tensor.matmul(core.bank[u][:], core.wup[:, k, m * P:(m + 1) * P],
                                            core.xT[:, k, h * HALF:(h + 1) * HALF], start=(k == 0), stop=(k == KC - 1))
                last.then_inc(up_ready, 1)
            for t in range(TT):
                pe.wait_ge(up_stored, 2 * (t // 4) + 2)
                b = 4 + t % 3
                if t >= 3:
                    pe.wait_ge(added, t - 2)
                for k in range(KC):
                    nc.tensor.matmul(core.bank[b][:, 0:D], hT[:, k, t * P:(t + 1) * P], core.wdn[:, k, :],
                                     start=(k == 0), stop=(k == KC - 1))
                for k in range(KC):
                    last = nc.tensor.matmul(core.bank[b][:, D:2 * D], core.xT[:, k, t * P:(t + 1) * P],
                                            core.wex[:, k, :], start=(k == 0), stop=(k == KC - 1))
                last.then_inc(out_ready, 1)

        @block.scalar
        def _(act):
            act.wait_ge(diff, 1)
            nc.scalar.activation(e21[:], d21[:], ACT.Exp).then_inc(exped, 1)
            for u in range(4):
                m, h = u % 2, u // 2
                act.wait_ge(up_ready, u + 1)
                nc.scalar.activation(hT[:, m, h * HALF:(h + 1) * HALF], core.bank[u][:], ACT.Relu).then_inc(up_stored, 1)

        @block.vector
        def _(dve):
            dve.wait_ge(logits_ready, 1)
            for t in range(TT):
                nc.vector.max(top[:, t, :], lg[:, t * ROUTES:(t + 1) * ROUTES]).then_inc(sorted_, 1)
            dve.wait_ge(sorted_, TT)
            nc.vector.tensor_tensor(d21[:], top[:, :, 1], top[:, :, 0], ALU.subtract).then_inc(diff, 1)
            dve.wait_ge(exped, 1)
            nc.vector.tensor_scalar(den[:], e21[:], 1.0, None, ALU.add).then_inc(step, 1)
            dve.wait_ge(step, 1)
            nc.vector.reciprocal(w1[:], den[:]).then_inc(step, 1)
            dve.wait_ge(step, 2)
            nc.vector.tensor_tensor(w2[:], e21[:], w1[:], ALU.mult).then_inc(step, 1)
            dve.wait_ge(step, 3)
            nc.vector.tensor_tensor(wsum[:], w1[:], w2[:], ALU.add).then_inc(step, 1)
            dve.wait_ge(step, 4)
            for t in range(TT):
                b = 4 + t % 3
                dve.wait_ge(out_ready, t + 1)
                nc.vector.tensor_tensor(core.x[:, t, :], core.x[:, t, :], core.bank[b][:, 0:D], ALU.add).then_inc(step, 1)
                dve.wait_ge(step, 5 + t)
                nc.vector.scalar_tensor_tensor(out=core.x[:, t, :], in0=core.bank[b][:, D:2 * D],
                                               scalar=wsum[:, t:t + 1], in1=core.x[:, t, :],
                                               op0=ALU.mult, op1=ALU.add).then_inc(added, 1)


def finish(core):
    nc = core.nc
    out_stored = core.sem("out_stored")
    with nc.Block() as block:
        @block.sync
        def _(sp):
            sp.dma_start(core.dram["out"].rearrange("b (t p) d -> p (b t) d", p=P), core.x[:]).then_inc(out_stored, 16)
            sp.wait_ge(out_stored, 16)


def moe(core, tag):
    with ExitStack() as ctx:
        parts = ExpertParts(core, ctx, tag)
        routing_weights(core, tag, parts)
        experts(core, tag, parts)


class ExpertParts:
    PIECES = 6
    COLS = GE * INTER
    LOADS = 2 * KC + 1

    def __init__(self, core, ctx, tag):
        nc, self.dram = core.nc, core.dram
        self.loaded = [core.sem(f"{tag}_wld{n}") for n in range(self.LOADS)]
        self.high_made, self.low_made = core.sem(f"{tag}_whi"), core.sem(f"{tag}_wlo")
        self.x_high_made, self.x_low_made = core.sem(f"{tag}_xhi"), core.sem(f"{tag}_xlo")

        def sb(name, shape, dt=F32R):
            return ctx.enter_context(nc.sbuf_tensor(f"{tag}_{name}", shape, dt))

        self.raw = sb("w_raw", [P, self.PIECES, self.COLS], F32)
        self.w = [sb("w_hi", [P, 2, self.PIECES, self.COLS]), sb("w_lo", [P, 2, self.PIECES, self.COLS])]
        self.x = [sb("x_hi", [P, KC, T]), sb("x_lo", [P, KC, T])]

    def up_or_gate(self, part, s, which, k, j):
        return self.w[part][:, s, KC * which + k, j * P:(j + 1) * P]

    def down(self, part, s, j, m):
        flat = self.w[part][:, s, 2 * KC:, :].rearrange("p a c -> p (a c)")
        return flat[:, j * D + m * P:j * D + (m + 1) * P]

    def load(self, sp, g, n):
        if n < 2 * KC:
            name, k = ("L0_ffn_w_gate", "L0_ffn_w_up")[n // KC], n % KC
            src = self.dram[name].rearrange("e (k p) i -> k p e i", p=P)[k]
            sp.dma_start(self.raw[:, n, :].rearrange("p (e i) -> p e i", e=GE),
                         src[:, bass.ds(g * GE, GE), :]).then_inc(self.loaded[n], 16)
        else:
            src = self.dram["L0_ffn_w_down"].rearrange("e i n -> (e i) n").rearrange("(j p) n -> p j n", p=P)
            dst = self.raw[:, 2 * KC:, :].rearrange("p a c -> p (a c)").rearrange("p (j n) -> p j n", n=D)
            sp.dma_start(dst, src[:, bass.ds(g * GC, GC), :]).then_inc(self.loaded[n], 16)


def routing_weights(core, tag, parts):
    nc = core.nc
    logits_ready, copied, max_ready, exped, recip_ready, probs_ready, top_ready, replaced = (
        core.sem(f"{tag}_{n}") for n in ("lg", "lgc", "max", "exp", "rec", "prob", "top", "repl"))
    sum_ready, scale_ready, kept, weighted, gate_loaded, turned, rows_copied, rows_stored = (
        core.sem(f"{tag}_{n}") for n in ("sum", "scale", "kept", "wtd", "gate", "turned", "rows", "rst"))
    core.rw_dram = nc.dram_tensor(f"{tag}_rw_dram", (EXPERTS, T), F32, kind="Internal").ap()
    with ExitStack() as ctx:
        def sb(name, shape):
            return ctx.enter_context(nc.sbuf_tensor(f"{tag}_{name}", shape, F32))

        wr = sb("wr", [P, KC, EXPERTS])
        lg = sb("lg_b", [P, TT, EXPERTS])
        probs = sb("probs", [P, TT, EXPERTS])
        repl = sb("repl_b", [P, TT, EXPERTS])
        top = sb("top_b", [P, TT, TOP])
        big, total, rtotal, tsum, rtsum = (sb(n, [P, TT]) for n in ("big", "total", "rtotal", "tsum", "rtsum"))
        rwT = sb("rwT", [EXPERTS, T])
        block = ctx.enter_context(nc.Block())

        @block.sync
        def _(sp):
            sp.dma_start(wr[:], core.dram["L0_ffn_gate_w"].rearrange("(k p) e -> p k e", p=P)).then_inc(gate_loaded, 16)
            for g in range(2):
                for n in range(parts.LOADS):
                    if g == 1:
                        sp.wait_ge(parts.low_made, n + 1 if n < 2 * KC else parts.PIECES)
                    parts.load(sp, g, n)
            sp.wait_ge(rows_copied, 2)
            sp.dma_start(core.rw_dram, rwT[:]).then_inc(rows_stored, 16)
            sp.wait_ge(rows_stored, 16)

        @block.tensor
        def _(pe):
            pe.wait_ge(gate_loaded, 16)
            for t in range(TT):
                for k in range(KC):
                    last = nc.tensor.matmul(core.bank[0][:, t * EXPERTS:(t + 1) * EXPERTS],
                                            core.xT[:, k, t * P:(t + 1) * P], wr[:, k, :],
                                            start=(k == 0), stop=(k == KC - 1))
            last.then_inc(logits_ready, 1)
            pe.wait_ge(weighted, 1)
            for t in range(TT):
                last = nc.tensor.transpose(core.bank[1 + t // 4][0:EXPERTS, (t % 4) * P:(t % 4 + 1) * P],
                                           probs[:, t, :], core.ident[:])
            last.then_inc(turned, 1)

        @block.scalar
        def _(act):
            for k in range(KC):
                nc.scalar.copy(parts.x[0][:, k, :], core.xT[:, k, :]).then_inc(parts.x_high_made, 1)
            act.wait_ge(max_ready, 1)
            nc.scalar.activation(lg[:], lg[:], ACT.Exp).then_inc(exped, 1)
            for p in range(parts.PIECES):
                act.wait_ge(parts.loaded[min(p, 2 * KC)], 16)
                nc.scalar.copy(parts.w[0][:, 0, p, :], parts.raw[:, p, :]).then_inc(parts.high_made, 1)
            act.wait_ge(turned, 1)
            nc.scalar.copy(rwT[:, 0:HALF], core.bank[1][0:EXPERTS, :]).then_inc(rows_copied, 1)

        @block.gpsimd
        def _(pool):
            for k in range(KC):
                pool.wait_ge(parts.x_high_made, k + 1)
                nc.gpsimd.tensor_tensor(parts.x[1][:, k, :], core.xT[:, k, :], parts.x[0][:, k, :],
                                        ALU.subtract).then_inc(parts.x_low_made, 1)
                pool.wait_ge(parts.x_low_made, k + 1)
            for p in range(parts.PIECES):
                pool.wait_ge(parts.high_made, p + 1)
                nc.gpsimd.tensor_tensor(parts.w[1][:, 0, p, :], parts.raw[:, p, :], parts.w[0][:, 0, p, :],
                                        ALU.subtract).then_inc(parts.low_made, 1)
                pool.wait_ge(parts.low_made, p + 1)

        @block.vector
        def _(dve):
            def rows(v):
                return v[:].unsqueeze(2).broadcast_to([P, TT, EXPERTS])

            dve.wait_ge(logits_ready, 1)
            raw = core.bank[0][:].rearrange("p (t e) -> p t e", e=EXPERTS)
            nc.vector.tensor_reduce(big[:], raw, AX_X, ALU.max).then_inc(copied, 1)
            dve.wait_ge(copied, 1)
            nc.vector.tensor_tensor(lg[:], raw, rows(big), ALU.subtract).then_inc(max_ready, 1)
            dve.wait_ge(exped, 1)
            nc.vector.tensor_reduce(total[:], lg[:], AX_X, ALU.add).then_inc(recip_ready, 1)
            dve.wait_ge(recip_ready, 1)
            nc.vector.reciprocal(rtotal[:], total[:]).then_inc(recip_ready, 1)
            dve.wait_ge(recip_ready, 2)
            nc.vector.tensor_tensor(probs[:], lg[:], rows(rtotal), ALU.mult).then_inc(probs_ready, 1)
            dve.wait_ge(probs_ready, 1)
            for t in range(TT):
                nc.vector.max(top[:, t, :], probs[:, t, :]).then_inc(top_ready, 1)
            for t in range(TT):
                dve.wait_ge(top_ready, t + 1)
                nc.vector.match_replace(repl[:, t, :], top[:, t, :], probs[:, t, :], -1.0).then_inc(replaced, 1)
            nc.vector.tensor_reduce(tsum[:], top[:], AX_X, ALU.add).then_inc(sum_ready, 1)
            dve.wait_ge(sum_ready, 1)
            nc.vector.reciprocal(rtsum[:], tsum[:]).then_inc(scale_ready, 1)
            dve.wait_ge(replaced, TT)
            nc.vector.tensor_scalar(repl[:], repl[:], 0.0, None, ALU.max).then_inc(kept, 1)
            dve.wait_ge(kept, 1)
            nc.vector.tensor_tensor(probs[:], probs[:], repl[:], ALU.subtract).then_inc(kept, 1)
            dve.wait_ge(kept, 2)
            dve.wait_ge(scale_ready, 1)
            nc.vector.tensor_tensor(probs[:], probs[:], rows(rtsum), ALU.mult).then_inc(weighted, 1)
            dve.wait_ge(turned, 1)
            nc.vector.tensor_copy(rwT[:, HALF:T], core.bank[2][0:EXPERTS, :]).then_inc(rows_copied, 1)


def experts(core, tag, parts):
    nc = core.nc
    UNITS = 2 * GC
    assert UNITS == parts.PIECES
    BODY = 2 * UNITS
    TURNS = GROUPS // 2
    LAG = 2
    PASSES = [(0, 0), (0, 1), (1, 0)]
    r_loaded = [core.sem(f"{tag}_rld{s}") for s in range(2)]
    gu_ready, silu_done, weighted, inner_ready, high_made, low_made, down_done, summed, sum_copied, turned, added = (
        core.sem(f"{tag}_{n}") for n in ("gu", "silu", "w2", "inner", "hi", "lo", "down", "summed", "scp", "st", "sadd"))
    spans = []
    for j in range(GC):
        for e in range(GE):
            a, b = max(j * P, e * INTER), min((j + 1) * P, (e + 1) * INTER)
            if a < b:
                spans.append((j, e, a - j * P, b - j * P))
    with ExitStack() as ctx:
        def sb(name, shape, dt=F32):
            return ctx.enter_context(nc.sbuf_tensor(f"{tag}_{name}", shape, dt))

        rw = sb("rw", [P, 2, GC, T])
        silu, wsilu, inner = (sb(n, [P, 2, HALF]) for n in ("silu_b", "wsilu", "inner_b"))
        inner_parts = [sb("inner_hi", [P, 3, HALF], F32R), sb("inner_lo", [P, 3, HALF], F32R)]
        oT = sb("oT", [P, KC, T])
        block = ctx.enter_context(nc.Block())
        gbank, ubank, obank = core.bank[0:2], core.bank[2:4], core.bank[4:8]

        def unit(i, u):
            return BODY * i + u

        def early(i, u, n):
            return isinstance(i, int) and unit(i, u) < n

        @block.sync
        def _(sp):
            def load_rows(g, s):
                for j, e, a, b in spans:
                    sp.dma_start(rw[a:b, s, j, :],
                                 core.rw_dram[bass.ds(g * GE + e, 1), :].broadcast_to([b - a, T])).then_inc(r_loaded[s], 16)

            def load_weights(g):
                for n in range(parts.LOADS):
                    sp.wait_ge(parts.low_made, UNITS * (g - 1) + (n + 1 if n < 2 * KC else UNITS))
                    parts.load(sp, g, n)

            for s in range(2):
                load_rows(s, s)
            with sp.Fori(1, TURNS) as i:
                for s in range(2):
                    load_weights(2 * i + s)
                    sp.wait_ge(weighted, BODY * i + UNITS * (s - 1))
                    load_rows(2 * i + s, s)

        @block.tensor
        def _(pe):
            def gate_up(i, u):
                s, j, h = u // UNITS, u % UNITS // 2, u % 2
                if h == 0 and j == 0:
                    pe.wait_ge(parts.low_made, unit(i, u) + 2 * KC)
                    pe.wait_ge(parts.high_made, unit(i, u) + 2 * KC)
                if not early(i, u, 2):
                    pe.wait_ge(inner_ready, unit(i, u) - 1)
                for which, bank in ((0, gbank), (1, ubank)):
                    steps = [(k, a, b) for k in range(KC) for a, b in PASSES]
                    for n, (k, a, b) in enumerate(steps):
                        last = nc.tensor.matmul(bank[u % 2][:], parts.up_or_gate(a, s, which, k, j),
                                                parts.x[b][:, k, h * HALF:(h + 1) * HALF],
                                                start=(n == 0), stop=(n == len(steps) - 1))
                last.then_inc(gu_ready, 1)

            def down(i, u):
                s, j, h = u // UNITS % 2, u % UNITS // 2, u % 2
                if h == 0 and j == 0:
                    pe.wait_ge(parts.low_made, unit(i, u) + UNITS)
                    pe.wait_ge(parts.high_made, unit(i, u) + UNITS)
                pe.wait_ge(low_made, unit(i, u) + 1)
                pe.wait_ge(high_made, unit(i, u) + 1)
                for m in range(KC):
                    for a, b in PASSES:
                        last = nc.tensor.matmul(obank[2 * h + m][:], parts.down(a, s, j, m), inner_parts[b][:, u % 3, :],
                                                start=False, stop=False, skip_group_check=True)
                last.then_inc(down_done, 1)

            def turn(i):
                for u in range(BODY):
                    gate_up(i, u)
                    if not early(i, u, LAG):
                        down(i, u - LAG)

            for b in range(4):
                nc.tensor.matmul(obank[b][:], core.zero_h[:, 0:P], core.zero_h[:], start=True, stop=False,
                                 skip_group_check=True)
            turn(0)
            with pe.Fori(1, TURNS) as i:
                turn(i)
            for u in range(BODY - LAG, BODY):
                down(TURNS - 1, u)
            for b in range(4):
                last = nc.tensor.matmul(obank[b][:], core.zero_h[:, 0:P], core.zero_h[:], start=False, stop=True,
                                        skip_group_check=True)
            last.then_inc(summed, 1)
            for t in range(TT):
                pe.wait_ge(sum_copied, 2 * (t // 4) + 2)
                if t >= 4:
                    pe.wait_ge(added, t - 3)
                for m in range(KC):
                    last = nc.tensor.transpose(core.bank[t % 4][:, m * P:(m + 1) * P], oT[:, m, t * P:(t + 1) * P],
                                               core.ident[:])
                last.then_inc(turned, 1)

        @block.scalar
        def _(act):
            def high_weights(i, u):
                s, p = u // UNITS, u % UNITS
                act.wait_ge(parts.loaded[min(p, 2 * KC)], 16 * (2 * i + s + 2))
                if p == 0:
                    if not early(i, u, UNITS):
                        act.wait_ge(down_done, unit(i, u))
                nc.scalar.copy(parts.w[0][:, 1 - s, p, :], parts.raw[:, p, :]).then_inc(parts.high_made, 1)

            def high_inner(i, u):
                act.wait_ge(inner_ready, unit(i, u) + 1)
                if not early(i, u, 3):
                    act.wait_ge(down_done, unit(i, u) - 2)
                nc.scalar.copy(inner_parts[0][:, u % 3, :], inner[:, u % 2, :]).then_inc(high_made, 1)

            def turn(i, final=False):
                for u in range(BODY):
                    act.wait_ge(gu_ready, unit(i, u) + 1)
                    if not early(i, u, 2):
                        act.wait_ge(weighted, unit(i, u) - 1)
                    nc.scalar.activation(silu[:, u % 2, :], gbank[u % 2][:], ACT.Silu).then_inc(silu_done, 1)
                    if not early(i, u, 1):
                        high_inner(i, u - 1)
                    if not (final and u >= UNITS):
                        high_weights(i, u)

            turn(0)
            with act.Fori(1, TURNS - 1) as i:
                turn(i)
            turn(TURNS - 1, final=True)
            high_inner(TURNS - 1, BODY - 1)
            act.wait_ge(summed, 1)
            for b in range(4):
                h, m = b // 2, b % 2
                nc.scalar.copy(oT[:, m, h * HALF:(h + 1) * HALF], obank[b][:]).then_inc(sum_copied, 1)

        @block.gpsimd
        def _(pool):
            def turn(i, final=False):
                for u in range(BODY):
                    s, j, h = u // UNITS, u % UNITS // 2, u % 2
                    if h == 0 and j == 0:
                        pool.wait_ge(r_loaded[s], 16 * len(spans) * (i + 1))
                    pool.wait_ge(silu_done, unit(i, u) + 1)
                    if not early(i, u, 2):
                        pool.wait_ge(inner_ready, unit(i, u) - 1)
                    nc.gpsimd.tensor_tensor(wsilu[:, u % 2, :], silu[:, u % 2, :],
                                            rw[:, s, j, h * HALF:(h + 1) * HALF], ALU.mult).then_inc(weighted, 1)
                    if final and u >= UNITS:
                        continue
                    p = u % UNITS
                    pool.wait_ge(weighted, unit(i, u) + 1)
                    pool.wait_ge(parts.high_made, unit(i, u) + UNITS + 1)
                    nc.gpsimd.tensor_tensor(parts.w[1][:, 1 - s, p, :], parts.raw[:, p, :], parts.w[0][:, 1 - s, p, :],
                                            ALU.subtract).then_inc(parts.low_made, 1)

            turn(0)
            with pool.Fori(1, TURNS - 1) as i:
                turn(i)
            turn(TURNS - 1, final=True)

        @block.vector
        def _(dve):
            def low_inner(i, u):
                dve.wait_ge(high_made, unit(i, u) + 1)
                nc.vector.tensor_tensor(inner_parts[1][:, u % 3, :], inner[:, u % 2, :], inner_parts[0][:, u % 3, :],
                                        ALU.subtract).then_inc(low_made, 1)

            def turn(i):
                for u in range(BODY):
                    if not early(i, u, 1):
                        low_inner(i, u - 1)
                    dve.wait_ge(weighted, unit(i, u) + 1)
                    if not early(i, u, 2):
                        dve.wait_ge(high_made, unit(i, u) - 1)
                        dve.wait_ge(low_made, unit(i, u) - 1)
                    nc.vector.tensor_tensor(inner[:, u % 2, :], ubank[u % 2][:], wsilu[:, u % 2, :],
                                            ALU.mult).then_inc(inner_ready, 1)

            turn(0)
            with dve.Fori(1, TURNS) as i:
                turn(i)
            low_inner(TURNS - 1, BODY - 1)
            for t in range(TT):
                dve.wait_ge(turned, t + 1)
                nc.vector.tensor_tensor(core.x[:, t, :], core.x[:, t, :], core.bank[t % 4][:, 0:D], ALU.add).then_inc(added, 1)


class Attention:

    def __init__(self, kv_heads, rotation, maxima, halves):
        self.kv_heads, self.rotation, self.maxima = kv_heads, rotation, maxima
        self.units = [u for half in halves for u in half]
        self.quads = []
        at = 0
        for h, half in enumerate(halves):
            for i in range(0, len(half), 4):
                n = min(4, len(half) - i)
                self.quads.append((h, list(range(at, at + n)), i == 0, i + n == len(half)))
                at += n
        self.qk_heads = HEADS + kv_heads
        self.width = (HEADS + 2 * kv_heads) * HD
        self.k_chunks = -(-kv_heads * HD // P)
        self.chunks = HEADS * HD // P + self.k_chunks


def _blocks_seen():
    maxima = [[(k, min(HALF, (t + 1) * P - k), None) for k in range(0, (t + 1) * P, HALF)] for t in range(TT)]
    units = [[(s, max(q, s), q + HALF - max(q, s), []) for s in range(0, q + HALF, P)] for q in (0, HALF)]
    return maxima, units


def _window_seen(sink=4):
    maxima = [[(0, P, "causal")], [(0, P, "prev1"), (P, P, "causal")]]
    maxima += [[(0, sink, None), ((t - 1) * P, P, "prev"), (t * P, P, "causal")] for t in range(2, TT)]
    units = []
    for q in (0, HALF):
        these = []
        for s in range(max(0, q - P), q + HALF, P):
            seen = [(x, m) for x, m in ((s, "causalT"), (s + P, "prev1T" if s == 0 else "prevT")) if q <= x < q + HALF]
            these.append((s, seen[0][0], P * len(seen), [(x - seen[0][0], m) for x, m in seen]))
        q0 = max(q, 2 * P)
        these.append((0, q0, q + HALF - q0, [(c, "sinkT") for c in range(0, q + HALF - q0, P)]))
        units.append(these)
    return maxima, units


def _all_seen():
    maxima = [[(0, HALF, None), (HALF, HALF, None)] for _ in range(TT)]
    units = [[(s * P, q, HALF, []) for s in range(TT)] for q in (0, HALF)]
    return maxima, units


ATT_A = Attention(4, "halves", *_blocks_seen())
ATT_B = Attention(4, None, *_window_seen())
ATT_C = Attention(16, "pairs", *_all_seen())


def attention(core, tag, cfg):
    with ExitStack() as ctx:
        def sb(name, shape, dt):
            return ctx.enter_context(core.nc.sbuf_tensor(f"{tag}_{name}", shape, dt))

        v = sb("v", [P, TT, cfg.kv_heads, HD + 1], F32)
        qs = sb("qs", [KROWS, HEADS, T], BF16)
        ks = sb("ks", [KROWS, cfg.kv_heads, T], BF16)
        project_and_stack(core, tag, cfg, v, qs, ks)
        ctxs = sb("ctxs", [P, TT, HEADS * HD], F32)
        attend(core, tag, cfg, v, qs, ks, ctxs)
        project_out(core, tag, ctxs, extra=core.xn if tag == "c" else None)


def project_and_stack(core, tag, cfg, v, qs, ks):
    nc, dram = core.nc, core.dram
    NQK = cfg.qk_heads * HD
    w_loaded, projected, copied, v_copied, rot, roped, turned = (
        core.sem(f"{tag}_{n}") for n in ("wl", "proj", "cp", "vcp", "rot", "roped", "tqk"))
    ones_made, part1, rest1, part2, part3, parts_stored, stacked = (
        core.sem(f"{tag}_{n}") for n in ("ones", "p1", "r1", "p2", "p3", "pst", "stk"))
    C = cfg.chunks
    parts_dram = nc.dram_tensor(f"{tag}_parts_dram", (PARTS, C, P, T), BF16, kind="Internal").ap()
    rows_of = [P if (j + 1) * P <= NQK else NQK - j * P for j in range(C)]
    rope = cfg.rotation is not None
    if not rope:
        roped = copied
    with ExitStack() as ctx:
        def sb(name, shape, dt=F32):
            return ctx.enter_context(nc.sbuf_tensor(f"{tag}_{name}", shape, dt))

        qk = sb("qk", [P, TT, cfg.qk_heads, HD])
        part = sb("part", [P, PARTS, C, T], BF16)
        rest = sb("rest", [P, 2, HALF])
        if tag == "b":
            w, loads = core.bqkv, []
        else:
            w = sb("wqkv", [P, KC, cfg.width])
            if tag == "a":
                loads = [(w[:, :, 0:256], "L0_attn_a_Wq"), (w[:, :, 256:320], "L0_attn_a_Wk"), (w[:, :, 320:384], "L0_attn_a_Wv")]
            else:
                loads = [(w[:], "L1_attn_a_W_in")]
        if rope:
            cos, sin = sb("cos", [P, TT, HD]), sb("sin", [P, TT, HD])
            turned_qk = sb("turned_qk", [P, 2, cfg.qk_heads, HD])
        n_loads = len(loads) + 2 * rope
        block = ctx.enter_context(nc.Block())

        @block.sync
        def _(sp):
            for dst, name in loads:
                sp.dma_start(dst, dram[name].rearrange("(k p) n -> p k n", p=P)).then_inc(w_loaded, 16)
            if rope:
                for dst, name in ((cos, f"c_cos_{tag}"), (sin, f"c_sin_{tag}")):
                    sp.dma_start(dst[:], dram[name].rearrange("(t p) d -> p t d", p=P)).then_inc(w_loaded, 16)
            for n in range(2 * C):
                h, j = n // C, n % C
                sp.wait_ge(part3, n + 1)
                sp.wait_ge(part2, n + 1)
                sp.wait_ge(part1, n + 1)
                sp.dma_start(parts_dram[:, j, 0:rows_of[j], h * HALF:(h + 1) * HALF].rearrange("a p t -> p a t"),
                             part[0:rows_of[j], :, j, h * HALF:(h + 1) * HALF]).then_inc(parts_stored, 16)
            sp.wait_ge(parts_stored, 16 * 2 * C)
            n_stacks = 0
            for c in range(HEADS * HD // P):
                for g, (pq, pk) in enumerate(PAIRS):
                    todo = [(qs, pq, c)]
                    if c < cfg.k_chunks:
                        todo.append((ks, pk, HEADS * HD // P + c))
                    for dst, which, j in todo:
                        heads = rows_of[j] // HD
                        h0 = 8 * c
                        sp.dma_start(dst[g * HD:(g + 1) * HD, h0:h0 + heads, :],
                                     parts_dram[which, j, 0:rows_of[j], :].rearrange("(h d) t -> d h t", d=HD)
                                     ).then_inc(stacked, 16)
                        n_stacks += 1
            sp.wait_ge(stacked, 16 * n_stacks)

        @block.tensor
        def _(pe):
            if n_loads:
                pe.wait_ge(w_loaded, 16 * n_loads)
            for t in range(TT):
                if t >= 2:
                    pe.wait_ge(copied, t - 1)
                    pe.wait_ge(v_copied, t - 1)
                for n0, b in ([(0, 0)] if cfg.width <= HALF else [(0, 0), (HALF, 1)]):
                    n = min(HALF, cfg.width - n0)
                    for k in range(KC):
                        last = nc.tensor.matmul(core.bank[2 * (t % 2) + b][:, 0:n], core.xT[:, k, t * P:(t + 1) * P],
                                                w[:, k, n0:n0 + n], start=(k == 0), stop=(k == KC - 1))
                last.then_inc(projected, 1)
            for n in range(2 * C):
                h, j = n // C, n % C
                pe.wait_ge(roped, 4 * h + 4)
                if n >= 4:
                    pe.wait_ge(rest1, n - 3)
                for t in range(4 * h, 4 * h + 4):
                    flat = qk[:, t, :, :].rearrange("p h d -> p (h d)")
                    last = nc.tensor.transpose(core.bank[4 + n % 4][0:rows_of[j], (t % 4) * P:(t % 4 + 1) * P],
                                               flat[:, j * P:j * P + rows_of[j]], core.ident[:])
                last.then_inc(turned, 1)

        @block.scalar
        def _(act):
            for t in range(TT):
                act.wait_ge(projected, t + 1)
                nc.scalar.copy(qk[:, t, :, :].rearrange("p h d -> p (h d)"),
                               core.bank[2 * (t % 2)][:, 0:NQK]).then_inc(copied, 1)
            for n in range(2 * C):
                h, j = n // C, n % C
                act.wait_ge(turned, n + 1)
                nc.scalar.copy(part[0:rows_of[j], 0, j, h * HALF:(h + 1) * HALF],
                               core.bank[4 + n % 4][0:rows_of[j], :]).then_inc(part1, 1)

        @block.vector
        def _(dve):
            for t in range(TT):
                dve.wait_ge(projected, t + 1)
                dve.wait_ge(copied, t + 1)
                b, c0 = (2 * (t % 2), NQK) if cfg.width <= HALF else (2 * (t % 2) + 1, 0)
                nc.vector.tensor_copy(v[:, t, :, 0:HD],
                                      core.bank[b][:, c0:c0 + cfg.kv_heads * HD].rearrange("p (h d) -> p h d", d=HD)
                                      ).then_inc(v_copied, 1)
                if not rope:
                    continue
                tq = turned_qk[:, t % 2, :, :]

                def over_heads(table, a, step, n):
                    return table[:, t, a:a + step * (n - 1) + 1:step].unsqueeze(1).broadcast_to([P, cfg.qk_heads, n])

                if cfg.rotation == "halves":
                    moves, step, n_rot = [(0, HD // 2), (HD // 2, 0)], 1, HD // 2
                else:
                    moves, step, n_rot = [(0, 1), (1, 0)], 2, HD // 4
                for to, frm in moves:
                    e = step * (n_rot - 1) + 1
                    nc.vector.tensor_tensor(tq[:, :, to:to + e:step], qk[:, t, :, frm:frm + e:step],
                                            over_heads(sin, to, step, n_rot), ALU.mult).then_inc(rot, 1)
                dve.wait_ge(rot, 3 * t + 2)
                nc.vector.tensor_tensor(qk[:, t, :, :], qk[:, t, :, :], over_heads(cos, 0, 1, HD), ALU.mult).then_inc(rot, 1)
                dve.wait_ge(rot, 3 * t + 3)
                rotated = HD if cfg.rotation == "halves" else HD // 2
                nc.vector.tensor_tensor(qk[:, t, :, 0:rotated], qk[:, t, :, 0:rotated], tq[:, :, 0:rotated],
                                        ALU.add).then_inc(roped, 1)
            for n in range(2 * C):
                h, j = n // C, n % C
                dve.wait_ge(part1, n + 1)
                if n >= 2:
                    dve.wait_ge(part3, n - 1)
                nc.vector.tensor_tensor(rest[0:rows_of[j], n % 2, :], core.bank[4 + n % 4][0:rows_of[j], :],
                                        part[0:rows_of[j], 0, j, h * HALF:(h + 1) * HALF], ALU.subtract).then_inc(rest1, 1)

        @block.gpsimd
        def _(pool):
            pool.memset(v[:, :, :, HD:HD + 1], 1.0).then_inc(ones_made, 1)
            pool.wait_ge(ones_made, 1)
            pool.memset(ks[ROWS:KROWS, :, :], 1.0).then_inc(ones_made, 1)
            pool.wait_ge(ones_made, 2)
            for n in range(2 * C):
                h, j = n // C, n % C
                span = slice(h * HALF, (h + 1) * HALF)
                pool.wait_ge(rest1, n + 1)
                nc.gpsimd.tensor_copy(part[0:rows_of[j], 1, j, span], rest[0:rows_of[j], n % 2, :]).then_inc(part2, 1)
                pool.wait_ge(part2, n + 1)
                nc.gpsimd.tensor_tensor(part[0:rows_of[j], 2, j, span], rest[0:rows_of[j], n % 2, :],
                                        part[0:rows_of[j], 1, j, span], ALU.subtract).then_inc(part3, 1)


def order_of_a_head(cfg):
    n = len(cfg.quads)
    slots = 2 * n - 1
    tiles = [[("max", t) for t in range(TT) if t * slots // TT == i] for i in range(slots)] + [[]]
    order = []
    for g, (_, units, _, _) in enumerate(cfg.quads):
        before, back = (g - 1, 0) if g else (n - 1, 1)
        order += [("scores", u) for u in units[0:2]] + tiles[2 * g] + [("values", before, back)]
        order += [("scores", u) for u in units[2:4]] + tiles[2 * g + 1]
        if cfg.quads[before][3]:
            order.append(("turn", cfg.quads[before][0], back))
    order.append(("shift",))
    return order


def attend(core, tag, cfg, v, qs, ks, ctxs):
    nc = core.nc
    U, Q = len(cfg.units), len(cfg.quads)
    UNROLL = 4
    TURNS = HEADS // UNROLL
    group = HEADS // cfg.kv_heads
    assert group in (1, UNROLL)
    scores_ready, max_done, shift_step, shift_ready, shift_rows, rows_stored = (
        core.sem(f"{tag}_{n}") for n in ("sc", "mxd", "shs", "shr", "shrow", "rst"))
    tsc_ready, probs_ready, probs_used, v_placed, acc_stored, turned, summed, inverted, ctx_stored = (
        core.sem(f"{tag}_{n}") for n in ("tsc", "pr", "pu", "vp", "accs", "turned", "summed", "inv", "cst"))
    order = order_of_a_head(cfg)
    quad_of = {u: (g, units.index(u)) for g, (_, units, _, _) in enumerate(cfg.quads) for u in units}
    last_quad = {half: g for g, (half, _, _, last) in enumerate(cfg.quads) if last}
    with ExitStack() as ctx:
        def sb(name, shape, dt=F32):
            return ctx.enter_context(nc.sbuf_tensor(f"{tag}_{name}", shape, dt))

        mx, rest = sb("mx", [P, TT]), sb("mrest", [P, TT])
        shift = sb("shift", [P, TT, PARTS], BF16)
        probs = sb("probs", [P, 8, HALF])
        V_BUFFERS = 1 if group == UNROLL else 2
        vh = sb("vh", [P, V_BUFFERS, TT, HD + 1])
        acc = sb("acc", [P, 2, HALF])
        sums, rden = sb("sums", [P, 2, 4, HD + 1]), sb("rden", [P, 2, 4])
        block = ctx.enter_context(nc.Block())
        acc_bank, small_bank = core.bank[6], core.bank[7]

        def is_at(h, n):
            return isinstance(h, int) and h == n

        def buffer_of(i, g, x=0):
            return 4 * ((Q * i + g) % 2) + x

        def kv_of(turn, i):
            return UNROLL * turn + i if group == 1 else turn + i // UNROLL

        def max_buffer(t):
            return core.psum[:, 2 * (t % 2):2 * (t % 2) + 2, :].rearrange("p b n -> p (b n)")

        @block.tensor
        def _(pe):
            def maxima(h, kv, t):
                if not (isinstance(h, int) and TT * h + t < 2):
                    pe.wait_ge(max_done, TT * h + t - 1)
                col = 0
                for k0, nk, mask in cfg.maxima[t]:
                    out = max_buffer(t)[:, col:col + nk]
                    last = nc.tensor.matmul(out, qs[0:ROWS, h, t * P:(t + 1) * P], ks[0:ROWS, kv, k0:k0 + nk],
                                            start=True, stop=mask is None, skip_group_check=True)
                    if mask is not None:
                        last = nc.tensor.matmul(out, core.ident_h[:], core.mask_h[mask][:, 0:nk],
                                                start=False, stop=True, skip_group_check=True)
                    col += nk
                last.then_inc(scores_ready, 1)

            def shift_to_rows(h):
                pe.wait_ge(shift_ready, h + 1)
                for half in range(2):
                    if half == 1:
                        pe.wait_ge(rows_stored, 2 * h + 1)
                    elif not is_at(h, 0):
                        pe.wait_ge(summed, 2 * h - 1)
                    for t in range(4):
                        last = nc.tensor.matmul(small_bank[ROWS:KROWS, t * P:(t + 1) * P], shift[:, 4 * half + t, :],
                                                core.ident_h[:], start=True, stop=True)
                    last.then_inc(shift_rows, 1)

            def scores(h, i, kv, u):
                k0, q0, nq, masks = cfg.units[u]
                if u == 0:
                    pe.wait_ge(rows_stored, 2 * h + 2)
                if not (isinstance(h, int) and U * h + u < 2):
                    pe.wait_ge(probs_ready, U * h + u - 1)
                bank = core.bank[4 + (U * i + u) % 2]
                last = nc.tensor.matmul(bank[:, 0:nq], ks[:, kv, k0:k0 + P], qs[:, h, q0:q0 + nq],
                                        start=True, stop=not masks, skip_group_check=True)
                for m, (c0, mask) in enumerate(masks):
                    last = nc.tensor.matmul(bank[:, c0:c0 + P], core.ident_h[:], core.mask_h[mask][:],
                                            start=False, stop=m == len(masks) - 1, skip_group_check=True)
                last.then_inc(tsc_ready, 1)

            def values(turn, h, i, g):
                half, units, first, last_of_half = cfg.quads[g]
                if first:
                    if g == 0:
                        pe.wait_ge(v_placed, turn + 1 if group == UNROLL else h + 1)
                    if not (is_at(h, 0) and half == 0):
                        pe.wait_ge(acc_stored, 2 * h + half)
                    nc.tensor.matmul(acc_bank[:], core.zero_h[:, 0:P], core.zero_h[:], start=True, stop=False,
                                     skip_group_check=True)
                pe.wait_ge(probs_ready, U * h + units[-1] + 1)
                for x, u in enumerate(units):
                    k0, q0, nq, _ = cfg.units[u]
                    last = nc.tensor.matmul(acc_bank[32 * x:32 * x + HD + 1, q0 % HALF:q0 % HALF + nq],
                                            vh[:, i % V_BUFFERS, k0 // P, :], probs[:, buffer_of(i, g, x), 0:nq],
                                            start=False, stop=last_of_half, skip_group_check=True)
                last.then_inc(probs_used, 1)

            def turn_sums(h, half):
                pe.wait_ge(acc_stored, 2 * h + half + 1)
                if half == 0 and is_at(h, 0):
                    pe.wait_ge(rows_stored, 2)
                elif half == 0:
                    pe.wait_ge(summed, 2 * h)
                elif is_at(h, HEADS - 1):
                    pe.wait_ge(summed, 2 * h + 1)
                else:
                    pe.wait_ge(rows_stored, 2 * h + 4)
                for t in range(4):
                    last = nc.tensor.transpose(small_bank[:, t * P:(t + 1) * P], acc[:, half, t * P:(t + 1) * P], core.ident[:])
                last.then_inc(turned, 1)

            def turn(g, final=False):
                for i in range(UNROLL):
                    h = UNROLL * g + i
                    is_last = final and i == UNROLL - 1
                    for what, *args in order:
                        if what == "scores":
                            scores(h, i, kv_of(g, i), args[0])
                        elif what == "max" and not is_last:
                            maxima(h + 1, kv_of(g, i + 1), args[0])
                        elif what == "values" and not (is_at(h, 0) and args[1]):
                            values(g, h - args[1], (i - args[1]) % UNROLL, args[0])
                        elif what == "turn" and not (is_at(h, 0) and args[1]):
                            turn_sums(h - args[1], args[0])
                        elif what == "shift" and not is_last:
                            shift_to_rows(h + 1)

            for t in range(TT):
                maxima(0, 0, t)
            shift_to_rows(0)
            turn(0)
            with pe.Fori(1, TURNS - 1) as g:
                turn(g)
            turn(TURNS - 1, final=True)
            values(TURNS - 1, HEADS - 1, UNROLL - 1, Q - 1)
            turn_sums(HEADS - 1, 1)

        @block.scalar
        def _(act):
            def store_rows(h):
                for half in range(2):
                    act.wait_ge(shift_rows, 2 * h + half + 1)
                    nc.scalar.copy(qs[ROWS:KROWS, h, half * HALF:(half + 1) * HALF],
                                   small_bank[ROWS:KROWS, :]).then_inc(rows_stored, 1)

            def exponentiate(h, i, u):
                nq = cfg.units[u][2]
                g, x = quad_of[u]
                act.wait_ge(tsc_ready, U * h + u + 1)
                if x == 0 and not (isinstance(h, int) and Q * h + g < 2):
                    act.wait_ge(probs_used, Q * h + g - 1)
                nc.scalar.activation(probs[:, buffer_of(i, g, x), 0:nq], core.bank[4 + (U * i + u) % 2][:, 0:nq],
                                     ACT.Exp, scale=HD ** -0.5).then_inc(probs_ready, 1)

            def store_sums(h, half):
                act.wait_ge(probs_used, Q * h + last_quad[half] + 1)
                if not is_at(h, 0):
                    act.wait_ge(turned, 2 * h + half - 1)
                nc.scalar.copy(acc[:, half, :], acc_bank[:]).then_inc(acc_stored, 1)

            def turn(g, final=False):
                for i in range(UNROLL):
                    h = UNROLL * g + i
                    for what, *args in order:
                        if what == "scores":
                            exponentiate(h, i, args[0])
                        elif what == "values" and not (is_at(h, 0) and args[1]):
                            if cfg.quads[args[0]][3]:
                                store_sums(h - args[1], cfg.quads[args[0]][0])
                        elif what == "shift" and not (final and i == UNROLL - 1):
                            store_rows(h + 1)

            store_rows(0)
            turn(0)
            with act.Fori(1, TURNS - 1) as g:
                turn(g)
            turn(TURNS - 1, final=True)
            store_sums(HEADS - 1, 1)

        @block.gpsimd
        def _(pool):
            def place(g, i):
                h = UNROLL * g + i
                if group == UNROLL:
                    if not is_at(h, 0):
                        pool.wait_ge(probs_used, Q * h)
                        pool.wait_ge(v_placed, g)
                    nc.gpsimd.tensor_copy(vh[:, 0, :, :], v[:, :, g, :]).then_inc(v_placed, 1)
                    return
                if not (isinstance(h, int) and h < 2):
                    pool.wait_ge(probs_used, Q * (h - 1))
                if not is_at(h, 0):
                    pool.wait_ge(v_placed, h)
                nc.gpsimd.tensor_copy(vh[:, i % 2, :, :], v[:, :, kv_of(g, i), :]).then_inc(v_placed, 1)

            placed = range(0, UNROLL, UNROLL if group == UNROLL else 1)
            for i in placed:
                place(0, i)
            with pool.Fori(1, TURNS) as g:
                for i in placed:
                    place(g, i)

        @block.vector
        def _(dve):
            def maximum(h, t):
                width = sum(nk for _, nk, _ in cfg.maxima[t])
                dve.wait_ge(scores_ready, TT * h + t + 1)
                if t == 0 and not is_at(h, 0):
                    dve.wait_ge(shift_step, 3 * h)
                nc.vector.tensor_reduce(mx[:, t:t + 1], max_buffer(t)[:, 0:width], AX_X, ALU.max).then_inc(max_done, 1)

            def make_shift(h):
                dve.wait_ge(max_done, TT * h + TT)
                if not is_at(h, 0):
                    dve.wait_ge(shift_rows, 2 * h)
                    dve.wait_ge(shift_ready, h)
                nc.vector.tensor_scalar(shift[:, :, 0], mx[:], -1.0, None, ALU.mult).then_inc(shift_step, 1)
                dve.wait_ge(shift_step, 3 * h + 1)
                nc.vector.scalar_tensor_tensor(out=rest[:], in0=mx[:], scalar=-1.0, in1=shift[:, :, 0],
                                               op0=ALU.mult, op1=ALU.subtract).then_inc(shift_step, 1)
                dve.wait_ge(shift_step, 3 * h + 2)
                nc.vector.tensor_copy(shift[:, :, 1], rest[:]).then_inc(shift_step, 1)
                dve.wait_ge(shift_step, 3 * h + 3)
                nc.vector.tensor_tensor(shift[:, :, 2], rest[:], shift[:, :, 1], ALU.subtract).then_inc(shift_ready, 1)

            def normalize_sums(h, half):
                n = 2 * h + half
                dve.wait_ge(turned, n + 1)
                if not is_at(h, 0):
                    dve.wait_ge(ctx_stored, n - 1)
                parts = small_bank[:].rearrange("p (t g c) -> p t c g", g=4, c=32)[:, :, 0:HD + 1, :]
                nc.vector.tensor_reduce(sums[:, half, :, :], parts, AX_X, ALU.add).then_inc(summed, 1)
                dve.wait_ge(summed, n + 1)
                nc.vector.reciprocal(rden[:, half, :], sums[:, half, :, HD]).then_inc(inverted, 1)
                dve.wait_ge(inverted, n + 1)
                nc.vector.tensor_tensor(ctxs[:, 4 * half:4 * half + 4, bass.ds(h * HD, HD)], sums[:, half, :, 0:HD],
                                        rden[:, half, :].unsqueeze(2).broadcast_to([P, 4, HD]), ALU.mult).then_inc(ctx_stored, 1)

            def turn(g, final=False):
                for i in range(UNROLL):
                    h = UNROLL * g + i
                    is_last = final and i == UNROLL - 1
                    for what, *args in order:
                        if what == "max" and not is_last:
                            maximum(h + 1, args[0])
                        elif what == "turn" and not (is_at(h, 0) and args[1]):
                            normalize_sums(h - args[1], args[0])
                        elif what == "shift" and not is_last:
                            make_shift(h + 1)

            for t in range(TT):
                maximum(0, t)
            make_shift(0)
            turn(0)
            with dve.Fori(1, TURNS - 1) as g:
                turn(g)
            turn(TURNS - 1, final=True)
            normalize_sums(HEADS - 1, 1)


def project_out(core, tag, ctxs, extra=None):
    nc, dram = core.nc, core.dram
    wo_loaded, turned, turn_copied, projected, step, added = (
        core.sem(f"{tag}_{n}") for n in ("wol", "tc", "tcc", "po", "poa", "pod"))
    with ExitStack() as ctx:
        ctxT = ctx.enter_context(nc.sbuf_tensor(f"{tag}_ctxT", [P, KC, T], F32))
        wo = core.bwo if tag == "b" else ctx.enter_context(nc.sbuf_tensor(f"{tag}_wo", [P, KC, D], F32))
        block = ctx.enter_context(nc.Block())

        if tag != "b":
            @block.sync
            def _(sp):
                name = {"a": "L0_attn_a_Wo", "c": "L1_attn_a_W_out"}[tag]
                sp.dma_start(wo[:], dram[name].rearrange("(k p) n -> p k n", p=P)).then_inc(wo_loaded, 16)

        @block.tensor
        def _(pe):
            for u in range(4):
                h, k = u // 2, u % 2
                for t in range(4 * h, 4 * h + 4):
                    last = nc.tensor.transpose(core.bank[u][:, (t % 4) * P:(t % 4 + 1) * P],
                                               ctxs[:, t, k * P:(k + 1) * P], core.ident[:])
                last.then_inc(turned, 1)
            if tag != "b":
                pe.wait_ge(wo_loaded, 16)
            for t in range(TT):
                pe.wait_ge(turn_copied, 2 * (t // 4) + 2)
                if t >= 4:
                    pe.wait_ge(added, t - 3)
                for k in range(KC):
                    last = nc.tensor.matmul(core.bank[4 + t % 4][:, 0:D], ctxT[:, k, t * P:(t + 1) * P], wo[:, k, :],
                                            start=(k == 0), stop=(k == KC - 1))
                last.then_inc(projected, 1)

        @block.scalar
        def _(act):
            for u in range(4):
                h, k = u // 2, u % 2
                act.wait_ge(turned, u + 1)
                nc.scalar.copy(ctxT[:, k, h * HALF:(h + 1) * HALF], core.bank[u][:]).then_inc(turn_copied, 1)

        @block.vector
        def _(dve):
            if extra is not None:
                nc.vector.tensor_tensor(core.x[:], core.x[:], extra[:], ALU.add).then_inc(step, 1)
                dve.wait_ge(step, 1)
            for t in range(TT):
                dve.wait_ge(projected, t + 1)
                nc.vector.tensor_tensor(core.x[:, t, :], core.x[:, t, :], core.bank[4 + t % 4][:, 0:D], ALU.add).then_inc(added, 1)


LSCALE = float(np.float32(1.0) / np.sqrt(np.float32(DN + DR)))
LPAIRS = HEADS // 2
UP = DN + DV


def latent(core, tag):
    with ExitStack() as ctx:
        def sb(name, shape, dt=F32):
            return ctx.enter_context(core.nc.sbuf_tensor(f"{tag}_{name}", shape, dt))

        wvo = sb("wvo", [P, LPAIRS, D])
        ctxs = sb("ctxs", [P, TT, HEADS * KVR])
        with ExitStack() as inner:
            def sbi(name, shape, dt=F32):
                return inner.enter_context(core.nc.sbuf_tensor(f"{tag}_{name}", shape, dt))

            wq = sbi("wq", [QR, HEADS, KVR + 2 * DR])
            qcT = sbi("qcT", [QR, T])
            kT = sbi("kT", [P, T])
            v = sbi("v", [P, TT, KVR + 1])
            latent_down(core, tag, qcT, kT, v)
            latent_weights(core, tag, wq, wvo)
            latent_attend(core, tag, wq, qcT, kT, v, ctxs)
        latent_out(core, tag, wvo, ctxs)


def latent_down(core, tag, qcT, kT, v):
    nc, dram = core.nc, core.dram
    W = QR + KVR + DR
    loaded, projected, copied, squared, meaned, rooted, inverted, normed, roped, valued, turned, qk_copied = (
        core.sem(f"{tag}d_{n}") for n in ("ld", "pr", "cp", "sq", "mean", "root", "inv", "norm", "rope", "val", "turn", "qkc"))
    with ExitStack() as ctx:
        def sb(name, shape, dt=F32):
            return ctx.enter_context(nc.sbuf_tensor(f"{tag}d_{name}", shape, dt))

        w = sb("w", [P, KC, W])
        lat = sb("lat", [P, TT, W])
        junk = sb("junk", [P, 2, QR])
        ssq, root, inv = (sb(n, [P, 2, TT]) for n in ("ssq", "rt", "iv"))
        cos, sin = sb("cos", [P, TT, DR]), sb("sin", [P, TT, DR])
        swapped = sb("swapped", [P, TT, DR])
        block = ctx.enter_context(nc.Block())
        spans = ((0, QR, "L1_attn_b_q_norm_w"), (QR, KVR, "L1_attn_b_kv_norm_w"))

        @block.sync
        def _(sp):
            for name, c0, n in (("wq_down", 0, QR), ("wkv_down", QR, KVR), ("wk_rope", QR + KVR, DR)):
                sp.dma_start(w[:, :, c0:c0 + n], dram[f"L1_attn_b_{name}"].rearrange("(k p) n -> p k n", p=P)).then_inc(loaded, 16)
            sp.dma_start(cos[:], dram["c_cos_k"].rearrange("(t p) d -> p t d", p=P)).then_inc(loaded, 16)
            sp.dma_start(sin[:], dram["c_sin_k"].rearrange("(t p) d -> p t d", p=P)).then_inc(loaded, 16)

        @block.tensor
        def _(pe):
            pe.wait_ge(loaded, 80)
            for t in range(TT):
                if t >= 4:
                    pe.wait_ge(copied, t - 3)
                for k in range(KC):
                    last = nc.tensor.matmul(core.bank[t % 4][:, 0:W], core.xT[:, k, t * P:(t + 1) * P], w[:, k, :],
                                            start=(k == 0), stop=(k == KC - 1))
                last.then_inc(projected, 1)
            pe.wait_ge(normed, 4)
            pe.wait_ge(roped, 4)
            for h in range(2):
                for t in range(4 * h, 4 * h + 4):
                    nc.tensor.transpose(core.bank[4 + h][0:QR, (t % 4) * P:(t % 4 + 1) * P], lat[:, t, 0:QR], core.ident[:])
                    last = nc.tensor.transpose(core.bank[6 + h][:, (t % 4) * P:(t % 4 + 1) * P], lat[:, t, QR:W], core.ident[:])
                last.then_inc(turned, 1)

        @block.scalar
        def _(act):
            for t in range(TT):
                act.wait_ge(projected, t + 1)
                nc.scalar.copy(lat[:, t, :], core.bank[t % 4][:, 0:W]).then_inc(copied, 1)
            act.wait_ge(meaned, 2)
            nc.scalar.activation(root[:], ssq[:], ACT.Sqrt).then_inc(rooted, 1)
            for h in range(2):
                act.wait_ge(turned, h + 1)
                nc.scalar.copy(kT[:, h * HALF:(h + 1) * HALF], core.bank[6 + h][:]).then_inc(qk_copied, 1)

        @block.vector
        def _(dve):
            for t in range(TT):
                dve.wait_ge(copied, t + 1)
                for i, (c0, n, _) in enumerate(spans):
                    if t >= 1:
                        dve.wait_ge(squared, 2 * t - 1 + i)
                    nc.vector.tensor_tensor_reduce(junk[:, i, 0:n], lat[:, t, c0:c0 + n], lat[:, t, c0:c0 + n], 1.0, 0.0,
                                                   ALU.mult, ALU.add, ssq[:, i, t:t + 1]).then_inc(squared, 1)
            dve.wait_ge(squared, 2 * TT)
            for i, (c0, n, _) in enumerate(spans):
                nc.vector.tensor_scalar(ssq[:, i, :], ssq[:, i, :], 1.0 / n, 1e-6, ALU.mult, ALU.add).then_inc(meaned, 1)
            dve.wait_ge(rooted, 1)
            nc.vector.reciprocal(inv[:], root[:]).then_inc(inverted, 1)
            dve.wait_ge(inverted, 1)
            for i, (c0, n, _) in enumerate(spans):
                nc.vector.tensor_tensor(lat[:, :, c0:c0 + n], lat[:, :, c0:c0 + n],
                                        inv[:, i, :].unsqueeze(2).broadcast_to([P, TT, n]), ALU.mult).then_inc(normed, 1)
            for i, (c0, n, name) in enumerate(spans):
                dve.wait_ge(normed, i + 1)
                nc.vector.tensor_tensor(lat[:, :, c0:c0 + n], lat[:, :, c0:c0 + n],
                                        core.row[name][:].unsqueeze(1).broadcast_to([P, TT, n]), ALU.mult).then_inc(normed, 1)
            k0 = QR + KVR
            for to, frm in ((0, 1), (1, 0)):
                nc.vector.tensor_tensor(swapped[:, :, to:to + DR - 1:2], lat[:, :, k0 + frm:k0 + frm + DR - 1:2],
                                        sin[:, :, to:to + DR - 1:2], ALU.mult).then_inc(roped, 1)
            dve.wait_ge(roped, 2)
            nc.vector.tensor_tensor(lat[:, :, k0:W], lat[:, :, k0:W], cos[:], ALU.mult).then_inc(roped, 1)
            dve.wait_ge(roped, 3)
            nc.vector.tensor_tensor(lat[:, :, k0:W], lat[:, :, k0:W], swapped[:], ALU.add).then_inc(roped, 1)
            dve.wait_ge(normed, 4)
            nc.vector.tensor_copy(v[:, :, 0:KVR], lat[:, :, QR:QR + KVR]).then_inc(valued, 1)
            nc.vector.memset(v[:, :, KVR:KVR + 1], 1.0).then_inc(valued, 1)
            for h in range(2):
                dve.wait_ge(turned, h + 1)
                nc.vector.tensor_copy(qcT[:, h * HALF:(h + 1) * HALF], core.bank[4 + h][0:QR, :]).then_inc(qk_copied, 1)


def latent_weights(core, tag, wq, wvo):
    nc, dram = core.nc, core.dram
    up_loaded, rope_copied, turned, turn_copied, folded, fold_copied = (
        core.sem(f"{tag}w_{n}") for n in ("ld", "rc", "turn", "tc", "fold", "fc"))
    NT = QR + 2 * KVR
    with ExitStack() as ctx:
        def sb(name, shape, dt=F32):
            return ctx.enter_context(nc.sbuf_tensor(f"{tag}w_{name}", shape, dt))

        wqu = sb("wqu", [QR, HEADS * DN])
        wkv = sb("wkv", [KVR, HEADS * UP])
        wo = sb("wo", [P, HEADS, D])
        wr = sb("wr", [QR, HEADS, DR])
        wt = sb("wt", [P, 2, NT])
        block = ctx.enter_context(nc.Block())

        @block.sync
        def _(sp):
            sp.dma_start(wqu[:], dram["L1_attn_b_wq_up"]).then_inc(up_loaded, 16)
            sp.dma_start(wkv[:], dram["L1_attn_b_wkv_up"]).then_inc(up_loaded, 16)
            sp.dma_start(wr[:], dram["L1_attn_b_wq_rope"].rearrange("r (h d) -> r h d", d=DR)).then_inc(up_loaded, 16)
            sp.dma_start(wo[:], dram["L1_attn_b_wo"].rearrange("(h p) n -> p h n", p=P)).then_inc(up_loaded, 16)

        @block.gpsimd
        def _(pool):
            pool.wait_ge(up_loaded, 64)
            nc.gpsimd.tensor_copy(wq[:, :, KVR:KVR + DR], wr[:]).then_inc(rope_copied, 1)
            for n, (to, frm) in enumerate(((0, 1), (1, 0))):
                pool.wait_ge(rope_copied, n + 1)
                nc.gpsimd.tensor_copy(wq[:, :, KVR + DR + to:KVR + 2 * DR:2], wr[:, :, frm:DR:2]).then_inc(rope_copied, 1)

        @block.tensor
        def _(pe):
            pe.wait_ge(up_loaded, 64)

            def turn(h):
                if h >= 2:
                    pe.wait_ge(turn_copied, h - 1)
                b = core.bank[h % 2]
                nc.tensor.transpose(b[:, 0:QR], wqu[:, h * DN:(h + 1) * DN], core.ident[0:QR, 0:QR])
                nc.tensor.transpose(b[:, QR:QR + KVR], wkv[:, h * UP:h * UP + DN], core.ident[0:KVR, 0:KVR])
                nc.tensor.transpose(b[:, QR + KVR:NT], wkv[:, h * UP + DN:(h + 1) * UP],
                                    core.ident[0:KVR, 0:KVR]).then_inc(turned, 1)

            def fold(h):
                pe.wait_ge(turn_copied, h + 1)
                if h >= 2:
                    pe.wait_ge(fold_copied, 2 * (h - 1))
                t = wt[:, h % 2, :]
                p0 = KVR * (h % 2)
                nc.tensor.matmul(core.bank[2 + h % 2][0:QR, 0:KVR], t[:, 0:QR], t[:, QR:QR + KVR], start=True, stop=True)
                nc.tensor.matmul(core.bank[4 + h % 2][p0:p0 + KVR, 0:D], t[:, QR + KVR:NT], wo[:, h, :],
                                 start=True, stop=True).then_inc(folded, 1)

            turn(0)
            for h in range(HEADS):
                if h + 1 < HEADS:
                    turn(h + 1)
                fold(h)

        @block.vector
        def _(dve):
            def turned_out(h):
                dve.wait_ge(turned, h + 1)
                if h >= 2:
                    dve.wait_ge(folded, h - 1)
                nc.vector.tensor_copy(wt[:, h % 2, :], core.bank[h % 2][:, 0:NT]).then_inc(turn_copied, 1)

            turned_out(0)
            for h in range(HEADS):
                if h + 1 < HEADS:
                    turned_out(h + 1)
                dve.wait_ge(folded, h + 1)
                nc.vector.tensor_copy(wq[:, h, 0:KVR], core.bank[2 + h % 2][0:QR, 0:KVR]).then_inc(fold_copied, 1)
                p0 = KVR * (h % 2)
                nc.vector.tensor_copy(wvo[p0:p0 + KVR, h // 2, :], core.bank[4 + h % 2][p0:p0 + KVR, 0:D]).then_inc(fold_copied, 1)


def latent_attend(core, tag, wq, qcT, kT, v, ctxs):
    nc, dram = core.nc, core.dram
    tab_loaded, w_placed, proj_ready, lat_copied, proj_used, q_ready = (
        core.sem(f"{tag}a_{n}") for n in ("tab", "wpl", "pj", "lc", "pjd", "qr"))
    score_ready, negmax_ready, exp_done, turned, turn_copied, pv_done, norm_step, ctx_stored = (
        core.sem(f"{tag}a_{n}") for n in ("sc", "nm", "ex", "tu", "tcp", "pv", "ns", "cs"))
    NP_, NT_ = 4, 4
    STEPS = 2 * TT
    TURNS = HEADS // 2
    batches = [[list(range(b, min(b + 4, t + 1))) for b in range(0, t + 1, 4)] for t in range(TT)]
    before = [sum(len(b) for b in batches[:t]) for t in range(TT + 1)]
    NBAT = before[TT]
    assert NBAT % NT_ == 0 and STEPS % NP_ == 0
    PROJ_AT = {0: 0, 2: 1, 4: 2, 6: 3}
    with ExitStack() as ctx:
        def sb(name, shape, dt=F32):
            return ctx.enter_context(nc.sbuf_tensor(f"{tag}a_{name}", shape, dt))

        cos, sin = sb("cos", [P, T]), sb("sin", [P, T])
        wh = sb("wh", [QR, 2, KVR + 2 * DR])
        q = sb("q", [P, 2, T])
        swapped = sb("swapped", [P, T])
        negmax = sb("negmax", [P, 2])
        rden = sb("rden", [P, 2])
        probs = sb("probs", [P, NP_, T])
        probsT = sb("probsT", [P, NT_, HALF])
        block = ctx.enter_context(nc.Block())
        pv = core.bank[6][:, 0:KVR + 1]

        def known(i, s):
            return isinstance(i, int)

        def head_of(i, s):
            return 2 * i + s // TT

        def through(i, s, back):
            s2 = s - back
            return NBAT * 2 * i + NBAT * (s2 // TT) + before[s2 % TT + 1]

        def scores_of(n2):
            return core.psum[:, 2 * n2:2 * n2 + 2, :].rearrange("p b n -> p (b n)")

        @block.sync
        def _(sp):
            sp.dma_start(cos[KVR:P, :], dram["c_cos_q"]).then_inc(tab_loaded, 16)
            sp.dma_start(sin[KVR:P, :], dram["c_sin_q"]).then_inc(tab_loaded, 16)

        @block.tensor
        def _(pe):
            def project(h, slot, c):
                half = c % 2
                if c == 0:
                    pe.wait_ge(w_placed, h + 1)
                if not (isinstance(h, int) and h == 0 and c == 0):
                    pe.wait_ge(proj_used, 4 * h + c)
                if c in (1, 2):
                    pe.wait_ge(lat_copied, 2 * h + c)
                rhs = qcT[:, half * HALF:(half + 1) * HALF]
                if c < 2:
                    last = nc.tensor.matmul(core.bank[7][:], wh[:, slot, 0:KVR + DR], rhs, start=True, stop=True)
                else:
                    last = nc.tensor.matmul(core.bank[7][KVR:P, :], wh[:, slot, KVR + DR:KVR + 2 * DR], rhs, start=True, stop=True)
                last.then_inc(proj_ready, 1)

            def score(i, s):
                h, t = head_of(i, s), s % TT
                if t == 0:
                    pe.wait_ge(q_ready, 2 * h + 2)
                    pe.wait_ge(lat_copied, 2 * h + 2)
                if not (known(i, s) and STEPS * i + s < 2):
                    pe.wait_ge(exp_done, STEPS * i + s - 1)
                out = scores_of(s % 2)
                for k0 in range(0, (t + 1) * P, HALF):
                    nk = min(HALF, (t + 1) * P - k0)
                    nc.tensor.matmul(out[:, k0:k0 + nk], q[:, s // TT % 2, t * P:(t + 1) * P], kT[:, k0:k0 + nk],
                                     start=True, stop=False, skip_group_check=True)
                nc.tensor.matmul(out[:, t * P:(t + 1) * P], core.ident_h[:], core.mask_h["causal"][:],
                                 start=False, stop=True, skip_group_check=True).then_inc(score_ready, 1)

            def back(i, s):
                s2 = s - 2
                t = s2 % TT
                first = through(i, s, 2) - len(batches[t])
                for b, blocks in enumerate(batches[t]):
                    if b == 0:
                        pe.wait_ge(exp_done, STEPS * i + s2 + 1)
                    if not (known(i, s) and first + b < 2):
                        pe.wait_ge(turn_copied, first + b - 1)
                    for x, k in enumerate(blocks):
                        last = nc.tensor.transpose(core.bank[4 + (before[t] + b) % 2][:, x * P:(x + 1) * P],
                                                   probs[:, s2 % NP_, k * P:(k + 1) * P], core.ident[:])
                    last.then_inc(turned, 1)
                for b, blocks in enumerate(batches[t]):
                    pe.wait_ge(turn_copied, first + b + 1)
                    if b == 0 and not (known(i, s) and STEPS * i + s2 == 0):
                        pe.wait_ge(ctx_stored, STEPS * i + s2)
                    for x, k in enumerate(blocks):
                        last = nc.tensor.matmul(pv, probsT[:, (before[t] + b) % NT_, x * P:(x + 1) * P], v[:, k, :],
                                                start=(k == 0), stop=(k == t))
                    last.then_inc(pv_done, 1)

            def turn(i, final=False):
                for s in range(STEPS):
                    score(i, s)
                    if s % TT in PROJ_AT and not (final and s >= TT):
                        project(head_of(i, s) + 1, (s // TT + 1) % 2, PROJ_AT[s % TT])
                    if not (known(i, s) and STEPS * i + s < 2):
                        back(i, s)

            for c in range(4):
                project(0, 0, c)
            turn(0)
            with pe.Fori(1, TURNS - 1) as i:
                turn(i)
            turn(TURNS - 1, final=True)
            back(TURNS - 1, STEPS)
            back(TURNS - 1, STEPS + 1)

        @block.scalar
        def _(act):
            def copy_latent(h, slot, c):
                act.wait_ge(proj_ready, 4 * h + c + 1)
                nc.scalar.activation(q[0:KVR, slot, c * HALF:(c + 1) * HALF], core.bank[7][0:KVR, :], ACT.Copy,
                                     scale=LSCALE).then_inc(lat_copied, 1)

            def copy_turned(i, s):
                s2 = s - 2
                t = s2 % TT
                first = through(i, s, 2) - len(batches[t])
                for b, blocks in enumerate(batches[t]):
                    act.wait_ge(turned, first + b + 1)
                    if not (known(i, s) and first + b < NT_):
                        act.wait_ge(pv_done, first + b - NT_ + 1)
                    n = len(blocks) * P
                    nc.scalar.copy(probsT[:, (before[t] + b) % NT_, 0:n],
                                   core.bank[4 + (before[t] + b) % 2][:, 0:n]).then_inc(turn_copied, 1)

            def turn(i, final=False):
                for s in range(STEPS):
                    t = s % TT
                    if PROJ_AT.get(t, 4) < 2 and not (final and s >= TT):
                        copy_latent(head_of(i, s) + 1, (s // TT + 1) % 2, PROJ_AT[t])
                    if not (known(i, s) and STEPS * i + s < 2):
                        copy_turned(i, s)
                    act.wait_ge(negmax_ready, STEPS * i + s + 1)
                    if not (known(i, s) and STEPS * i + s < NP_):
                        act.wait_ge(turned, through(i, s, NP_))
                    w = (t + 1) * P
                    nc.scalar.activation(probs[:, s % NP_, 0:w], scores_of(s % 2)[:, 0:w], ACT.Exp,
                                         bias=negmax[:, s % 2:s % 2 + 1]).then_inc(exp_done, 1)

            for c in range(2):
                copy_latent(0, 0, c)
            turn(0)
            with act.Fori(1, TURNS - 1) as i:
                turn(i)
            turn(TURNS - 1, final=True)
            copy_turned(TURNS - 1, STEPS)
            copy_turned(TURNS - 1, STEPS + 1)

        @block.gpsimd
        def _(pool):
            def place(h, slot, first=False):
                if not first:
                    pool.wait_ge(proj_ready, 4 * (h - 1))
                    pool.wait_ge(q_ready, 2 * h - 2)
                elif h == 1:
                    pool.wait_ge(w_placed, 1)
                nc.gpsimd.tensor_copy(wh[:, slot, :], wq[:, bass.ds(h, 1), :].rearrange("r a c -> r (a c)")).then_inc(w_placed, 1)

            def add(h, slot, last=False):
                if last:
                    pool.wait_ge(q_ready, 2 * h)
                else:
                    pool.wait_ge(w_placed, h + 2)
                for half in range(2):
                    if half == 1:
                        pool.wait_ge(q_ready, 2 * h + 1)
                    pool.wait_ge(proj_used, 4 * h + 3 + half)
                    span = slice(half * HALF, (half + 1) * HALF)
                    nc.gpsimd.tensor_tensor(q[KVR:P, slot, span], q[KVR:P, slot, span], swapped[KVR:P, span],
                                            ALU.add).then_inc(q_ready, 1)

            place(0, 0, first=True)
            place(1, 1, first=True)
            add(0, 0)
            with pool.Fori(1, TURNS) as i:
                place(2 * i, 0)
                add(2 * i - 1, 1)
                place(2 * i + 1, 1)
                add(2 * i, 0)
            add(HEADS - 1, 1, last=True)

        @block.vector
        def _(dve):
            def rotate(h, slot, c):
                half = c % 2
                span = slice(half * HALF, (half + 1) * HALF)
                dve.wait_ge(proj_ready, 4 * h + c + 1)
                if c >= 2 and not (isinstance(h, int) and h == 0):
                    dve.wait_ge(q_ready, 2 * h + half - 1)
                out, table = (q[KVR:P, slot, span], cos) if c < 2 else (swapped[KVR:P, span], sin)
                nc.vector.scalar_tensor_tensor(out=out, in0=core.bank[7][KVR:P, :], scalar=LSCALE,
                                               in1=table[KVR:P, span], op0=ALU.mult, op1=ALU.mult).then_inc(proj_used, 1)

            def store(i, s):
                s2 = s - 2
                h, t = 2 * i + s2 // TT, s2 % TT
                n = STEPS * i + s2
                dve.wait_ge(pv_done, through(i, s, 2))
                nc.vector.reciprocal(rden[:, s2 % 2:s2 % 2 + 1], pv[:, KVR:KVR + 1]).then_inc(norm_step, 1)
                dve.wait_ge(norm_step, n + 1)
                nc.vector.tensor_scalar(ctxs[:, t, bass.ds(h * KVR, KVR)], pv[:, 0:KVR], rden[:, s2 % 2:s2 % 2 + 1],
                                        None, ALU.mult).then_inc(ctx_stored, 1)

            def turn(i, final=False):
                for s in range(STEPS):
                    t = s % TT
                    dve.wait_ge(score_ready, STEPS * i + s + 1)
                    if not (known(i, s) and STEPS * i + s < 2):
                        dve.wait_ge(exp_done, STEPS * i + s - 1)
                    nc.vector.tensor_reduce(negmax[:, s % 2:s % 2 + 1], scores_of(s % 2)[:, 0:(t + 1) * P], AX_X, ALU.max,
                                            negate=True).then_inc(negmax_ready, 1)
                    if t in PROJ_AT and not (final and s >= TT):
                        rotate(head_of(i, s) + 1, (s // TT + 1) % 2, PROJ_AT[t])
                    if not (known(i, s) and STEPS * i + s < 2):
                        store(i, s)

            dve.wait_ge(tab_loaded, 32)
            for c in range(4):
                rotate(0, 0, c)
            turn(0)
            with dve.Fori(1, TURNS - 1) as i:
                turn(i)
            turn(TURNS - 1, final=True)
            store(TURNS - 1, STEPS)
            store(TURNS - 1, STEPS + 1)


def latent_out(core, tag, wvo, ctxs):
    nc = core.nc
    turned, copied_act, copied_dve, projected, added = (core.sem(f"{tag}o_{n}") for n in ("tu", "ca", "cd", "pr", "ad"))
    with ExitStack() as ctx:
        ctxT = ctx.enter_context(nc.sbuf_tensor(f"{tag}o_ctxT", [P, LPAIRS, T], F32))
        block = ctx.enter_context(nc.Block())

        @block.tensor
        def _(pe):
            for h in range(2):
                for c in range(LPAIRS):
                    u = LPAIRS * h + c
                    if u >= 4:
                        pe.wait_ge(copied_act if u % 2 == 0 else copied_dve, (u - 4) // 2 + 1)
                    for t in range(4 * h, 4 * h + 4):
                        last = nc.tensor.transpose(core.bank[u % 4][:, (t % 4) * P:(t % 4 + 1) * P],
                                                   ctxs[:, t, c * P:(c + 1) * P], core.ident[:])
                    last.then_inc(turned, 1)
                for t in range(4 * h, 4 * h + 4):
                    pe.wait_ge(copied_act, 4 * h + 4)
                    pe.wait_ge(copied_dve, 4 * h + 4)
                    if t >= 4:
                        pe.wait_ge(added, t - 3)
                    for c in range(LPAIRS):
                        last = nc.tensor.matmul(core.bank[4 + t % 4][:, 0:D], ctxT[:, c, t * P:(t + 1) * P], wvo[:, c, :],
                                                start=(c == 0), stop=(c == LPAIRS - 1))
                    last.then_inc(projected, 1)

        @block.scalar
        def _(act):
            for u in range(0, 2 * LPAIRS, 2):
                act.wait_ge(turned, u + 1)
                h, c = u // LPAIRS, u % LPAIRS
                nc.scalar.copy(ctxT[:, c, h * HALF:(h + 1) * HALF], core.bank[u % 4][:]).then_inc(copied_act, 1)

        @block.vector
        def _(dve):
            for h in range(2):
                for u in range(h * LPAIRS + 1, (h + 1) * LPAIRS, 2):
                    dve.wait_ge(turned, u + 1)
                    nc.vector.tensor_copy(ctxT[:, u % LPAIRS, h * HALF:(h + 1) * HALF], core.bank[u % 4][:]).then_inc(copied_dve, 1)
                for t in range(4 * h, 4 * h + 4):
                    dve.wait_ge(projected, t + 1)
                    nc.vector.tensor_tensor(core.x[:, t, :], core.x[:, t, :], core.bank[4 + t % 4][:, 0:D], ALU.add).then_inc(added, 1)


def program(nc, dram):
    with ExitStack() as ctx:
        core = Core(nc, ctx, dram)
        start(core)
        normalize(core, "n1", core.x, core.xn)
        attention(core, "a", ATT_A)
        normalize(core, "n2", core.x, core.xn)
        moe(core, "e1")
        core.clear_semaphores()
        normalize(core, "n3", core.x, core.xn)
        attention(core, "b", ATT_B)
        normalize(core, "n4", core.x, core.xn)
        moe(core, "e2")
        core.clear_semaphores()
        normalize(core, "n5", core.x, core.xn, turn=False)
        normalize(core, "n5i", core.xn, core.xi, affine=(core.row["L1_attn_a_ln_w"], core.row["L1_attn_a_ln_b"]))
        attention(core, "c", ATT_C)
        normalize(core, "n6", core.x, core.xn)
        ffn(core, "f1")
        core.clear_semaphores()
        normalize(core, "n7", core.x, core.xn)
        latent(core, "l")
        normalize(core, "n8", core.x, core.xn)
        ffn(core, "f2")
        finish(core)


def _constants():
    c = {}
    c["c_ident"] = np.eye(P, dtype=np.float32)
    i, j = np.arange(P)[:, None], np.arange(P)[None, :]
    neg = np.float32(NEG)
    causal = np.where(j <= i, np.float32(0), neg)
    prev = np.where(j > i, np.float32(0), neg)
    prev1 = np.where((j > i) | (j < 4), np.float32(0), neg)
    for n, m in (("causal", causal), ("prev", prev), ("prev1", prev1)):
        c[f"c_{n}"] = np.ascontiguousarray(m.astype(np.float32))
        c[f"c_{n}T"] = np.ascontiguousarray(m.T.astype(np.float32))
    c["c_sinkT"] = np.where(np.broadcast_to(i, (P, P)) < 4, np.float32(0), neg).astype(np.float32)
    t = np.arange(T, dtype=np.float32)

    def angles(n):
        inv = np.float32(1) / np.float32(10000) ** (np.arange(0, n, 2, dtype=np.float32) / np.float32(n))
        a = t[:, None] * inv[None, :].astype(np.float32)
        return np.cos(a).astype(np.float32), np.sin(a).astype(np.float32)

    cos, sin = angles(HD)
    c["c_cos_a"] = np.concatenate([cos, cos], 1)
    c["c_sin_a"] = np.concatenate([-sin, sin], 1)
    cos, sin = angles(HD // 2)
    c["c_cos_c"] = np.concatenate([np.repeat(cos, 2, 1), np.ones((T, HD // 2), np.float32)], 1)
    s = np.repeat(sin, 2, 1)
    s[:, 0::2] *= -1
    c["c_sin_c"] = np.concatenate([s, np.zeros((T, HD // 2), np.float32)], 1)
    cos, sin = angles(DR)
    s = np.repeat(sin, 2, 1)
    s[:, 0::2] *= -1
    c["c_cos_k"] = np.repeat(cos, 2, 1)
    c["c_sin_k"] = s
    c["c_cos_q"] = np.repeat(cos, 2, 1).T
    c["c_sin_q"] = s.T
    return {k: np.ascontiguousarray(v, dtype=np.float32) for k, v in c.items()}


def kernel(**inputs):
    import concourse.bacc as _bacc
    from concourse.bass_utils import run_bass_kernel_spmd as _run

    nc = _bacc.Bacc("TRN2", target_bir_lowering=False, num_devices=1)
    arrays, dram = {}, {}
    for name, a in {**inputs, **_constants()}.items():
        a = np.ascontiguousarray(a)
        arrays[f"in_{name}"] = a
        dram[name] = nc.dram_tensor(f"in_{name}", a.shape, mybir.dt.from_np(a.dtype), kind="ExternalInput").ap()
    dram["out"] = nc.dram_tensor("out_0", (1, T, D), F32, kind="ExternalOutput").ap()
    program(nc, dram)
    r = _run(nc, [arrays], core_ids=[0])
    return r.results[0]["out_0"]
```

```python
from contextlib import ExitStack

import numpy as np

import concourse.bass as bass
from concourse import mybir

ALU = mybir.AluOpType
ACT = mybir.ActivationFunctionType
AX_X = mybir.AxisListType.X
F32 = mybir.dt.float32
BF16 = mybir.dt.bfloat16
F32R = mybir.dt.float32r

P = 128
T = 1024
TT = T // P
D = 256
KC = D // P
HALF = 512
NEG = -1.0e30

HEADS = 16
HD = 16
PAIRS = [(0, 0), (0, 1), (1, 0), (0, 2), (1, 1), (2, 0)]
PARTS = 3
ROWS = HD * len(PAIRS)
KROWS = ROWS + PARTS

EXPERTS = 64
INTER = 96
TOP = 8
GE = 4
GC = GE * INTER // P
GROUPS = EXPERTS // GE

ROUTES = 8

QR, KVR, DN, DR, DV = 96, 64, 128, 64, 128


class Core:

    def __init__(self, nc, ctx, dram):
        self.nc, self.ctx, self.dram = nc, ctx, dram
        self.sems = []
        self.x = self.sb("x", [P, TT, D], F32)
        self.xn = self.sb("xn", [P, TT, D], F32)
        self.xi = self.sb("xi", [P, TT, D], F32)
        self.xT = self.sb("xT", [P, KC, T], F32)
        self.ident = self.sb("ident", [P, P], F32)
        self.ident_h = self.sb("ident_h", [P, P], BF16)
        self.zero_h = self.sb("zero_h", [P, HALF], BF16)
        self.psum = ctx.enter_context(nc.psum_tensor("psum", [P, 8, HALF], F32))
        self.bank = [self.psum[:, i, :] for i in range(8)]

    def sb(self, name, shape, dt):
        return self.ctx.enter_context(self.nc.sbuf_tensor(name, shape, dt))

    def sem(self, name):
        self.sems.append(self.nc.alloc_semaphore(name))
        return self.sems[-1]

    def clear_semaphores(self):
        self.nc.clear_and_free_semaphores(self.sems)
        self.sems = []
        self.nc.all_engine_barrier()


def start(core):
    nc, dram = core.nc, core.dram
    loaded, const_made, turned, stored = (core.sem(f"start_{n}") for n in ("loaded", "const", "turned", "stored"))
    core.mask = {n: core.sb(f"m_{n}", [P, P], F32) for n in ("causal", "causalT", "prev", "prevT", "prev1", "prev1T", "sinkT")}
    core.mask_h = {n: core.sb(f"mh_{n}", [P, P], BF16) for n in core.mask}
    core.wup = core.sb("wup", [P, KC, D], F32)
    core.wdn = core.sb("wdn", [P, KC, D], F32)
    core.wex = core.sb("wex", [P, KC, D], F32)
    core.wrt = core.sb("wrt", [P, KC, ROUTES], F32)
    core.bqkv = core.sb("bqkv", [P, KC, 384], F32)
    core.bwo = core.sb("bwo", [P, KC, D], F32)
    core.row = {n: core.sb(f"row_{n}", [P, w], F32) for n, w in
            (("L1_attn_a_ln_w", D), ("L1_attn_a_ln_b", D), ("L1_attn_b_q_norm_w", QR), ("L1_attn_b_kv_norm_w", KVR))}
    with ExitStack() as ctx:
        raw = []
        plan = [("L1_ffn_W_up", core.wup, 0, D), ("L1_ffn_W_down", core.wdn, 0, D),
                ("L0_attn_b_Wq", core.bqkv, 0, D), ("L0_attn_b_Wk", core.bqkv, 256, 64),
                ("L0_attn_b_Wv", core.bqkv, 320, 64), ("L0_attn_b_Wo", core.bwo, 0, D),
                ("L1_ffn_W_gate", core.wrt, 0, ROUTES)]
        for name, dst, col, rows in plan:
            for r in range(0, rows, P):
                n = min(P, rows - r)
                t = ctx.enter_context(nc.sbuf_tensor(f"raw_{name}_{r}", [P, D], F32))
                raw.append((name, t, dst, col + r, r, n))
        block = ctx.enter_context(nc.Block())
        loads = len(raw) + 3 + len(core.mask) + len(core.row)

        @block.sync
        def _(sp):
            sp.dma_start(core.ident[:], dram["c_ident"]).then_inc(loaded, 16)
            for name, t, _, _, r, n in raw:
                sp.dma_start(t[0:n, :], dram[name][r:r + n, :]).then_inc(loaded, 16)
            for name in core.mask:
                sp.dma_start(core.mask[name][:], dram[f"c_{name}"]).then_inc(loaded, 16)
            for name, row in core.row.items():
                sp.dma_start(row[:], dram[name].unsqueeze(0).broadcast_to(list(row.shape))).then_inc(loaded, 16)
            sp.dma_start(core.wex[:], dram["L1_ffn_W_expert"].rearrange("(k p) n -> p k n", p=P)).then_inc(loaded, 16)
            sp.dma_start(core.x[:], dram["L0_attn_a_x"].rearrange("b (t p) d -> p (b t) d", p=P)).then_inc(loaded, 16)

        @block.gpsimd
        def _(pool):
            pool.memset(core.zero_h[:], 0.0)
            pool.wait_ge(loaded, 16 * loads)
            pool.tensor_copy(core.ident_h[:], core.ident[:])
            for name in core.mask:
                pool.tensor_copy(core.mask_h[name][:], core.mask[name][:])

        @block.tensor
        def _(pe):
            pe.wait_ge(loaded, 16 * loads)
            for i, (_, t, _, _, _, n) in enumerate(raw):
                if i >= 8:
                    pe.wait_ge(stored, i - 7)
                for k in range(KC):
                    last = nc.tensor.transpose(core.bank[i % 8][:, k * P:k * P + n],
                                               t[0:n, k * P:(k + 1) * P], core.ident[0:n, 0:n])
                last.then_inc(turned, 1)

        @block.vector
        def _(dve):
            for i, (_, _, dst, col, _, n) in enumerate(raw):
                dve.wait_ge(turned, i + 1)
                src = core.bank[i % 8][:, 0:KC * P].rearrange("p (k n) -> p k n", k=KC)
                nc.vector.tensor_copy(dst[:, :, col:col + n], src[:, :, 0:n]).then_inc(stored, 1)


def normalize(core, tag, src, dst, eps=1e-5, turn=True, affine=None, load=None):
    nc = core.nc
    stats_done, mv_done, var_ready, std_ready, rstd_done, scaled, normed, turned = (
        core.sem(f"{tag}_{n}") for n in ("stats", "mv", "var", "std", "rstd", "scaled", "normed", "turned"))
    with ExitStack() as ctx:
        stats = ctx.enter_context(nc.sbuf_tensor(f"{tag}_stats_b", [P, TT, 6], F32))
        mv = ctx.enter_context(nc.sbuf_tensor(f"{tag}_mv_b", [P, TT, 2], F32))
        var, std, rstd = (ctx.enter_context(nc.sbuf_tensor(f"{tag}_{n}_b", [P, TT], F32)) for n in ("var", "std", "rstd"))
        block = ctx.enter_context(nc.Block())

        if load is not None:
            @block.sync
            def _(sp):
                load(sp)

        @block.vector
        def _(dve):
            for t in range(TT):
                nc.vector.bn_stats(stats[:, t, :], src[:, t, :]).then_inc(stats_done, 1)
            for t in range(TT):
                dve.wait_ge(stats_done, t + 1)
                nc.vector.bn_aggr(mv[:, t, :], stats[:, t, :]).then_inc(mv_done, 1)
            dve.wait_ge(mv_done, TT)
            nc.vector.tensor_scalar(var[:], mv[:, :, 1], eps, None, ALU.add).then_inc(var_ready, 1)
            dve.wait_ge(std_ready, 1)
            nc.vector.reciprocal(rstd[:], std[:]).then_inc(rstd_done, 1)
            dve.wait_ge(rstd_done, 1)
            n_scaled = 0
            for t in range(TT):
                last = nc.vector.tensor_scalar(dst[:, t, :], src[:, t, :], mv[:, t, 0:1], rstd[:, t:t + 1],
                                               ALU.subtract, ALU.mult)
                if affine is not None:
                    for row, op in zip(affine, (ALU.mult, ALU.add)):
                        last.then_inc(scaled, 1)
                        n_scaled += 1
                        dve.wait_ge(scaled, n_scaled)
                        last = nc.vector.tensor_tensor(dst[:, t, :], dst[:, t, :], row[:], op)
                last.then_inc(normed, 1)
            if turn:
                for h in range(2):
                    dve.wait_ge(turned, 4 * h + 4)
                    nc.vector.tensor_copy(core.xT[:, 1, h * HALF:(h + 1) * HALF], core.bank[2 * h + 1][:])

        @block.scalar
        def _(act):
            act.wait_ge(var_ready, 1)
            nc.scalar.activation(std[:], var[:], ACT.Sqrt).then_inc(std_ready, 1)
            if turn:
                for h in range(2):
                    act.wait_ge(turned, 4 * h + 4)
                    nc.scalar.copy(core.xT[:, 0, h * HALF:(h + 1) * HALF], core.bank[2 * h][:])

        if turn:
            @block.tensor
            def _(pe):
                for t in range(TT):
                    pe.wait_ge(normed, t + 1)
                    for k in range(KC):
                        last = nc.tensor.transpose(core.bank[2 * (t // 4) + k][:, (t % 4) * P:(t % 4 + 1) * P],
                                                   dst[:, t, k * P:(k + 1) * P], core.ident[:])
                    last.then_inc(turned, 1)


def ffn(core, tag):
    nc = core.nc
    up_ready, up_stored, out_ready, logits_ready, sorted_, diff, exped, step, added = (
        core.sem(f"{tag}_{n}") for n in ("up", "ups", "out", "lg", "sort", "diff", "exp", "step", "added"))
    with ExitStack() as ctx:
        hT = ctx.enter_context(nc.sbuf_tensor(f"{tag}_hT", [P, KC, T], F32))
        top = ctx.enter_context(nc.sbuf_tensor(f"{tag}_top", [P, TT, ROUTES], F32))
        d21 = ctx.enter_context(nc.sbuf_tensor(f"{tag}_d21", [P, TT], F32))
        e21 = ctx.enter_context(nc.sbuf_tensor(f"{tag}_e21", [P, TT], F32))
        den = ctx.enter_context(nc.sbuf_tensor(f"{tag}_den", [P, TT], F32))
        w1 = ctx.enter_context(nc.sbuf_tensor(f"{tag}_w1", [P, TT], F32))
        w2 = ctx.enter_context(nc.sbuf_tensor(f"{tag}_w2", [P, TT], F32))
        wsum = ctx.enter_context(nc.sbuf_tensor(f"{tag}_wsum", [P, TT], F32))
        block = ctx.enter_context(nc.Block())
        lg = core.bank[7]

        @block.tensor
        def _(pe):
            for t in range(TT):
                for k in range(KC):
                    last = nc.tensor.matmul(lg[:, t * ROUTES:(t + 1) * ROUTES], core.xT[:, k, t * P:(t + 1) * P],
                                            core.wrt[:, k, :], start=(k == 0), stop=(k == KC - 1))
            last.then_inc(logits_ready, 1)
            for u in range(4):
                m, h = u % 2, u // 2
                for k in range(KC):
                    last = nc.tensor.matmul(core.bank[u][:], core.wup[:, k, m * P:(m + 1) * P],
                                            core.xT[:, k, h * HALF:(h + 1) * HALF], start=(k == 0), stop=(k == KC - 1))
                last.then_inc(up_ready, 1)
            for t in range(TT):
                pe.wait_ge(up_stored, 2 * (t // 4) + 2)
                b = 4 + t % 3
                if t >= 3:
                    pe.wait_ge(added, t - 2)
                for k in range(KC):
                    nc.tensor.matmul(core.bank[b][:, 0:D], hT[:, k, t * P:(t + 1) * P], core.wdn[:, k, :],
                                     start=(k == 0), stop=(k == KC - 1))
                for k in range(KC):
                    last = nc.tensor.matmul(core.bank[b][:, D:2 * D], core.xT[:, k, t * P:(t + 1) * P],
                                            core.wex[:, k, :], start=(k == 0), stop=(k == KC - 1))
                last.then_inc(out_ready, 1)

        @block.scalar
        def _(act):
            act.wait_ge(diff, 1)
            nc.scalar.activation(e21[:], d21[:], ACT.Exp).then_inc(exped, 1)
            for u in range(4):
                m, h = u % 2, u // 2
                act.wait_ge(up_ready, u + 1)
                nc.scalar.activation(hT[:, m, h * HALF:(h + 1) * HALF], core.bank[u][:], ACT.Relu).then_inc(up_stored, 1)

        @block.vector
        def _(dve):
            dve.wait_ge(logits_ready, 1)
            for t in range(TT):
                nc.vector.max(top[:, t, :], lg[:, t * ROUTES:(t + 1) * ROUTES]).then_inc(sorted_, 1)
            dve.wait_ge(sorted_, TT)
            nc.vector.tensor_tensor(d21[:], top[:, :, 1], top[:, :, 0], ALU.subtract).then_inc(diff, 1)
            dve.wait_ge(exped, 1)
            nc.vector.tensor_scalar(den[:], e21[:], 1.0, None, ALU.add).then_inc(step, 1)
            dve.wait_ge(step, 1)
            nc.vector.reciprocal(w1[:], den[:]).then_inc(step, 1)
            dve.wait_ge(step, 2)
            nc.vector.tensor_tensor(w2[:], e21[:], w1[:], ALU.mult).then_inc(step, 1)
            dve.wait_ge(step, 3)
            nc.vector.tensor_tensor(wsum[:], w1[:], w2[:], ALU.add).then_inc(step, 1)
            dve.wait_ge(step, 4)
            for t in range(TT):
                b = 4 + t % 3
                dve.wait_ge(out_ready, t + 1)
                nc.vector.tensor_tensor(core.x[:, t, :], core.x[:, t, :], core.bank[b][:, 0:D], ALU.add).then_inc(step, 1)
                dve.wait_ge(step, 5 + t)
                nc.vector.scalar_tensor_tensor(out=core.x[:, t, :], in0=core.bank[b][:, D:2 * D],
                                               scalar=wsum[:, t:t + 1], in1=core.x[:, t, :],
                                               op0=ALU.mult, op1=ALU.add).then_inc(added, 1)


def finish(core):
    nc = core.nc
    out_stored = core.sem("out_stored")
    with nc.Block() as block:
        @block.sync
        def _(sp):
            sp.dma_start(core.dram["out"].rearrange("b (t p) d -> p (b t) d", p=P), core.x[:]).then_inc(out_stored, 16)
            sp.wait_ge(out_stored, 16)


def moe(core, tag, norm):
    with ExitStack() as ctx:
        parts = ExpertParts(core, ctx, tag)
        routing_weights(core, tag, norm, parts)
        experts(core, tag, parts)


class ExpertParts:
    PIECES = 6
    COLS = GE * INTER
    LOADS = 2 * KC + 1

    def __init__(self, core, ctx, tag):
        nc, self.dram = core.nc, core.dram
        self.loaded = [core.sem(f"{tag}_wld{n}") for n in range(self.LOADS)]
        self.high_made, self.low_made = core.sem(f"{tag}_whi"), core.sem(f"{tag}_wlo")
        self.x_high_made, self.x_low_made = core.sem(f"{tag}_xhi"), core.sem(f"{tag}_xlo")

        def sb(name, shape, dt=F32R):
            return ctx.enter_context(nc.sbuf_tensor(f"{tag}_{name}", shape, dt))

        self.raw = sb("w_raw", [P, self.PIECES, self.COLS], F32)
        self.w = [sb("w_hi", [P, 2, self.PIECES, self.COLS]), sb("w_lo", [P, 2, self.PIECES, self.COLS])]
        self.x = [sb("x_hi", [P, KC, T]), sb("x_lo", [P, KC, T])]

    def up_or_gate(self, part, s, which, k, j):
        return self.w[part][:, s, KC * which + k, j * P:(j + 1) * P]

    def down(self, part, s, j, m):
        flat = self.w[part][:, s, 2 * KC:, :].rearrange("p a c -> p (a c)")
        return flat[:, j * D + m * P:j * D + (m + 1) * P]

    def load(self, sp, g, n):
        if n < 2 * KC:
            name, k = ("L0_ffn_w_gate", "L0_ffn_w_up")[n // KC], n % KC
            src = self.dram[name].rearrange("e (k p) i -> k p e i", p=P)[k]
            sp.dma_start(self.raw[:, n, :].rearrange("p (e i) -> p e i", e=GE),
                         src[:, bass.ds(g * GE, GE), :]).then_inc(self.loaded[n], 16)
        else:
            src = self.dram["L0_ffn_w_down"].rearrange("e i n -> (e i) n").rearrange("(j p) n -> p j n", p=P)
            dst = self.raw[:, 2 * KC:, :].rearrange("p a c -> p (a c)").rearrange("p (j n) -> p j n", n=D)
            sp.dma_start(dst, src[:, bass.ds(g * GC, GC), :]).then_inc(self.loaded[n], 16)


def routing_weights(core, tag, norm, parts):
    nc = core.nc
    logits_ready, copied, max_ready, exped, recip_ready, probs_ready, top_ready, replaced = (
        core.sem(f"{tag}_{n}") for n in ("lg", "lgc", "max", "exp", "rec", "prob", "top", "repl"))
    sum_ready, scale_ready, kept, weighted, gate_loaded, turned, rows_copied, rows_stored = (
        core.sem(f"{tag}_{n}") for n in ("sum", "scale", "kept", "wtd", "gate", "turned", "rows", "rst"))
    core.rw_dram = nc.dram_tensor(f"{tag}_rw_dram", (EXPERTS, T), F32, kind="Internal").ap()
    with ExitStack() as ctx:
        def sb(name, shape):
            return ctx.enter_context(nc.sbuf_tensor(f"{tag}_{name}", shape, F32))

        wr = sb("wr", [P, KC, EXPERTS])
        lg = sb("lg_b", [P, TT, EXPERTS])
        probs = sb("probs", [P, TT, EXPERTS])
        repl = sb("repl_b", [P, TT, EXPERTS])
        top = sb("top_b", [P, TT, TOP])
        big, total, rtotal, tsum, rtsum = (sb(n, [P, TT]) for n in ("big", "total", "rtotal", "tsum", "rtsum"))
        rwT = sb("rwT", [EXPERTS, T])

        def load(sp):
            sp.dma_start(wr[:], core.dram["L0_ffn_gate_w"].rearrange("(k p) e -> p k e", p=P)).then_inc(gate_loaded, 16)
            for n in range(parts.LOADS):
                parts.load(sp, 0, n)

        norm(load)
        block = ctx.enter_context(nc.Block())

        @block.sync
        def _(sp):
            for n in range(parts.LOADS):
                sp.wait_ge(parts.low_made, n + 1 if n < 2 * KC else parts.PIECES)
                parts.load(sp, 1, n)
            sp.wait_ge(rows_copied, 2)
            sp.dma_start(core.rw_dram, rwT[:]).then_inc(rows_stored, 16)
            sp.wait_ge(rows_stored, 16)

        @block.tensor
        def _(pe):
            pe.wait_ge(gate_loaded, 16)
            for t in range(TT):
                for k in range(KC):
                    last = nc.tensor.matmul(core.bank[0][:, t * EXPERTS:(t + 1) * EXPERTS],
                                            core.xT[:, k, t * P:(t + 1) * P], wr[:, k, :],
                                            start=(k == 0), stop=(k == KC - 1))
            last.then_inc(logits_ready, 1)
            pe.wait_ge(weighted, 1)
            for t in range(TT):
                last = nc.tensor.transpose(core.bank[1 + t // 4][0:EXPERTS, (t % 4) * P:(t % 4 + 1) * P],
                                           probs[:, t, :], core.ident[:])
            last.then_inc(turned, 1)

        @block.scalar
        def _(act):
            for k in range(KC):
                nc.scalar.copy(parts.x[0][:, k, :], core.xT[:, k, :]).then_inc(parts.x_high_made, 1)
            act.wait_ge(max_ready, 1)
            nc.scalar.activation(lg[:], lg[:], ACT.Exp).then_inc(exped, 1)
            for p in range(parts.PIECES):
                act.wait_ge(parts.loaded[min(p, 2 * KC)], 16)
                nc.scalar.copy(parts.w[0][:, 0, p, :], parts.raw[:, p, :]).then_inc(parts.high_made, 1)
            act.wait_ge(turned, 1)
            nc.scalar.copy(rwT[:, 0:HALF], core.bank[1][0:EXPERTS, :]).then_inc(rows_copied, 1)

        @block.gpsimd
        def _(pool):
            for k in range(KC):
                pool.wait_ge(parts.x_high_made, k + 1)
                nc.gpsimd.tensor_tensor(parts.x[1][:, k, :], core.xT[:, k, :], parts.x[0][:, k, :],
                                        ALU.subtract).then_inc(parts.x_low_made, 1)
                pool.wait_ge(parts.x_low_made, k + 1)
            for p in range(parts.PIECES):
                pool.wait_ge(parts.high_made, p + 1)
                nc.gpsimd.tensor_tensor(parts.w[1][:, 0, p, :], parts.raw[:, p, :], parts.w[0][:, 0, p, :],
                                        ALU.subtract).then_inc(parts.low_made, 1)
                pool.wait_ge(parts.low_made, p + 1)

        @block.vector
        def _(dve):
            def rows(v):
                return v[:].unsqueeze(2).broadcast_to([P, TT, EXPERTS])

            dve.wait_ge(logits_ready, 1)
            raw = core.bank[0][:].rearrange("p (t e) -> p t e", e=EXPERTS)
            nc.vector.tensor_reduce(big[:], raw, AX_X, ALU.max).then_inc(copied, 1)
            dve.wait_ge(copied, 1)
            nc.vector.tensor_tensor(lg[:], raw, rows(big), ALU.subtract).then_inc(max_ready, 1)
            dve.wait_ge(exped, 1)
            nc.vector.tensor_reduce(total[:], lg[:], AX_X, ALU.add).then_inc(recip_ready, 1)
            dve.wait_ge(recip_ready, 1)
            nc.vector.reciprocal(rtotal[:], total[:]).then_inc(recip_ready, 1)
            dve.wait_ge(recip_ready, 2)
            nc.vector.tensor_tensor(probs[:], lg[:], rows(rtotal), ALU.mult).then_inc(probs_ready, 1)
            dve.wait_ge(probs_ready, 1)
            for t in range(TT):
                nc.vector.max(top[:, t, :], probs[:, t, :]).then_inc(top_ready, 1)
            for t in range(TT):
                dve.wait_ge(top_ready, t + 1)
                nc.vector.match_replace(repl[:, t, :], top[:, t, :], probs[:, t, :], -1.0).then_inc(replaced, 1)
            nc.vector.tensor_reduce(tsum[:], top[:], AX_X, ALU.add).then_inc(sum_ready, 1)
            dve.wait_ge(sum_ready, 1)
            nc.vector.reciprocal(rtsum[:], tsum[:]).then_inc(scale_ready, 1)
            dve.wait_ge(replaced, TT)
            nc.vector.tensor_scalar(repl[:], repl[:], 0.0, None, ALU.max).then_inc(kept, 1)
            dve.wait_ge(kept, 1)
            nc.vector.tensor_tensor(probs[:], probs[:], repl[:], ALU.subtract).then_inc(kept, 1)
            dve.wait_ge(kept, 2)
            dve.wait_ge(scale_ready, 1)
            nc.vector.tensor_tensor(probs[:], probs[:], rows(rtsum), ALU.mult).then_inc(weighted, 1)
            dve.wait_ge(turned, 1)
            nc.vector.tensor_copy(rwT[:, HALF:T], core.bank[2][0:EXPERTS, :]).then_inc(rows_copied, 1)


def experts(core, tag, parts):
    nc = core.nc
    UNITS = 2 * GC
    assert UNITS == parts.PIECES
    BODY = 2 * UNITS
    TURNS = GROUPS // 2
    LAG = 2
    PASSES = [(0, 0), (0, 1), (1, 0)]
    r_loaded = [core.sem(f"{tag}_rld{s}") for s in range(2)]
    gu_ready, silu_done, weighted, inner_ready, high_made, low_made, down_done, summed, sum_copied, turned, added = (
        core.sem(f"{tag}_{n}") for n in ("gu", "silu", "w2", "inner", "hi", "lo", "down", "summed", "scp", "st", "sadd"))
    spans = []
    for j in range(GC):
        for e in range(GE):
            a, b = max(j * P, e * INTER), min((j + 1) * P, (e + 1) * INTER)
            if a < b:
                spans.append((j, e, a - j * P, b - j * P))
    with ExitStack() as ctx:
        def sb(name, shape, dt=F32):
            return ctx.enter_context(nc.sbuf_tensor(f"{tag}_{name}", shape, dt))

        rw = sb("rw", [P, 2, GC, T])
        silu, wsilu, inner = (sb(n, [P, 2, HALF]) for n in ("silu_b", "wsilu", "inner_b"))
        inner_parts = [sb("inner_hi", [P, 3, HALF], F32R), sb("inner_lo", [P, 3, HALF], F32R)]
        oT = sb("oT", [P, KC, T])
        block = ctx.enter_context(nc.Block())
        gbank, ubank, obank = core.bank[0:2], core.bank[2:4], core.bank[4:8]

        def unit(i, u):
            return BODY * i + u

        def early(i, u, n):
            return isinstance(i, int) and unit(i, u) < n

        @block.sync
        def _(sp):
            def load_rows(g, s):
                for j, e, a, b in spans:
                    sp.dma_start(rw[a:b, s, j, :],
                                 core.rw_dram[bass.ds(g * GE + e, 1), :].broadcast_to([b - a, T])).then_inc(r_loaded[s], 16)

            def load_weights(g):
                for n in range(parts.LOADS):
                    sp.wait_ge(parts.low_made, UNITS * (g - 1) + (n + 1 if n < 2 * KC else UNITS))
                    parts.load(sp, g, n)

            for s in range(2):
                load_rows(s, s)
            with sp.Fori(1, TURNS) as i:
                for s in range(2):
                    load_weights(2 * i + s)
                    sp.wait_ge(weighted, BODY * i + UNITS * (s - 1))
                    load_rows(2 * i + s, s)

        @block.tensor
        def _(pe):
            def gate_up(i, u):
                s, j, h = u // UNITS, u % UNITS // 2, u % 2
                if h == 0 and j == 0:
                    pe.wait_ge(parts.low_made, unit(i, u) + 2 * KC)
                    pe.wait_ge(parts.high_made, unit(i, u) + 2 * KC)
                if not early(i, u, 2):
                    pe.wait_ge(inner_ready, unit(i, u) - 1)
                for which, bank in ((0, gbank), (1, ubank)):
                    steps = [(k, a, b) for k in range(KC) for a, b in PASSES]
                    for n, (k, a, b) in enumerate(steps):
                        last = nc.tensor.matmul(bank[u % 2][:], parts.up_or_gate(a, s, which, k, j),
                                                parts.x[b][:, k, h * HALF:(h + 1) * HALF],
                                                start=(n == 0), stop=(n == len(steps) - 1))
                last.then_inc(gu_ready, 1)

            def down(i, u):
                s, j, h = u // UNITS % 2, u % UNITS // 2, u % 2
                if h == 0 and j == 0:
                    pe.wait_ge(parts.low_made, unit(i, u) + UNITS)
                    pe.wait_ge(parts.high_made, unit(i, u) + UNITS)
                pe.wait_ge(low_made, unit(i, u) + 1)
                pe.wait_ge(high_made, unit(i, u) + 1)
                for m in range(KC):
                    for a, b in PASSES:
                        last = nc.tensor.matmul(obank[2 * h + m][:], parts.down(a, s, j, m), inner_parts[b][:, u % 3, :],
                                                start=False, stop=False, skip_group_check=True)
                last.then_inc(down_done, 1)

            def turn(i):
                for u in range(BODY):
                    gate_up(i, u)
                    if not early(i, u, LAG):
                        down(i, u - LAG)

            for b in range(4):
                nc.tensor.matmul(obank[b][:], core.zero_h[:, 0:P], core.zero_h[:], start=True, stop=False,
                                 skip_group_check=True)
            turn(0)
            with pe.Fori(1, TURNS) as i:
                turn(i)
            for u in range(BODY - LAG, BODY):
                down(TURNS - 1, u)
            for b in range(4):
                last = nc.tensor.matmul(obank[b][:], core.zero_h[:, 0:P], core.zero_h[:], start=False, stop=True,
                                        skip_group_check=True)
            last.then_inc(summed, 1)
            for t in range(TT):
                pe.wait_ge(sum_copied, 2 * (t // 4) + 2)
                if t >= 4:
                    pe.wait_ge(added, t - 3)
                for m in range(KC):
                    last = nc.tensor.transpose(core.bank[t % 4][:, m * P:(m + 1) * P], oT[:, m, t * P:(t + 1) * P],
                                               core.ident[:])
                last.then_inc(turned, 1)

        @block.scalar
        def _(act):
            def high_weights(i, u):
                s, p = u // UNITS, u % UNITS
                act.wait_ge(parts.loaded[min(p, 2 * KC)], 16 * (2 * i + s + 2))
                if p == 0:
                    if not early(i, u, UNITS):
                        act.wait_ge(down_done, unit(i, u))
                nc.scalar.copy(parts.w[0][:, 1 - s, p, :], parts.raw[:, p, :]).then_inc(parts.high_made, 1)

            def high_inner(i, u):
                act.wait_ge(inner_ready, unit(i, u) + 1)
                if not early(i, u, 3):
                    act.wait_ge(down_done, unit(i, u) - 2)
                nc.scalar.copy(inner_parts[0][:, u % 3, :], inner[:, u % 2, :]).then_inc(high_made, 1)

            def turn(i, final=False):
                for u in range(BODY):
                    act.wait_ge(gu_ready, unit(i, u) + 1)
                    if not early(i, u, 2):
                        act.wait_ge(weighted, unit(i, u) - 1)
                    nc.scalar.activation(silu[:, u % 2, :], gbank[u % 2][:], ACT.Silu).then_inc(silu_done, 1)
                    if not early(i, u, 1):
                        high_inner(i, u - 1)
                    if not (final and u >= UNITS):
                        high_weights(i, u)

            turn(0)
            with act.Fori(1, TURNS - 1) as i:
                turn(i)
            turn(TURNS - 1, final=True)
            high_inner(TURNS - 1, BODY - 1)
            act.wait_ge(summed, 1)
            for b in range(4):
                h, m = b // 2, b % 2
                nc.scalar.copy(oT[:, m, h * HALF:(h + 1) * HALF], obank[b][:]).then_inc(sum_copied, 1)

        @block.gpsimd
        def _(pool):
            def turn(i, final=False):
                for u in range(BODY):
                    s, j, h = u // UNITS, u % UNITS // 2, u % 2
                    if h == 0 and j == 0:
                        pool.wait_ge(r_loaded[s], 16 * len(spans) * (i + 1))
                    pool.wait_ge(silu_done, unit(i, u) + 1)
                    if not early(i, u, 2):
                        pool.wait_ge(inner_ready, unit(i, u) - 1)
                    nc.gpsimd.tensor_tensor(wsilu[:, u % 2, :], silu[:, u % 2, :],
                                            rw[:, s, j, h * HALF:(h + 1) * HALF], ALU.mult).then_inc(weighted, 1)
                    if final and u >= UNITS:
                        continue
                    p = u % UNITS
                    pool.wait_ge(weighted, unit(i, u) + 1)
                    pool.wait_ge(parts.high_made, unit(i, u) + UNITS + 1)
                    nc.gpsimd.tensor_tensor(parts.w[1][:, 1 - s, p, :], parts.raw[:, p, :], parts.w[0][:, 1 - s, p, :],
                                            ALU.subtract).then_inc(parts.low_made, 1)

            turn(0)
            with pool.Fori(1, TURNS - 1) as i:
                turn(i)
            turn(TURNS - 1, final=True)

        @block.vector
        def _(dve):
            def low_inner(i, u):
                dve.wait_ge(high_made, unit(i, u) + 1)
                nc.vector.tensor_tensor(inner_parts[1][:, u % 3, :], inner[:, u % 2, :], inner_parts[0][:, u % 3, :],
                                        ALU.subtract).then_inc(low_made, 1)

            def turn(i):
                for u in range(BODY):
                    if not early(i, u, 1):
                        low_inner(i, u - 1)
                    dve.wait_ge(weighted, unit(i, u) + 1)
                    if not early(i, u, 2):
                        dve.wait_ge(high_made, unit(i, u) - 1)
                        dve.wait_ge(low_made, unit(i, u) - 1)
                    nc.vector.tensor_tensor(inner[:, u % 2, :], ubank[u % 2][:], wsilu[:, u % 2, :],
                                            ALU.mult).then_inc(inner_ready, 1)

            turn(0)
            with dve.Fori(1, TURNS) as i:
                turn(i)
            low_inner(TURNS - 1, BODY - 1)
            for t in range(TT):
                dve.wait_ge(turned, t + 1)
                nc.vector.tensor_tensor(core.x[:, t, :], core.x[:, t, :], core.bank[t % 4][:, 0:D], ALU.add).then_inc(added, 1)


class Attention:

    def __init__(self, kv_heads, rotation, maxima, halves):
        self.kv_heads, self.rotation, self.maxima = kv_heads, rotation, maxima
        self.units = [u for half in halves for u in half]
        self.quads = []
        at = 0
        for h, half in enumerate(halves):
            for i in range(0, len(half), 4):
                n = min(4, len(half) - i)
                self.quads.append((h, list(range(at, at + n)), i == 0, i + n == len(half)))
                at += n
        self.qk_heads = HEADS + kv_heads
        self.width = (HEADS + 2 * kv_heads) * HD
        self.k_chunks = -(-kv_heads * HD // P)
        self.chunks = HEADS * HD // P + self.k_chunks


def _blocks_seen():
    maxima = [[(k, min(HALF, (t + 1) * P - k), None) for k in range(0, (t + 1) * P, HALF)] for t in range(TT)]
    units = [[(s, max(q, s), q + HALF - max(q, s), []) for s in range(0, q + HALF, P)] for q in (0, HALF)]
    return maxima, units


def _window_seen(sink=4):
    maxima = [[(0, P, "causal")], [(0, P, "prev1"), (P, P, "causal")]]
    maxima += [[(0, sink, None), ((t - 1) * P, P, "prev"), (t * P, P, "causal")] for t in range(2, TT)]
    units = []
    for q in (0, HALF):
        these = []
        for s in range(max(0, q - P), q + HALF, P):
            seen = [(x, m) for x, m in ((s, "causalT"), (s + P, "prev1T" if s == 0 else "prevT")) if q <= x < q + HALF]
            these.append((s, seen[0][0], P * len(seen), [(x - seen[0][0], m) for x, m in seen]))
        q0 = max(q, 2 * P)
        these.append((0, q0, q + HALF - q0, [(c, "sinkT") for c in range(0, q + HALF - q0, P)]))
        units.append(these)
    return maxima, units


def _all_seen():
    maxima = [[(0, HALF, None), (HALF, HALF, None)] for _ in range(TT)]
    units = [[(s * P, q, HALF, []) for s in range(TT)] for q in (0, HALF)]
    return maxima, units


ATT_A = Attention(4, "halves", *_blocks_seen())
ATT_B = Attention(4, None, *_window_seen())
ATT_C = Attention(16, "pairs", *_all_seen())


def attention(core, tag, cfg, norm):
    with ExitStack() as ctx:
        def sb(name, shape, dt):
            return ctx.enter_context(core.nc.sbuf_tensor(f"{tag}_{name}", shape, dt))

        v = sb("v", [P, TT, cfg.kv_heads, HD + 1], F32)
        qs = sb("qs", [KROWS, HEADS, T], BF16)
        ks = sb("ks", [KROWS, cfg.kv_heads, T], BF16)
        ctxs = sb("ctxs", [P, TT, HEADS * HD], F32)
        wo = core.bwo if tag == "b" else sb("wo", [P, KC, D], F32)
        stacked = [core.sem(f"{tag}_stk{c}") for c in range(HEADS * HD // P)]
        wo_loaded = core.sem(f"{tag}_wol")
        part = sb("part", [P, PARTS, cfg.chunks, T], BF16)
        more_stacks = project_and_stack(core, tag, cfg, norm, v, qs, ks, part, wo, stacked, wo_loaded)
        attend(core, tag, cfg, v, qs, ks, ctxs, stacked, more_stacks)
        project_out(core, tag, ctxs, wo, wo_loaded, extra=core.xn if tag == "c" else None)


def stacks_of_chunk(cfg, c):
    return len(PAIRS) * (2 if c < cfg.k_chunks else 1)


def project_and_stack(core, tag, cfg, norm, v, qs, ks, part, wo, stacked, wo_loaded):
    nc, dram = core.nc, core.dram
    NQK = cfg.qk_heads * HD
    w_loaded, projected, copied, v_copied, rot, roped, turned = (
        core.sem(f"{tag}_{n}") for n in ("wl", "proj", "cp", "vcp", "rot", "roped", "tqk"))
    ones_made, part1, rest1, part2, part3, parts_stored = (
        core.sem(f"{tag}_{n}") for n in ("ones", "p1", "r1", "p2", "p3", "pst"))
    C = cfg.chunks
    parts_dram = nc.dram_tensor(f"{tag}_parts_dram", (PARTS, C, P, T), BF16, kind="Internal").ap()
    rows_of = [P if (j + 1) * P <= NQK else NQK - j * P for j in range(C)]
    QC = HEADS * HD // P
    chunk_order = [j for c in range(QC) for j in ([c, QC + c] if c < cfg.k_chunks else [c])]
    units = [(h, j) for j in chunk_order for h in range(2)]
    rope = cfg.rotation is not None
    if not rope:
        roped = copied
    with ExitStack() as ctx:
        def sb(name, shape, dt=F32):
            return ctx.enter_context(nc.sbuf_tensor(f"{tag}_{name}", shape, dt))

        qk = sb("qk", [P, TT, cfg.qk_heads, HD])
        rest = sb("rest", [P, 3, HALF])
        if tag == "b":
            w, loads = core.bqkv, []
        else:
            w = sb("wqkv", [P, KC, cfg.width])
            if tag == "a":
                loads = [(w[:, :, 0:256], "L0_attn_a_Wq"), (w[:, :, 256:320], "L0_attn_a_Wk"), (w[:, :, 320:384], "L0_attn_a_Wv")]
            else:
                loads = [(w[:], "L1_attn_a_W_in")]
        if rope:
            cos, sin = sb("cos", [P, TT, HD]), sb("sin", [P, TT, HD])
            turned_qk = sb("turned_qk", [P, 2, cfg.qk_heads, HD])
        n_loads = len(loads) + 2 * rope

        def load(sp):
            for dst, name in loads:
                sp.dma_start(dst, dram[name].rearrange("(k p) n -> p k n", p=P)).then_inc(w_loaded, 16)
            if rope:
                for dst, name in ((cos, f"c_cos_{tag}"), (sin, f"c_sin_{tag}")):
                    sp.dma_start(dst[:], dram[name].rearrange("(t p) d -> p t d", p=P)).then_inc(w_loaded, 16)
            if tag != "b":
                name = {"a": "L0_attn_a_Wo", "c": "L1_attn_a_W_out"}[tag]
                sp.dma_start(wo[:], dram[name].rearrange("(k p) n -> p k n", p=P)).then_inc(wo_loaded, 16)

        norm(load)
        block = ctx.enter_context(nc.Block())

        def stack(sp, some):
            for n, (h, j) in some:
                sp.wait_ge(part3, n + 1)
                sp.wait_ge(part2, n + 1)
                sp.wait_ge(part1, n + 1)
                sp.dma_start(parts_dram[:, j, 0:rows_of[j], h * HALF:(h + 1) * HALF].rearrange("a p t -> p a t"),
                             part[0:rows_of[j], :, j, h * HALF:(h + 1) * HALF]).then_inc(parts_stored, 16)
                c = j - QC if j >= QC else j
                if h == 0 or (j < QC and c < cfg.k_chunks):
                    continue
                sp.wait_ge(parts_stored, 16 * (n + 1))
                for g, (pq, pk) in enumerate(PAIRS):
                    todo = [(qs, pq, c)]
                    if c < cfg.k_chunks:
                        todo.append((ks, pk, QC + c))
                    for dst, which, i in todo:
                        heads = rows_of[i] // HD
                        h0 = 8 * c
                        sp.dma_start(dst[g * HD:(g + 1) * HD, h0:h0 + heads, :],
                                     parts_dram[which, i, 0:rows_of[i], :].rearrange("(h d) t -> d h t", d=HD)
                                     ).then_inc(stacked[c], 16)

        numbered = list(enumerate(units))
        first = 4

        @block.sync
        def _(sp):
            stack(sp, numbered[:first])

        @block.tensor
        def _(pe):
            if n_loads:
                pe.wait_ge(w_loaded, 16 * n_loads)
            for t in range(TT):
                if t >= 2:
                    pe.wait_ge(copied, t - 1)
                    pe.wait_ge(v_copied, t - 1)
                for n0, b in ([(0, 0)] if cfg.width <= HALF else [(0, 0), (HALF, 1)]):
                    n = min(HALF, cfg.width - n0)
                    for k in range(KC):
                        last = nc.tensor.matmul(core.bank[2 * (t % 2) + b][:, 0:n], core.xT[:, k, t * P:(t + 1) * P],
                                                w[:, k, n0:n0 + n], start=(k == 0), stop=(k == KC - 1))
                last.then_inc(projected, 1)
            for n, (h, j) in enumerate(units):
                pe.wait_ge(roped, 4 * h + 4)
                if n >= 4:
                    pe.wait_ge(rest1, n - 3)
                for t in range(4 * h, 4 * h + 4):
                    flat = qk[:, t, :, :].rearrange("p h d -> p (h d)")
                    last = nc.tensor.transpose(core.bank[4 + n % 4][0:rows_of[j], (t % 4) * P:(t % 4 + 1) * P],
                                               flat[:, j * P:j * P + rows_of[j]], core.ident[:])
                last.then_inc(turned, 1)

        @block.scalar
        def _(act):
            for t in range(TT):
                act.wait_ge(projected, t + 1)
                nc.scalar.copy(qk[:, t, :, :].rearrange("p h d -> p (h d)"),
                               core.bank[2 * (t % 2)][:, 0:NQK]).then_inc(copied, 1)
            for n in range(len(units) + 1):
                if n < len(units):
                    h, j = units[n]
                    act.wait_ge(turned, n + 1)
                    nc.scalar.copy(part[0:rows_of[j], 0, j, h * HALF:(h + 1) * HALF],
                                   core.bank[4 + n % 4][0:rows_of[j], :]).then_inc(part1, 1)
                if n >= 1:
                    h, j = units[n - 1]
                    act.wait_ge(rest1, n)
                    nc.scalar.copy(part[0:rows_of[j], 1, j, h * HALF:(h + 1) * HALF],
                                   rest[0:rows_of[j], (n - 1) % 3, :]).then_inc(part2, 1)

        @block.vector
        def _(dve):
            for t in range(TT):
                dve.wait_ge(projected, t + 1)
                dve.wait_ge(copied, t + 1)
                b, c0 = (2 * (t % 2), NQK) if cfg.width <= HALF else (2 * (t % 2) + 1, 0)
                nc.vector.tensor_copy(v[:, t, :, 0:HD],
                                      core.bank[b][:, c0:c0 + cfg.kv_heads * HD].rearrange("p (h d) -> p h d", d=HD)
                                      ).then_inc(v_copied, 1)
                if not rope:
                    continue
                tq = turned_qk[:, t % 2, :, :]

                def over_heads(table, a, step, n):
                    return table[:, t, a:a + step * (n - 1) + 1:step].unsqueeze(1).broadcast_to([P, cfg.qk_heads, n])

                if cfg.rotation == "halves":
                    moves, step, n_rot = [(0, HD // 2), (HD // 2, 0)], 1, HD // 2
                else:
                    moves, step, n_rot = [(0, 1), (1, 0)], 2, HD // 4
                for to, frm in moves:
                    e = step * (n_rot - 1) + 1
                    nc.vector.tensor_tensor(tq[:, :, to:to + e:step], qk[:, t, :, frm:frm + e:step],
                                            over_heads(sin, to, step, n_rot), ALU.mult).then_inc(rot, 1)
                dve.wait_ge(rot, 3 * t + 2)
                nc.vector.tensor_tensor(qk[:, t, :, :], qk[:, t, :, :], over_heads(cos, 0, 1, HD), ALU.mult).then_inc(rot, 1)
                dve.wait_ge(rot, 3 * t + 3)
                rotated = HD if cfg.rotation == "halves" else HD // 2
                nc.vector.tensor_tensor(qk[:, t, :, 0:rotated], qk[:, t, :, 0:rotated], tq[:, :, 0:rotated],
                                        ALU.add).then_inc(roped, 1)
            for n, (h, j) in enumerate(units):
                dve.wait_ge(part1, n + 1)
                if n >= 3:
                    dve.wait_ge(part3, n - 2)
                nc.vector.tensor_tensor(rest[0:rows_of[j], n % 3, :], core.bank[4 + n % 4][0:rows_of[j], :],
                                        part[0:rows_of[j], 0, j, h * HALF:(h + 1) * HALF], ALU.subtract).then_inc(rest1, 1)

        @block.gpsimd
        def _(pool):
            pool.memset(v[:, :, :, HD:HD + 1], 1.0).then_inc(ones_made, 1)
            pool.wait_ge(ones_made, 1)
            pool.memset(ks[ROWS:KROWS, :, :], 1.0).then_inc(ones_made, 1)
            pool.wait_ge(ones_made, 2)
            for n, (h, j) in enumerate(units):
                span = slice(h * HALF, (h + 1) * HALF)
                pool.wait_ge(part2, n + 1)
                if n >= 1:
                    pool.wait_ge(part3, n)
                nc.gpsimd.tensor_tensor(part[0:rows_of[j], 2, j, span], rest[0:rows_of[j], n % 3, :],
                                        part[0:rows_of[j], 1, j, span], ALU.subtract).then_inc(part3, 1)
    return lambda sp: stack(sp, numbered[first:])


def woven(a, b):
    return [x for i in range(max(len(a), len(b))) for x in a[i:i + 1] + b[i:i + 1]]


def order_of_a_head(cfg):
    n = len(cfg.quads)
    short = len(cfg.quads[-1][1]) <= 2
    slots = 2 * n - 2 - short
    tiles = [[("max", t) for t in range(TT) if t * slots // TT == i] for i in range(2 * n)]
    tiles[slots - 1].append(("make_shift",))
    order = []
    for g, (_, units, _, _) in enumerate(cfg.quads):
        before, back = (g - 1, 0) if g else (n - 1, 1)
        first_half, second_half = ([("shift", 0)], [("shift", 1)]) if g == n - 1 else ([], [])
        order += woven(tiles[2 * g], [("scores", u) for u in units[0:2]])
        order += first_half + [("values", before, back)] if short else [("values", before, back)] + first_half
        order += woven(tiles[2 * g + 1], [("scores", u) for u in units[2:4]]) + second_half
        if cfg.quads[before][3]:
            order.append(("turn", cfg.quads[before][0], back))
    return order


def attend(core, tag, cfg, v, qs, ks, ctxs, stacked, more_stacks):
    nc = core.nc
    U, Q = len(cfg.units), len(cfg.quads)
    UNROLL = 4
    TURNS = HEADS // UNROLL
    group = HEADS // cfg.kv_heads
    assert group in (1, UNROLL)
    scores_ready, max_done, shift_step, shift_ready, shift_rows, rows_stored = (
        core.sem(f"{tag}_{n}") for n in ("sc", "mxd", "shs", "shr", "shrow", "rst"))
    tsc_ready, probs_ready, probs_used, v_placed, acc_stored, turned, summed, inverted, ctx_stored = (
        core.sem(f"{tag}_{n}") for n in ("tsc", "pr", "pu", "vp", "accs", "turned", "summed", "inv", "cst"))
    order = order_of_a_head(cfg)
    quad_of = {u: (g, units.index(u)) for g, (_, units, _, _) in enumerate(cfg.quads) for u in units}
    first_units = [units[0] for _, units, first, _ in cfg.quads if first]
    last_quad = {half: g for g, (half, _, _, last) in enumerate(cfg.quads) if last}
    with ExitStack() as ctx:
        def sb(name, shape, dt=F32):
            return ctx.enter_context(nc.sbuf_tensor(f"{tag}_{name}", shape, dt))

        mx, rest = sb("mx", [P, TT]), sb("mrest", [P, TT])
        shift = sb("shift", [P, TT, PARTS], BF16)
        probs = sb("probs", [P, 8, HALF])
        V_BUFFERS = 1 if group == UNROLL else 2
        vh = sb("vh", [P, V_BUFFERS, TT, HD + 1])
        acc = sb("acc", [P, 2, HALF])
        sums, rden = sb("sums", [P, 2, 4, HD + 1]), sb("rden", [P, 2, 4])
        block = ctx.enter_context(nc.Block())
        acc_bank, small_bank = core.bank[6], core.bank[7]

        @block.sync
        def _(sp):
            more_stacks(sp)

        def is_at(h, n):
            return isinstance(h, int) and h == n

        def buffer_of(i, g, x=0):
            return 4 * ((Q * i + g) % 2) + x

        def kv_of(turn, i):
            return UNROLL * turn + i if group == 1 else turn + i // UNROLL

        def max_buffer(t):
            return core.psum[:, 2 * (t % 2):2 * (t % 2) + 2, :].rearrange("p b n -> p (b n)")

        @block.tensor
        def _(pe):
            def maxima(h, kv, t):
                if not (isinstance(h, int) and TT * h + t < 2):
                    pe.wait_ge(max_done, TT * h + t - 1)
                col = 0
                for k0, nk, mask in cfg.maxima[t]:
                    out = max_buffer(t)[:, col:col + nk]
                    last = nc.tensor.matmul(out, qs[0:ROWS, h, t * P:(t + 1) * P], ks[0:ROWS, kv, k0:k0 + nk],
                                            start=True, stop=mask is None, skip_group_check=True)
                    if mask is not None:
                        last = nc.tensor.matmul(out, core.ident_h[:], core.mask_h[mask][:, 0:nk],
                                                start=False, stop=True, skip_group_check=True)
                    col += nk
                last.then_inc(scores_ready, 1)

            def shift_to_rows(h, half):
                if half == 0:
                    pe.wait_ge(shift_ready, h + 1)
                if half == 1:
                    pe.wait_ge(rows_stored, 2 * h + 1)
                elif not is_at(h, 0):
                    pe.wait_ge(summed, 2 * h - 1)
                for t in range(4):
                    last = nc.tensor.matmul(small_bank[ROWS:KROWS, t * P:(t + 1) * P], shift[:, 4 * half + t, :],
                                            core.ident_h[:], start=True, stop=True)
                last.then_inc(shift_rows, 1)

            def scores(h, i, kv, u):
                k0, q0, nq, masks = cfg.units[u]
                if u in first_units:
                    pe.wait_ge(rows_stored, 2 * h + 1 + first_units.index(u))
                if not (isinstance(h, int) and U * h + u < 2):
                    pe.wait_ge(probs_ready, U * h + u - 1)
                bank = core.bank[4 + (U * i + u) % 2]
                last = nc.tensor.matmul(bank[:, 0:nq], ks[:, kv, k0:k0 + P], qs[:, h, q0:q0 + nq],
                                        start=True, stop=not masks, skip_group_check=True)
                for m, (c0, mask) in enumerate(masks):
                    last = nc.tensor.matmul(bank[:, c0:c0 + P], core.ident_h[:], core.mask_h[mask][:],
                                            start=False, stop=m == len(masks) - 1, skip_group_check=True)
                last.then_inc(tsc_ready, 1)

            def values(turn, h, i, g):
                half, units, first, last_of_half = cfg.quads[g]
                if first:
                    if g == 0:
                        pe.wait_ge(v_placed, turn + 1 if group == UNROLL else h + 1)
                    if not (is_at(h, 0) and half == 0):
                        pe.wait_ge(acc_stored, 2 * h + half)
                    nc.tensor.matmul(acc_bank[:], core.zero_h[:, 0:P], core.zero_h[:], start=True, stop=False,
                                     skip_group_check=True)
                pe.wait_ge(probs_ready, U * h + units[-1] + 1)
                for x, u in enumerate(units):
                    k0, q0, nq, _ = cfg.units[u]
                    last = nc.tensor.matmul(acc_bank[32 * x:32 * x + HD + 1, q0 % HALF:q0 % HALF + nq],
                                            vh[:, i % V_BUFFERS, k0 // P, :], probs[:, buffer_of(i, g, x), 0:nq],
                                            start=False, stop=last_of_half, skip_group_check=True)
                last.then_inc(probs_used, 1)

            def turn_sums(h, half):
                pe.wait_ge(acc_stored, 2 * h + half + 1)
                if half == 0 and is_at(h, 0):
                    pe.wait_ge(rows_stored, 2)
                elif half == 0:
                    pe.wait_ge(summed, 2 * h)
                elif is_at(h, HEADS - 1):
                    pe.wait_ge(summed, 2 * h + 1)
                else:
                    pe.wait_ge(rows_stored, 2 * h + 4)
                for t in range(4):
                    last = nc.tensor.transpose(small_bank[:, t * P:(t + 1) * P], acc[:, half, t * P:(t + 1) * P], core.ident[:])
                last.then_inc(turned, 1)

            def turn(g, final=False):
                for i in range(UNROLL):
                    h = UNROLL * g + i
                    is_last = final and i == UNROLL - 1
                    if i == UNROLL - 1 and not isinstance(h, int):
                        pe.wait_ge(stacked[1], 16 * stacks_of_chunk(cfg, 1))
                    for what, *args in order:
                        if what == "scores":
                            scores(h, i, kv_of(g, i), args[0])
                        elif what == "max" and not is_last:
                            maxima(h + 1, kv_of(g, i + 1), args[0])
                        elif what == "values" and not (is_at(h, 0) and args[1]):
                            values(g, h - args[1], (i - args[1]) % UNROLL, args[0])
                        elif what == "turn" and not (is_at(h, 0) and args[1]):
                            turn_sums(h - args[1], args[0])
                        elif what == "shift" and not is_last:
                            shift_to_rows(h + 1, args[0])

            pe.wait_ge(stacked[0], 16 * stacks_of_chunk(cfg, 0))
            for t in range(TT):
                maxima(0, 0, t)
            for half in range(2):
                shift_to_rows(0, half)
            turn(0)
            with pe.Fori(1, TURNS - 1) as g:
                turn(g)
            turn(TURNS - 1, final=True)
            values(TURNS - 1, HEADS - 1, UNROLL - 1, Q - 1)
            turn_sums(HEADS - 1, 1)

        @block.scalar
        def _(act):
            def store_rows(h, half):
                act.wait_ge(shift_rows, 2 * h + half + 1)
                nc.scalar.copy(qs[ROWS:KROWS, h, half * HALF:(half + 1) * HALF],
                               small_bank[ROWS:KROWS, :]).then_inc(rows_stored, 1)

            def exponentiate(h, i, u):
                nq = cfg.units[u][2]
                g, x = quad_of[u]
                act.wait_ge(tsc_ready, U * h + u + 1)
                if x == 0 and not (isinstance(h, int) and Q * h + g < 2):
                    act.wait_ge(probs_used, Q * h + g - 1)
                nc.scalar.activation(probs[:, buffer_of(i, g, x), 0:nq], core.bank[4 + (U * i + u) % 2][:, 0:nq],
                                     ACT.Exp, scale=HD ** -0.5).then_inc(probs_ready, 1)

            def store_sums(h, half):
                act.wait_ge(probs_used, Q * h + last_quad[half] + 1)
                if not is_at(h, 0):
                    act.wait_ge(turned, 2 * h + half - 1)
                nc.scalar.copy(acc[:, half, :], acc_bank[:]).then_inc(acc_stored, 1)

            def turn(g, final=False):
                for i in range(UNROLL):
                    h = UNROLL * g + i
                    for what, *args in order:
                        if what == "scores":
                            exponentiate(h, i, args[0])
                        elif what == "values" and not (is_at(h, 0) and args[1]):
                            if cfg.quads[args[0]][3]:
                                store_sums(h - args[1], cfg.quads[args[0]][0])
                        elif what == "shift" and not (final and i == UNROLL - 1):
                            store_rows(h + 1, args[0])

            for half in range(2):
                store_rows(0, half)
            turn(0)
            with act.Fori(1, TURNS - 1) as g:
                turn(g)
            turn(TURNS - 1, final=True)
            store_sums(HEADS - 1, 1)

        @block.gpsimd
        def _(pool):
            def place(g, i):
                h = UNROLL * g + i
                if group == UNROLL:
                    if not is_at(h, 0):
                        pool.wait_ge(probs_used, Q * h)
                        pool.wait_ge(v_placed, g)
                    nc.gpsimd.tensor_copy(vh[:, 0, :, :], v[:, :, g, :]).then_inc(v_placed, 1)
                    return
                if not (isinstance(h, int) and h < 2):
                    pool.wait_ge(probs_used, Q * (h - 1))
                if not is_at(h, 0):
                    pool.wait_ge(v_placed, h)
                nc.gpsimd.tensor_copy(vh[:, i % 2, :, :], v[:, :, kv_of(g, i), :]).then_inc(v_placed, 1)

            placed = range(0, UNROLL, UNROLL if group == UNROLL else 1)
            for i in placed:
                place(0, i)
            with pool.Fori(1, TURNS) as g:
                for i in placed:
                    place(g, i)

        @block.vector
        def _(dve):
            def maximum(h, t):
                width = sum(nk for _, nk, _ in cfg.maxima[t])
                dve.wait_ge(scores_ready, TT * h + t + 1)
                if t == 0 and not is_at(h, 0):
                    dve.wait_ge(shift_step, 3 * h)
                nc.vector.tensor_reduce(mx[:, t:t + 1], max_buffer(t)[:, 0:width], AX_X, ALU.max).then_inc(max_done, 1)

            def make_shift(h):
                dve.wait_ge(max_done, TT * h + TT)
                if not is_at(h, 0):
                    dve.wait_ge(shift_rows, 2 * h)
                    dve.wait_ge(shift_ready, h)
                nc.vector.tensor_scalar(shift[:, :, 0], mx[:], -1.0, None, ALU.mult).then_inc(shift_step, 1)
                dve.wait_ge(shift_step, 3 * h + 1)
                nc.vector.scalar_tensor_tensor(out=rest[:], in0=mx[:], scalar=-1.0, in1=shift[:, :, 0],
                                               op0=ALU.mult, op1=ALU.subtract).then_inc(shift_step, 1)
                dve.wait_ge(shift_step, 3 * h + 2)
                nc.vector.tensor_copy(shift[:, :, 1], rest[:]).then_inc(shift_step, 1)
                dve.wait_ge(shift_step, 3 * h + 3)
                nc.vector.tensor_tensor(shift[:, :, 2], rest[:], shift[:, :, 1], ALU.subtract).then_inc(shift_ready, 1)

            def normalize_sums(h, half):
                n = 2 * h + half
                dve.wait_ge(turned, n + 1)
                if not is_at(h, 0):
                    dve.wait_ge(ctx_stored, n - 1)
                parts = small_bank[:].rearrange("p (t g c) -> p t c g", g=4, c=32)[:, :, 0:HD + 1, :]
                nc.vector.tensor_reduce(sums[:, half, :, :], parts, AX_X, ALU.add).then_inc(summed, 1)
                dve.wait_ge(summed, n + 1)
                nc.vector.reciprocal(rden[:, half, :], sums[:, half, :, HD]).then_inc(inverted, 1)
                dve.wait_ge(inverted, n + 1)
                nc.vector.tensor_tensor(ctxs[:, 4 * half:4 * half + 4, bass.ds(h * HD, HD)], sums[:, half, :, 0:HD],
                                        rden[:, half, :].unsqueeze(2).broadcast_to([P, 4, HD]), ALU.mult).then_inc(ctx_stored, 1)

            def turn(g, final=False):
                for i in range(UNROLL):
                    h = UNROLL * g + i
                    is_last = final and i == UNROLL - 1
                    for what, *args in order:
                        if what == "max" and not is_last:
                            maximum(h + 1, args[0])
                        elif what == "turn" and not (is_at(h, 0) and args[1]):
                            normalize_sums(h - args[1], args[0])
                        elif what == "make_shift" and not is_last:
                            make_shift(h + 1)

            for t in range(TT):
                maximum(0, t)
            make_shift(0)
            turn(0)
            with dve.Fori(1, TURNS - 1) as g:
                turn(g)
            turn(TURNS - 1, final=True)
            normalize_sums(HEADS - 1, 1)


def project_out(core, tag, ctxs, wo, wo_loaded, extra=None):
    nc = core.nc
    turned, turn_copied, projected, step, added = (
        core.sem(f"{tag}_{n}") for n in ("tc", "tcc", "po", "poa", "pod"))
    with ExitStack() as ctx:
        ctxT = ctx.enter_context(nc.sbuf_tensor(f"{tag}_ctxT", [P, KC, T], F32))
        block = ctx.enter_context(nc.Block())

        @block.tensor
        def _(pe):
            for u in range(4):
                h, k = u // 2, u % 2
                for t in range(4 * h, 4 * h + 4):
                    last = nc.tensor.transpose(core.bank[u][:, (t % 4) * P:(t % 4 + 1) * P],
                                               ctxs[:, t, k * P:(k + 1) * P], core.ident[:])
                last.then_inc(turned, 1)
            if tag != "b":
                pe.wait_ge(wo_loaded, 16)
            for t in range(TT):
                pe.wait_ge(turn_copied, 2 * (t // 4) + 2)
                if t >= 4:
                    pe.wait_ge(added, t - 3)
                for k in range(KC):
                    last = nc.tensor.matmul(core.bank[4 + t % 4][:, 0:D], ctxT[:, k, t * P:(t + 1) * P], wo[:, k, :],
                                            start=(k == 0), stop=(k == KC - 1))
                last.then_inc(projected, 1)

        @block.scalar
        def _(act):
            for u in range(4):
                h, k = u // 2, u % 2
                act.wait_ge(turned, u + 1)
                nc.scalar.copy(ctxT[:, k, h * HALF:(h + 1) * HALF], core.bank[u][:]).then_inc(turn_copied, 1)

        @block.vector
        def _(dve):
            if extra is not None:
                nc.vector.tensor_tensor(core.x[:], core.x[:], extra[:], ALU.add).then_inc(step, 1)
                dve.wait_ge(step, 1)
            for t in range(TT):
                dve.wait_ge(projected, t + 1)
                nc.vector.tensor_tensor(core.x[:, t, :], core.x[:, t, :], core.bank[4 + t % 4][:, 0:D], ALU.add).then_inc(added, 1)


LSCALE = float(np.float32(1.0) / np.sqrt(np.float32(DN + DR)))
LPAIRS = HEADS // 2
UP = DN + DV


def latent(core, tag, norm):
    with ExitStack() as ctx:
        def sb(name, shape, dt=F32):
            return ctx.enter_context(core.nc.sbuf_tensor(f"{tag}_{name}", shape, dt))

        wvo = sb("wvo", [P, LPAIRS, D])
        ctxT = sb("ctxT", [P, LPAIRS, T])
        with ExitStack() as inner:
            def sbi(name, shape, dt=F32):
                return inner.enter_context(core.nc.sbuf_tensor(f"{tag}_{name}", shape, dt))

            wq = sbi("wq", [QR, HEADS, KVR + 2 * DR])
            qcT = sbi("qcT", [QR, T])
            kT = sbi("kT", [P, T])
            v = sbi("v", [P, TT, KVR])
            cos, sin = sbi("cos", [P, T]), sbi("sin", [P, T])
            wqu = sbi("wqu", [QR, HEADS * DN])
            wkv = sbi("wkv", [KVR, HEADS * UP])
            wo = sbi("wo", [P, HEADS, D])
            wr = sbi("wr", [QR, HEADS, DR])
            up_loaded, tab_loaded = core.sem(f"{tag}_up"), core.sem(f"{tag}_tab")

            def load(sp):
                sp.dma_start(wqu[:], core.dram["L1_attn_b_wq_up"]).then_inc(up_loaded, 16)
                sp.dma_start(wkv[:], core.dram["L1_attn_b_wkv_up"]).then_inc(up_loaded, 16)
                sp.dma_start(wr[:], core.dram["L1_attn_b_wq_rope"].rearrange("r (h d) -> r h d", d=DR)).then_inc(up_loaded, 16)
                sp.dma_start(wo[:], core.dram["L1_attn_b_wo"].rearrange("(h p) n -> p h n", p=P)).then_inc(up_loaded, 16)
                sp.dma_start(cos[KVR:P, :], core.dram["c_cos_q"]).then_inc(tab_loaded, 16)
                sp.dma_start(sin[KVR:P, :], core.dram["c_sin_q"]).then_inc(tab_loaded, 16)

            latent_down(core, tag, norm, load, qcT, kT, v)
            latent_weights(core, tag, wqu, wkv, wo, wr, up_loaded, wq, wvo)
            latent_attend(core, tag, wq, qcT, kT, v, ctxT, cos, sin, tab_loaded)
        latent_out(core, tag, wvo, ctxT)


def latent_down(core, tag, norm, load_more, qcT, kT, v):
    nc, dram = core.nc, core.dram
    W = QR + KVR + DR
    loaded, projected, copied, squared, meaned, rooted, inverted, normed, roped, valued, turned, qk_copied = (
        core.sem(f"{tag}d_{n}") for n in ("ld", "pr", "cp", "sq", "mean", "root", "inv", "norm", "rope", "val", "turn", "qkc"))
    with ExitStack() as ctx:
        def sb(name, shape, dt=F32):
            return ctx.enter_context(nc.sbuf_tensor(f"{tag}d_{name}", shape, dt))

        w = sb("w", [P, KC, W])
        lat = sb("lat", [P, TT, W])
        junk = sb("junk", [P, 2, QR])
        ssq, root, inv = (sb(n, [P, 2, TT]) for n in ("ssq", "rt", "iv"))
        cos, sin = sb("cos", [P, TT, DR]), sb("sin", [P, TT, DR])
        swapped = sb("swapped", [P, TT, DR])
        spans = ((0, QR, "L1_attn_b_q_norm_w"), (QR, KVR, "L1_attn_b_kv_norm_w"))

        def load(sp):
            for name, c0, n in (("wq_down", 0, QR), ("wkv_down", QR, KVR), ("wk_rope", QR + KVR, DR)):
                sp.dma_start(w[:, :, c0:c0 + n], dram[f"L1_attn_b_{name}"].rearrange("(k p) n -> p k n", p=P)).then_inc(loaded, 16)
            sp.dma_start(cos[:], dram["c_cos_k"].rearrange("(t p) d -> p t d", p=P)).then_inc(loaded, 16)
            sp.dma_start(sin[:], dram["c_sin_k"].rearrange("(t p) d -> p t d", p=P)).then_inc(loaded, 16)
            load_more(sp)

        norm(load)
        block = ctx.enter_context(nc.Block())

        @block.tensor
        def _(pe):
            pe.wait_ge(loaded, 80)
            for t in range(TT):
                if t >= 4:
                    pe.wait_ge(copied, t - 3)
                for k in range(KC):
                    last = nc.tensor.matmul(core.bank[t % 4][:, 0:W], core.xT[:, k, t * P:(t + 1) * P], w[:, k, :],
                                            start=(k == 0), stop=(k == KC - 1))
                last.then_inc(projected, 1)
            pe.wait_ge(normed, 4)
            pe.wait_ge(roped, 4)
            for h in range(2):
                for t in range(4 * h, 4 * h + 4):
                    nc.tensor.transpose(core.bank[4 + h][0:QR, (t % 4) * P:(t % 4 + 1) * P], lat[:, t, 0:QR], core.ident[:])
                    last = nc.tensor.transpose(core.bank[6 + h][:, (t % 4) * P:(t % 4 + 1) * P], lat[:, t, QR:W], core.ident[:])
                last.then_inc(turned, 1)

        @block.scalar
        def _(act):
            for t in range(TT):
                act.wait_ge(projected, t + 1)
                nc.scalar.copy(lat[:, t, :], core.bank[t % 4][:, 0:W]).then_inc(copied, 1)
            act.wait_ge(meaned, 2)
            nc.scalar.activation(root[:], ssq[:], ACT.Sqrt).then_inc(rooted, 1)
            for h in range(2):
                act.wait_ge(turned, h + 1)
                nc.scalar.copy(kT[:, h * HALF:(h + 1) * HALF], core.bank[6 + h][:]).then_inc(qk_copied, 1)

        @block.vector
        def _(dve):
            for t in range(TT):
                dve.wait_ge(copied, t + 1)
                for i, (c0, n, _) in enumerate(spans):
                    if t >= 1:
                        dve.wait_ge(squared, 2 * t - 1 + i)
                    nc.vector.tensor_tensor_reduce(junk[:, i, 0:n], lat[:, t, c0:c0 + n], lat[:, t, c0:c0 + n], 1.0, 0.0,
                                                   ALU.mult, ALU.add, ssq[:, i, t:t + 1]).then_inc(squared, 1)
            dve.wait_ge(squared, 2 * TT)
            for i, (c0, n, _) in enumerate(spans):
                nc.vector.tensor_scalar(ssq[:, i, :], ssq[:, i, :], 1.0 / n, 1e-6, ALU.mult, ALU.add).then_inc(meaned, 1)
            dve.wait_ge(rooted, 1)
            nc.vector.reciprocal(inv[:], root[:]).then_inc(inverted, 1)
            dve.wait_ge(inverted, 1)
            for i, (c0, n, _) in enumerate(spans):
                nc.vector.tensor_tensor(lat[:, :, c0:c0 + n], lat[:, :, c0:c0 + n],
                                        inv[:, i, :].unsqueeze(2).broadcast_to([P, TT, n]), ALU.mult).then_inc(normed, 1)
            for i, (c0, n, name) in enumerate(spans):
                dve.wait_ge(normed, i + 1)
                nc.vector.tensor_tensor(lat[:, :, c0:c0 + n], lat[:, :, c0:c0 + n],
                                        core.row[name][:].unsqueeze(1).broadcast_to([P, TT, n]), ALU.mult).then_inc(normed, 1)
            k0 = QR + KVR
            for to, frm in ((0, 1), (1, 0)):
                nc.vector.tensor_tensor(swapped[:, :, to:to + DR - 1:2], lat[:, :, k0 + frm:k0 + frm + DR - 1:2],
                                        sin[:, :, to:to + DR - 1:2], ALU.mult).then_inc(roped, 1)
            dve.wait_ge(roped, 2)
            nc.vector.tensor_tensor(lat[:, :, k0:W], lat[:, :, k0:W], cos[:], ALU.mult).then_inc(roped, 1)
            dve.wait_ge(roped, 3)
            nc.vector.tensor_tensor(lat[:, :, k0:W], lat[:, :, k0:W], swapped[:], ALU.add).then_inc(roped, 1)
            dve.wait_ge(normed, 4)
            nc.vector.tensor_copy(v[:], lat[:, :, QR:QR + KVR]).then_inc(valued, 1)
            for h in range(2):
                dve.wait_ge(turned, h + 1)
                nc.vector.tensor_copy(qcT[:, h * HALF:(h + 1) * HALF], core.bank[4 + h][0:QR, :]).then_inc(qk_copied, 1)


def latent_weights(core, tag, wqu, wkv, wo, wr, up_loaded, wq, wvo):
    nc = core.nc
    rope_copied, turned, turn_copied, folded, fold_copied = (
        core.sem(f"{tag}w_{n}") for n in ("rc", "turn", "tc", "fold", "fc"))
    NT = QR + 2 * KVR
    with ExitStack() as ctx:
        def sb(name, shape, dt=F32):
            return ctx.enter_context(nc.sbuf_tensor(f"{tag}w_{name}", shape, dt))

        wt = sb("wt", [P, 2, NT])
        block = ctx.enter_context(nc.Block())

        @block.gpsimd
        def _(pool):
            pool.wait_ge(up_loaded, 64)
            nc.gpsimd.tensor_copy(wq[:, :, KVR:KVR + DR], wr[:]).then_inc(rope_copied, 1)
            for n, (to, frm) in enumerate(((0, 1), (1, 0))):
                pool.wait_ge(rope_copied, n + 1)
                nc.gpsimd.tensor_copy(wq[:, :, KVR + DR + to:KVR + 2 * DR:2], wr[:, :, frm:DR:2]).then_inc(rope_copied, 1)

        @block.tensor
        def _(pe):
            pe.wait_ge(up_loaded, 64)

            def turn(h):
                if h >= 2:
                    pe.wait_ge(turn_copied, h - 1)
                b = core.bank[h % 2]
                nc.tensor.transpose(b[:, 0:QR], wqu[:, h * DN:(h + 1) * DN], core.ident[0:QR, 0:QR])
                nc.tensor.transpose(b[:, QR:QR + KVR], wkv[:, h * UP:h * UP + DN], core.ident[0:KVR, 0:KVR])
                nc.tensor.transpose(b[:, QR + KVR:NT], wkv[:, h * UP + DN:(h + 1) * UP],
                                    core.ident[0:KVR, 0:KVR]).then_inc(turned, 1)

            def fold(h):
                pe.wait_ge(turn_copied, h + 1)
                if h >= 2:
                    pe.wait_ge(fold_copied, 2 * (h - 1))
                t = wt[:, h % 2, :]
                p0 = KVR * (h % 2)
                nc.tensor.matmul(core.bank[2 + h % 2][0:QR, 0:KVR], t[:, 0:QR], t[:, QR:QR + KVR], start=True, stop=True)
                nc.tensor.matmul(core.bank[4 + h % 2][p0:p0 + KVR, 0:D], t[:, QR + KVR:NT], wo[:, h, :],
                                 start=True, stop=True).then_inc(folded, 1)

            turn(0)
            for h in range(HEADS):
                if h + 1 < HEADS:
                    turn(h + 1)
                fold(h)

        @block.vector
        def _(dve):
            def turned_out(h):
                dve.wait_ge(turned, h + 1)
                if h >= 2:
                    dve.wait_ge(folded, h - 1)
                nc.vector.tensor_copy(wt[:, h % 2, :], core.bank[h % 2][:, 0:NT]).then_inc(turn_copied, 1)

            turned_out(0)
            for h in range(HEADS):
                if h + 1 < HEADS:
                    turned_out(h + 1)
                dve.wait_ge(folded, h + 1)
                nc.vector.tensor_copy(wq[:, h, 0:KVR], core.bank[2 + h % 2][0:QR, 0:KVR]).then_inc(fold_copied, 1)
                p0 = KVR * (h % 2)
                nc.vector.tensor_copy(wvo[p0:p0 + KVR, h // 2, :], core.bank[4 + h % 2][p0:p0 + KVR, 0:D]).then_inc(fold_copied, 1)


def latent_attend(core, tag, wq, qcT, kT, v, ctxT, cos, sin, tab_loaded):
    nc = core.nc
    w_placed, proj_ready, lat_copied, proj_used, q_ready = (
        core.sem(f"{tag}a_{n}") for n in ("wpl", "pj", "lc", "pjd", "qr"))
    score_ready, negmax_ready, exp_done, inverted, scaled, turned, turn_copied, pv_done, ctx_copied = (
        core.sem(f"{tag}a_{n}") for n in ("sc", "nm", "ex", "inv", "scl", "tu", "tcp", "pv", "cs"))
    groups = [[list(range(k, min(k + 4, t + 1))) for k in range(0, t + 1, 4)] for t in range(TT)]
    before = [sum(len(g) for g in groups[:t]) for t in range(TT + 1)]
    NG = before[TT]
    assert NG % 2 == 0 and TT % 2 == 0
    HT = TT // 2
    with ExitStack() as ctx:
        def sb(name, shape, dt=F32):
            return ctx.enter_context(nc.sbuf_tensor(f"{tag}a_{name}", shape, dt))

        wh = sb("wh", [QR, 2, KVR + 2 * DR])
        q = sb("q", [P, 2, T])
        swapped = sb("swapped", [P, 2, HALF])
        negmax, inv = sb("negmax", [P, 2]), sb("inv", [P, 2])
        sums = sb("sums", [P, 2, 2])
        probs = sb("probs", [P, 2, 2, T])
        probsT = sb("probsT", [P, 2, 2, HALF])
        block = ctx.enter_context(nc.Block())
        pv = core.bank[6]

        def n_tile(i, t, a=0):
            return 2 * (TT * i + t) + a

        def n_group(i, t, g=0):
            return NG * i + before[t] + g

        def early(i, t, n):
            return isinstance(i, int) and TT * i + t < n

        def scores_of(a):
            return core.psum[:, 2 * a:2 * a + 2, :].rearrange("p b n -> p (b n)")

        def part_of(i, t):
            return 4 * i + 2 + t // 2, t % 2, t // 2 % 2, 1 - t // HT

        def projects(t, final):
            return not (final and t >= HT)

        FIRST = [(0, 0, 0, 0), (0, 1, 0, 0), (1, 0, 1, 0), (1, 1, 1, 0)]

        @block.tensor
        def _(pe):
            def project(n, part, a, half, placed=None):
                if placed is not None:
                    pe.wait_ge(w_placed, placed)
                if not (isinstance(n, int) and n == 0 and part == 0):
                    pe.wait_ge(proj_used, 2 * n + part)
                if part == 1:
                    pe.wait_ge(lat_copied, n + 1)
                rhs = qcT[:, half * HALF:(half + 1) * HALF]
                if part == 0:
                    last = nc.tensor.matmul(core.bank[7][:], wh[:, a, 0:KVR + DR], rhs, start=True, stop=True)
                else:
                    last = nc.tensor.matmul(core.bank[7][KVR:P, :], wh[:, a, KVR + DR:KVR + 2 * DR], rhs, start=True, stop=True)
                last.then_inc(proj_ready, 1)

            def score(i, t, a):
                if t % HT == 0:
                    unit = 4 * i + 2 * (t // HT) + a
                    pe.wait_ge(q_ready, unit + 1)
                    pe.wait_ge(lat_copied, unit + 1)
                if not early(i, t, 1):
                    pe.wait_ge(exp_done, n_tile(i, t, a) - 1)
                out = scores_of(a)
                for k0 in range(0, (t + 1) * P, HALF):
                    nk = min(HALF, (t + 1) * P - k0)
                    nc.tensor.matmul(out[:, k0:k0 + nk], q[:, a, t * P:(t + 1) * P], kT[:, k0:k0 + nk],
                                     start=True, stop=False, skip_group_check=True)
                nc.tensor.matmul(out[:, t * P:(t + 1) * P], core.ident_h[:], core.mask_h["causal"][:],
                                 start=False, stop=True, skip_group_check=True).then_inc(score_ready, 1)

            def transposes(i, t, g):
                for a in range(2):
                    if g == 0:
                        pe.wait_ge(scaled, n_tile(i, t, a) + 1)
                    if not (early(i, t, 1) and g == 0):
                        pe.wait_ge(turn_copied, 2 * n_group(i, t, g) + a - 1)
                    for x, k in enumerate(groups[t][g]):
                        last = nc.tensor.transpose(core.bank[4 + a][:, x * P:(x + 1) * P],
                                                   probs[:, a, t % 2, k * P:(k + 1) * P], core.ident[:])
                    last.then_inc(turned, 1)

            def values(i, t, g):
                pe.wait_ge(turn_copied, 2 * n_group(i, t, g) + 2)
                if g == 0 and t % HT == 0 and not early(i, t, 1):
                    pe.wait_ge(ctx_copied, 2 * i + t // HT)
                for x, k in enumerate(groups[t][g]):
                    for a in range(2):
                        last = nc.tensor.matmul(pv[KVR * a:KVR * (a + 1), (t % HT) * P:(t % HT + 1) * P], v[:, k, :],
                                                probsT[:, a, (before[t] + g) % 2, x * P:(x + 1) * P],
                                                start=(k == 0), stop=(k == t), skip_group_check=True)
                last.then_inc(pv_done, 1)

            def back(i, t, between=None):
                transposes(i, t, 0)
                if between is not None:
                    between()
                for g in range(1, len(groups[t])):
                    transposes(i, t, g)
                for g in range(len(groups[t])):
                    values(i, t, g)

            def pair(i, final=False):
                for t in range(TT):
                    for a in range(2):
                        score(i, t, a)

                    def next_part():
                        if projects(t, final):
                            n, part, a, half = part_of(i, t)
                            project(n, part, a, half, placed=2 * i + 3 + a if t >= HT and part == 0 else None)

                    if early(i, t, 1):
                        next_part()
                    else:
                        back(*((i, t - 1) if t else (i - 1, TT - 1)), between=next_part)

            for n, part, a, half in FIRST:
                project(n, part, a, half, placed=a + 1 if part == 0 else None)
            pair(0)
            with pe.Fori(1, LPAIRS - 1) as i:
                pair(i)
            pair(LPAIRS - 1, final=True)
            back(LPAIRS - 1, TT - 1)

        @block.scalar
        def _(act):
            def copy_latent(n, a, half, scores_read=None):
                act.wait_ge(proj_ready, 2 * n + 1)
                if scores_read is not None:
                    act.wait_ge(score_ready, scores_read)
                nc.scalar.activation(q[0:KVR, a, half * HALF:(half + 1) * HALF], core.bank[7][0:KVR, :], ACT.Copy,
                                     scale=LSCALE).then_inc(lat_copied, 1)

            def exponentiate(i, t, a):
                act.wait_ge(negmax_ready, n_tile(i, t, a) + 1)
                if not early(i, t, 2):
                    act.wait_ge(turned, 2 * (n_group(i, t - 1) if t else n_group(i - 1, TT - 1)))
                w = (t + 1) * P
                nc.scalar.activation(probs[:, a, t % 2, 0:w], scores_of(a)[:, 0:w], ACT.Exp, bias=negmax[:, a:a + 1],
                                     accum_out=sums[:, a, t % 2:t % 2 + 1]).then_inc(exp_done, 1)

            def copy_turned(i, t, g, a):
                n = len(groups[t][g]) * P
                act.wait_ge(turned, 2 * n_group(i, t, g) + a + 1)
                if not (early(i, t, TT) and before[t] + g < 2):
                    act.wait_ge(pv_done, n_group(i, t, g) - 1)
                nc.scalar.copy(probsT[:, a, (before[t] + g) % 2, 0:n], core.bank[4 + a][:, 0:n]).then_inc(turn_copied, 1)

            def pair(i, final=False):
                for t in range(TT):
                    former = None if early(i, t, 1) else (i, t - 1) if t else (i - 1, TT - 1)
                    exponentiate(i, t, 0)
                    if former:
                        for a in range(2):
                            copy_turned(*former, 0, a)
                    exponentiate(i, t, 1)
                    if t % 2 == 0 and projects(t, final):
                        n, _, a, half = part_of(i, t)
                        copy_latent(n, a, half, None if early(i, t, HT) else n_tile(i, t // HT * HT))
                    if former and len(groups[former[1]]) > 1:
                        for a in range(2):
                            copy_turned(*former, 1, a)

            for n, part, a, half in FIRST:
                if part == 0:
                    copy_latent(n, a, half)
            pair(0)
            with act.Fori(1, LPAIRS - 1) as i:
                pair(i)
            pair(LPAIRS - 1, final=True)
            for g in range(len(groups[TT - 1])):
                for a in range(2):
                    copy_turned(LPAIRS - 1, TT - 1, g, a)

        @block.gpsimd
        def _(pool):
            def place(i, a):
                if not (isinstance(i, int) and i == 0):
                    pool.wait_ge(proj_ready, 4 + 8 * (i - 1) + 2 * a + 2)
                    pool.wait_ge(q_ready, 4 * (i - 1) + 4)
                if not (isinstance(i, int) and i == 0 and a == 0):
                    pool.wait_ge(w_placed, 2 * i + a)
                nc.gpsimd.tensor_copy(wh[:, a, :], wq[:, bass.ds(2 * i + a, 1), :].rearrange("r a c -> r (a c)")).then_inc(w_placed, 1)

            def add(n, a, half, placed):
                pool.wait_ge(w_placed, placed)
                if not (isinstance(n, int) and n == 0):
                    pool.wait_ge(q_ready, n)
                pool.wait_ge(proj_used, 2 * n + 2)
                span = slice(half * HALF, (half + 1) * HALF)
                nc.gpsimd.tensor_tensor(q[KVR:P, a, span], q[KVR:P, a, span], swapped[KVR:P, a, :], ALU.add).then_inc(q_ready, 1)

            def pair(i, final=False):
                for a in range(2):
                    add(4 * i + 2 + a, a, 1, 2 * i + 2)
                if not final:
                    for a in range(2):
                        place(i + 1, a)
                    for a in range(2):
                        add(4 * i + 4 + a, a, 0, 2 * i + 4)

            for a in range(2):
                place(0, a)
            for a in range(2):
                add(a, a, 0, 2)
            with pool.Fori(0, LPAIRS - 1) as i:
                pair(i)
            pair(LPAIRS - 1, final=True)

        @block.vector
        def _(dve):
            def rotate(n, part, a, half):
                span = slice(half * HALF, (half + 1) * HALF)
                dve.wait_ge(proj_ready, 2 * n + part + 1)
                if part == 1 and not (isinstance(n, int) and n < 2):
                    dve.wait_ge(q_ready, n - 1)
                out, table = (q[KVR:P, a, span], cos) if part == 0 else (swapped[KVR:P, a, :], sin)
                nc.vector.scalar_tensor_tensor(out=out, in0=core.bank[7][KVR:P, :], scalar=LSCALE,
                                               in1=table[KVR:P, span], op0=ALU.mult, op1=ALU.mult).then_inc(proj_used, 1)

            def maximum(i, t, a):
                dve.wait_ge(score_ready, n_tile(i, t, a) + 1)
                nc.vector.tensor_reduce(negmax[:, a:a + 1], scores_of(a)[:, 0:(t + 1) * P], AX_X, ALU.max,
                                        negate=True).then_inc(negmax_ready, 1)

            def scale(i, t, a):
                dve.wait_ge(exp_done, n_tile(i, t, a) + 1)
                if not early(i, t, 1):
                    dve.wait_ge(scaled, n_tile(i, t, a) - 1)
                nc.vector.reciprocal(inv[:, a:a + 1], sums[:, a, t % 2:t % 2 + 1]).then_inc(inverted, 1)
                dve.wait_ge(inverted, n_tile(i, t, a) + 1)
                w = (t + 1) * P
                nc.vector.tensor_scalar(probs[:, a, t % 2, 0:w], probs[:, a, t % 2, 0:w], inv[:, a:a + 1], None,
                                        ALU.mult).then_inc(scaled, 1)

            def store(i, half):
                dve.wait_ge(pv_done, n_group(i, HT * (half + 1) - 1) + len(groups[HT * (half + 1) - 1]))
                nc.vector.tensor_scalar(ctxT[:, bass.ds(i, 1), half * HALF:(half + 1) * HALF].rearrange("p a t -> p (a t)"),
                                        pv[:], 1.0, None, ALU.mult).then_inc(ctx_copied, 1)

            def pair(i, final=False):
                for t in range(TT):
                    for a in range(2):
                        maximum(i, t, a)
                    scale(i, t, 0)
                    if projects(t, final):
                        rotate(*part_of(i, t))
                    scale(i, t, 1)
                    if t % HT == 0 and not early(i, t, 1):
                        store(*((i, 0) if t else (i - 1, 1)))

            dve.wait_ge(tab_loaded, 32)
            for unit in FIRST:
                rotate(*unit)
            pair(0)
            with dve.Fori(1, LPAIRS - 1) as i:
                pair(i)
            pair(LPAIRS - 1, final=True)
            store(LPAIRS - 1, 1)


def latent_out(core, tag, wvo, ctxT):
    nc = core.nc
    projected, added = (core.sem(f"{tag}o_{n}") for n in ("pr", "ad"))
    with nc.Block() as block:
        @block.tensor
        def _(pe):
            for t in range(TT):
                for c in range(LPAIRS):
                    last = nc.tensor.matmul(core.bank[t][:, 0:D], ctxT[:, c, t * P:(t + 1) * P], wvo[:, c, :],
                                            start=(c == 0), stop=(c == LPAIRS - 1))
                last.then_inc(projected, 1)

        @block.vector
        def _(dve):
            for t in range(TT):
                dve.wait_ge(projected, t + 1)
                nc.vector.tensor_tensor(core.x[:, t, :], core.x[:, t, :], core.bank[t][:, 0:D], ALU.add).then_inc(added, 1)


def program(nc, dram):
    with ExitStack() as ctx:
        core = Core(nc, ctx, dram)
        start(core)
        attention(core, "a", ATT_A, lambda load: normalize(core, "n1", core.x, core.xn, load=load))
        moe(core, "e1", lambda load: normalize(core, "n2", core.x, core.xn, load=load))
        core.clear_semaphores()
        attention(core, "b", ATT_B, lambda load: normalize(core, "n3", core.x, core.xn, load=load))
        moe(core, "e2", lambda load: normalize(core, "n4", core.x, core.xn, load=load))
        core.clear_semaphores()
        normalize(core, "n5", core.x, core.xn, turn=False)
        inner = (core.row["L1_attn_a_ln_w"], core.row["L1_attn_a_ln_b"])
        attention(core, "c", ATT_C, lambda load: normalize(core, "n5i", core.xn, core.xi, affine=inner, load=load))
        normalize(core, "n6", core.x, core.xn)
        ffn(core, "f1")
        core.clear_semaphores()
        latent(core, "l", lambda load: normalize(core, "n7", core.x, core.xn, load=load))
        normalize(core, "n8", core.x, core.xn)
        ffn(core, "f2")
        finish(core)


def _constants():
    c = {}
    c["c_ident"] = np.eye(P, dtype=np.float32)
    i, j = np.arange(P)[:, None], np.arange(P)[None, :]
    neg = np.float32(NEG)
    causal = np.where(j <= i, np.float32(0), neg)
    prev = np.where(j > i, np.float32(0), neg)
    prev1 = np.where((j > i) | (j < 4), np.float32(0), neg)
    for n, m in (("causal", causal), ("prev", prev), ("prev1", prev1)):
        c[f"c_{n}"] = np.ascontiguousarray(m.astype(np.float32))
        c[f"c_{n}T"] = np.ascontiguousarray(m.T.astype(np.float32))
    c["c_sinkT"] = np.where(np.broadcast_to(i, (P, P)) < 4, np.float32(0), neg).astype(np.float32)
    t = np.arange(T, dtype=np.float32)

    def angles(n):
        inv = np.float32(1) / np.float32(10000) ** (np.arange(0, n, 2, dtype=np.float32) / np.float32(n))
        a = t[:, None] * inv[None, :].astype(np.float32)
        return np.cos(a).astype(np.float32), np.sin(a).astype(np.float32)

    cos, sin = angles(HD)
    c["c_cos_a"] = np.concatenate([cos, cos], 1)
    c["c_sin_a"] = np.concatenate([-sin, sin], 1)
    cos, sin = angles(HD // 2)
    c["c_cos_c"] = np.concatenate([np.repeat(cos, 2, 1), np.ones((T, HD // 2), np.float32)], 1)
    s = np.repeat(sin, 2, 1)
    s[:, 0::2] *= -1
    c["c_sin_c"] = np.concatenate([s, np.zeros((T, HD // 2), np.float32)], 1)
    cos, sin = angles(DR)
    s = np.repeat(sin, 2, 1)
    s[:, 0::2] *= -1
    c["c_cos_k"] = np.repeat(cos, 2, 1)
    c["c_sin_k"] = s
    c["c_cos_q"] = np.repeat(cos, 2, 1).T
    c["c_sin_q"] = s.T
    return {k: np.ascontiguousarray(v, dtype=np.float32) for k, v in c.items()}


def kernel(**inputs):
    import concourse.bacc as _bacc
    from concourse.bass_utils import run_bass_kernel_spmd as _run

    nc = _bacc.Bacc("TRN2", target_bir_lowering=False, num_devices=1)
    arrays, dram = {}, {}
    for name, a in {**inputs, **_constants()}.items():
        a = np.ascontiguousarray(a)
        arrays[f"in_{name}"] = a
        dram[name] = nc.dram_tensor(f"in_{name}", a.shape, mybir.dt.from_np(a.dtype), kind="ExternalInput").ap()
    dram["out"] = nc.dram_tensor("out_0", (1, T, D), F32, kind="ExternalOutput").ap()
    program(nc, dram)
    r = _run(nc, [arrays], core_ids=[0])
    return r.results[0]["out_0"]
```
